# Optimizing a Trainium2 kernel written in Bass

```python
import numpy as np
import jax
import jax.numpy as jnp

def _softmax(x, axis=-1):
    return jax.nn.softmax(x, axis=axis)

def _gelu(x):
    return jax.nn.gelu(x, approximate=True)

def _silu(x):
    return jax.nn.silu(x)

def _sigmoid(x):
    return jax.nn.sigmoid(x)

def _layernorm(x, axis=-1, eps=1e-05):
    m = jnp.mean(x, axis=axis, keepdims=True)
    v = jnp.var(x, axis=axis, keepdims=True)
    return (x - m) / jnp.sqrt(v + eps)

def _scatter_add(tgt, idx, src, axis=0):
    return tgt.at[idx].add(src)

def _segment_sum(src, seg, n):
    return jax.ops.segment_sum(src, seg, n)
kernel_name = 'mk_gnn_preln_d4_gnn_r8_ff053d'

def setup_inputs(seed: int=0):
    np.random.seed(seed)
    _w = jnp.asarray

    def _rec_inputs():
        import jax
        import jax.numpy as jnp
        _gk = jax.random.key(seed)
        x = -0.0008691 + 1 * jax.random.normal(jax.random.fold_in(_gk, 1), (6250, 128), jnp.float32)
        src = jax.random.randint(jax.random.fold_in(_gk, 2), (100000,), 0, 6250, jnp.int32)
        dst = jnp.minimum((6250 * jax.random.uniform(jax.random.fold_in(_gk, 3), (100000,)) ** 2.0).astype(jnp.int32), 49999)
        _o = jnp.argsort(dst, stable=True)
        src = src[_o]
        dst = dst[_o]
        edge_attr_50 = 0.000152336 + 1.00009 * jax.random.normal(jax.random.fold_in(_gk, 12), (100000, 50), jnp.float32)
        edge_weight = jax.random.uniform(jax.random.fold_in(_gk, 14), (100000,), jnp.float32, 0.0, 12)
        return (x, src, dst, edge_attr_50, edge_weight)
    x, src, dst, edge_attr_50, edge_weight = _rec_inputs()

    def _L0_gnn_setup():
        import jax, jax.numpy as jnp
        import numpy as np
        PI = float(np.pi)
        LOG2 = float(np.log(2.0))
        CUTOFF = 10.0
        N_NODES = 1250
        N_EDGES = 80000
        HIDDEN = 128
        NUM_FILTERS = 128
        NUM_GAUSSIANS = 50

        def ssp(x):
            return jax.nn.softplus(x) - LOG2
        key = jax.random.key(seed)
        ks = jax.random.split(key, 12)
        x = jax.random.normal(ks[0], (N_NODES, HIDDEN), dtype=jnp.float32)
        edge_index = jax.random.randint(ks[1], (2, N_EDGES), 0, N_NODES, dtype=jnp.int64)
        edge_length = jax.random.uniform(ks[2], (N_EDGES,), dtype=jnp.float32) * (1.2 * CUTOFF)
        edge_attr = jax.random.normal(ks[3], (N_EDGES, NUM_GAUSSIANS), dtype=jnp.float32)

        def xavier(k, shape):
            fan_in, fan_out = (shape[0], shape[1])
            lim = float(np.sqrt(6.0 / (fan_in + fan_out)))
            return jax.random.uniform(k, shape, dtype=jnp.float32, minval=-lim, maxval=lim)
        mlp_w1 = xavier(ks[4], (NUM_GAUSSIANS, NUM_FILTERS))
        mlp_b1 = jnp.zeros((NUM_FILTERS,), dtype=jnp.float32)
        mlp_w2 = xavier(ks[5], (NUM_FILTERS, NUM_FILTERS))
        mlp_b2 = jnp.zeros((NUM_FILTERS,), dtype=jnp.float32)
        lin1_w = xavier(ks[6], (HIDDEN, NUM_FILTERS))
        lin2_w = xavier(ks[7], (NUM_FILTERS, HIDDEN))
        lin2_b = jnp.zeros((HIDDEN,), dtype=jnp.float32)
        lin_w = xavier(ks[8], (HIDDEN, HIDDEN))
        lin_b = jnp.zeros((HIDDEN,), dtype=jnp.float32)
        return {'x': x, 'edge_index': edge_index, 'edge_length': edge_length, 'edge_attr': edge_attr, 'mlp_w1': mlp_w1, 'mlp_b1': mlp_b1, 'mlp_w2': mlp_w2, 'mlp_b2': mlp_b2, 'lin1_w': lin1_w, 'lin2_w': lin2_w, 'lin2_b': lin2_b, 'lin_w': lin_w, 'lin_b': lin_b}
    _L0_gnn_all = _L0_gnn_setup()
    _L0_gnn_in = {k: v for k, v in _L0_gnn_all.items() if k in ('mlp_w1', 'mlp_b1', 'mlp_w2', 'mlp_b2', 'lin1_w', 'lin2_w', 'lin2_b', 'lin_w', 'lin_b')}
    del _L0_gnn_all

    def _L1_gnn_setup():
        import jax, jax.numpy as jnp
        import numpy as np
        N, IN, H, D = (6250, 128, 4, 32)
        HID = H * D
        E = 100000
        key = jax.random.key(seed)
        ks = jax.random.split(key, 16)
        s_in = 1.0 / np.sqrt(IN)
        s_g = 1.0 / np.sqrt(3 * HID)
        inp = {'feat': jax.random.normal(ks[0], (N, IN), jnp.float32), 'src': jax.random.randint(ks[1], (E,), 0, N, jnp.int32), 'dst': jax.random.randint(ks[2], (E,), 0, N, jnp.int32), 'Wq': jax.random.normal(ks[3], (IN, HID), jnp.float32) * s_in, 'bq': jnp.zeros((HID,), jnp.float32), 'Wk': jax.random.normal(ks[4], (IN, HID), jnp.float32) * s_in, 'bk': jnp.zeros((HID,), jnp.float32), 'Wv': jax.random.normal(ks[5], (IN, HID), jnp.float32) * s_in, 'bv': jnp.zeros((HID,), jnp.float32), 'Ws': jax.random.normal(ks[6], (IN, HID), jnp.float32) * s_in, 'bs': jnp.zeros((HID,), jnp.float32), 'Wg': jax.random.normal(ks[7], (3 * HID, 1), jnp.float32) * s_g, 'bg': jnp.zeros((1,), jnp.float32), 'gamma': jnp.ones((HID,), jnp.float32), 'beta': jnp.zeros((HID,), jnp.float32), 'alpha': jnp.asarray(0.25, jnp.float32)}
        return inp
    _L1_gnn_all = _L1_gnn_setup()
    _L1_gnn_in = {k: v for k, v in _L1_gnn_all.items() if k in ('Wq', 'bq', 'Wk', 'bk', 'Wv', 'bv', 'Ws', 'bs', 'Wg', 'bg', 'gamma', 'beta', 'alpha')}
    del _L1_gnn_all

    def _L2_gnn_setup():
        import jax, jax.numpy as jnp
        import numpy as np
        N_NODES = 12500
        N_EDGES = 200000
        IN_DIM, HID_DIM, OUT_DIM = (128, 64, 128)

        def _glorot(key, shape):
            fan_in, fan_out = (shape[1], shape[0])
            lim = jnp.sqrt(6.0 / (fan_in + fan_out)).astype(jnp.float32)
            return jax.random.uniform(key, shape, jnp.float32, -lim, lim)

        def _mean_aggregate(x, src, dst, num_nodes):
            msg = x[src]
            summed = jax.ops.segment_sum(msg, dst, num_segments=num_nodes)
            deg = jax.ops.segment_sum(jnp.ones_like(dst, jnp.float32), dst, num_segments=num_nodes)
            return summed / jnp.maximum(deg, 1.0)[:, None]

        def _sage_conv(x, src, dst, W_l, W_r, b, num_nodes):
            aggr = _mean_aggregate(x, src, dst, num_nodes)
            return aggr @ W_l.T + b + x @ W_r.T
        key = jax.random.key(seed)
        ks = jax.random.split(key, 8)
        x = jax.random.normal(ks[0], (N_NODES, IN_DIM), jnp.float32)
        edge_index = jax.random.randint(ks[1], (2, N_EDGES), 0, N_NODES, jnp.int32)
        W_l1 = _glorot(ks[2], (HID_DIM, IN_DIM))
        W_r1 = _glorot(ks[3], (HID_DIM, IN_DIM))
        b1 = jnp.zeros((HID_DIM,), jnp.float32)
        W_l2 = _glorot(ks[4], (OUT_DIM, HID_DIM))
        W_r2 = _glorot(ks[5], (OUT_DIM, HID_DIM))
        b2 = jnp.zeros((OUT_DIM,), jnp.float32)
        return {'x': x, 'edge_index': edge_index, 'W_l1': W_l1, 'W_r1': W_r1, 'b1': b1, 'W_l2': W_l2, 'W_r2': W_r2, 'b2': b2}
    _L2_gnn_all = _L2_gnn_setup()
    _L2_gnn_in = {k: v for k, v in _L2_gnn_all.items() if k in ('W_l1', 'W_r1', 'b1', 'W_l2', 'W_r2', 'b2')}
    del _L2_gnn_all

    def _L3_gnn_setup():
        import jax, jax.numpy as jnp
        import numpy as np
        EPS = 1e-07
        N_NODES, N_EDGES, D = (1250, 20000, 128)

        def mobius_add(x, y):
            x2 = jnp.sum(x * x, axis=-1, keepdims=True)
            y2 = jnp.sum(y * y, axis=-1, keepdims=True)
            xy = jnp.sum(x * y, axis=-1, keepdims=True)
            num = (1.0 + 2.0 * xy + y2) * x + (1.0 - x2) * y
            den = 1.0 + 2.0 * xy + x2 * y2
            return num / jnp.maximum(den, EPS)

        def mobius_scalar_mul(r, x):
            nrm = jnp.sqrt(jnp.sum(x * x, axis=-1, keepdims=True))
            nrm_c = jnp.clip(nrm, EPS, 1.0 - EPS)
            scaled = jnp.tanh(r * jnp.arctanh(nrm_c)) * (x / nrm_c)
            return jnp.where(nrm > EPS, scaled, jnp.zeros_like(x))
        key = jax.random.key(seed)
        kx, ke = jax.random.split(key)
        raw = jax.random.normal(kx, (N_NODES, D), dtype=jnp.float32)
        x = 0.4 * raw / (1.0 + jnp.linalg.norm(raw, axis=-1, keepdims=True))
        edge_index = jax.random.randint(ke, (2, N_EDGES), 0, N_NODES, dtype=jnp.int64)
        return {'x': x, 'edge_index': edge_index}
    _L3_gnn_all = _L3_gnn_setup()
    _L3_gnn_in = {k: v for k, v in _L3_gnn_all.items() if k in ()}
    del _L3_gnn_all
    return {'x': x, 'src': src, 'dst': dst, 'edge_attr_50': edge_attr_50, 'edge_weight': edge_weight, 'L0_gnn_mlp_w1': _L0_gnn_in['mlp_w1'], 'L0_gnn_mlp_b1': _L0_gnn_in['mlp_b1'], 'L0_gnn_mlp_w2': _L0_gnn_in['mlp_w2'], 'L0_gnn_mlp_b2': _L0_gnn_in['mlp_b2'], 'L0_gnn_lin1_w': _L0_gnn_in['lin1_w'], 'L0_gnn_lin2_w': _L0_gnn_in['lin2_w'], 'L0_gnn_lin2_b': _L0_gnn_in['lin2_b'], 'L0_gnn_lin_w': _L0_gnn_in['lin_w'], 'L0_gnn_lin_b': _L0_gnn_in['lin_b'], 'L1_gnn_Wq': _L1_gnn_in['Wq'], 'L1_gnn_bq': _L1_gnn_in['bq'], 'L1_gnn_Wk': _L1_gnn_in['Wk'], 'L1_gnn_bk': _L1_gnn_in['bk'], 'L1_gnn_Wv': _L1_gnn_in['Wv'], 'L1_gnn_bv': _L1_gnn_in['bv'], 'L1_gnn_Ws': _L1_gnn_in['Ws'], 'L1_gnn_bs': _L1_gnn_in['bs'], 'L1_gnn_Wg': _L1_gnn_in['Wg'], 'L1_gnn_bg': _L1_gnn_in['bg'], 'L1_gnn_gamma': _L1_gnn_in['gamma'], 'L1_gnn_beta': _L1_gnn_in['beta'], 'L1_gnn_alpha': _L1_gnn_in['alpha'], 'L2_gnn_W_l1': _L2_gnn_in['W_l1'], 'L2_gnn_W_r1': _L2_gnn_in['W_r1'], 'L2_gnn_b1': _L2_gnn_in['b1'], 'L2_gnn_W_l2': _L2_gnn_in['W_l2'], 'L2_gnn_W_r2': _L2_gnn_in['W_r2'], 'L2_gnn_b2': _L2_gnn_in['b2']}

def reference(x, src, dst, edge_attr_50, edge_weight, L0_gnn_mlp_w1, L0_gnn_mlp_b1, L0_gnn_mlp_w2, L0_gnn_mlp_b2, L0_gnn_lin1_w, L0_gnn_lin2_w, L0_gnn_lin2_b, L0_gnn_lin_w, L0_gnn_lin_b, L1_gnn_Wq, L1_gnn_bq, L1_gnn_Wk, L1_gnn_bk, L1_gnn_Wv, L1_gnn_bv, L1_gnn_Ws, L1_gnn_bs, L1_gnn_Wg, L1_gnn_bg, L1_gnn_gamma, L1_gnn_beta, L1_gnn_alpha, L2_gnn_W_l1, L2_gnn_W_r1, L2_gnn_b1, L2_gnn_W_l2, L2_gnn_W_r2, L2_gnn_b2):
    import jax
    import jax.numpy as jnp

    def _L0_gnn_ref(x, edge_index, edge_length, edge_attr, mlp_w1, mlp_b1, mlp_w2, mlp_b2, lin1_w, lin2_w, lin2_b, lin_w, lin_b):
        import jax, jax.numpy as jnp
        import numpy as np
        PI = float(np.pi)
        LOG2 = float(np.log(2.0))
        CUTOFF = 10.0
        N_NODES = 1250
        N_EDGES = 80000
        HIDDEN = 128
        NUM_FILTERS = 128
        NUM_GAUSSIANS = 50

        def ssp(x):
            return jax.nn.softplus(x) - LOG2
        C = 0.5 * (jnp.cos(edge_length * PI / CUTOFF) + 1.0)
        C = C * (edge_length <= CUTOFF) * (edge_length >= 0.0)
        W = ssp(edge_attr @ mlp_w1 + mlp_b1) @ mlp_w2 + mlp_b2
        W = W * C[:, None]
        h = x @ lin1_w
        src, dst = (edge_index[0], edge_index[1])
        msg = h[src] * W
        agg = jax.ops.segment_sum(msg, dst, num_segments=x.shape[0])
        h = agg @ lin2_w + lin2_b
        return ssp(h) @ lin_w + lin_b

    def _L1_gnn_ref(feat, src, dst, Wq, bq, Wk, bk, Wv, bv, Ws, bs, Wg, bg, gamma, beta, alpha):
        import jax, jax.numpy as jnp
        import numpy as np
        N, IN, H, D = (6250, 128, 4, 32)
        HID = H * D
        E = 100000
        n = feat.shape[0]
        q = (feat @ Wq + bq).reshape(n, H, D)
        k = (feat @ Wk + bk).reshape(n, H, D)
        v = (feat @ Wv + bv).reshape(n, H, D)
        a = jnp.einsum('ehd,ehd->eh', q[src], k[dst]) / jnp.sqrt(jnp.float32(D))
        m = jax.ops.segment_max(a, dst, num_segments=n)
        m = jax.lax.stop_gradient(jnp.where(jnp.isfinite(m), m, 0.0))
        ex = jnp.exp(a - m[dst])
        denom = jax.ops.segment_sum(ex, dst, num_segments=n)
        denom = jnp.where(denom > 0, denom, 1.0)
        sa = ex / denom[dst]
        msg = v[src] * sa[:, :, None]
        agg = jax.ops.segment_sum(msg, dst, num_segments=n).reshape(n, HID)
        skip = feat @ Ws + bs
        g = jax.nn.sigmoid(jnp.concatenate([skip, agg, skip - agg], axis=-1) @ Wg + bg)
        rst = g * skip + (1.0 - g) * agg
        mu = rst.mean(-1, keepdims=True)
        var = rst.var(-1, keepdims=True)
        rst = (rst - mu) * jax.lax.rsqrt(var + 1e-05) * gamma + beta
        rst = jnp.where(rst >= 0, rst, alpha * rst)
        return rst

    def _L2_gnn_ref(x, edge_index, W_l1, W_r1, b1, W_l2, W_r2, b2):
        import jax, jax.numpy as jnp
        import numpy as np
        N_NODES = 12500
        N_EDGES = 200000
        IN_DIM, HID_DIM, OUT_DIM = (128, 64, 128)

        def _glorot(key, shape):
            fan_in, fan_out = (shape[1], shape[0])
            lim = jnp.sqrt(6.0 / (fan_in + fan_out)).astype(jnp.float32)
            return jax.random.uniform(key, shape, jnp.float32, -lim, lim)

        def _mean_aggregate(x, src, dst, num_nodes):
            msg = x[src]
            summed = jax.ops.segment_sum(msg, dst, num_segments=num_nodes)
            deg = jax.ops.segment_sum(jnp.ones_like(dst, jnp.float32), dst, num_segments=num_nodes)
            return summed / jnp.maximum(deg, 1.0)[:, None]

        def _sage_conv(x, src, dst, W_l, W_r, b, num_nodes):
            aggr = _mean_aggregate(x, src, dst, num_nodes)
            return aggr @ W_l.T + b + x @ W_r.T
        src, dst = (edge_index[0], edge_index[1])
        n = x.shape[0]
        h = _sage_conv(x, src, dst, W_l1, W_r1, b1, n)
        h = jax.nn.relu(h)
        out = _sage_conv(h, src, dst, W_l2, W_r2, b2, n)
        return out

    def _L3_gnn_ref(x, edge_index):
        import jax, jax.numpy as jnp
        import numpy as np
        EPS = 1e-07
        N_NODES, N_EDGES, D = (1250, 20000, 128)

        def mobius_add(x, y):
            x2 = jnp.sum(x * x, axis=-1, keepdims=True)
            y2 = jnp.sum(y * y, axis=-1, keepdims=True)
            xy = jnp.sum(x * y, axis=-1, keepdims=True)
            num = (1.0 + 2.0 * xy + y2) * x + (1.0 - x2) * y
            den = 1.0 + 2.0 * xy + x2 * y2
            return num / jnp.maximum(den, EPS)

        def mobius_scalar_mul(r, x):
            nrm = jnp.sqrt(jnp.sum(x * x, axis=-1, keepdims=True))
            nrm_c = jnp.clip(nrm, EPS, 1.0 - EPS)
            scaled = jnp.tanh(r * jnp.arctanh(nrm_c)) * (x / nrm_c)
            return jnp.where(nrm > EPS, scaled, jnp.zeros_like(x))
        src, dst = (edge_index[0], edge_index[1])
        n, d = x.shape
        messages = mobius_add(x[src], -x[dst])

        def body(out, em):
            m, idx = em
            return (out.at[idx].set(mobius_add(out[idx], m)), None)
        out0 = jnp.zeros((n, d), dtype=x.dtype)
        total, _ = jax.lax.scan(body, out0, (messages, dst))
        count = jnp.zeros((n,), dtype=x.dtype).at[dst].add(1.0)
        scale = 1.0 / jnp.maximum(count, 1.0)
        aggr = mobius_scalar_mul(scale[:, None], total)
        return mobius_add(x, aggr)
    edge_index = jnp.stack([src, dst])
    h = jnp.maximum(_layernorm(x, axis=-1), 0.0)
    x = x + _L0_gnn_ref(h, edge_index, edge_weight, edge_attr_50, L0_gnn_mlp_w1, L0_gnn_mlp_b1, L0_gnn_mlp_w2, L0_gnn_mlp_b2, L0_gnn_lin1_w, L0_gnn_lin2_w, L0_gnn_lin2_b, L0_gnn_lin_w, L0_gnn_lin_b)
    h = jnp.maximum(_layernorm(x, axis=-1), 0.0)
    x = x + _L1_gnn_ref(h, src, dst, L1_gnn_Wq, L1_gnn_bq, L1_gnn_Wk, L1_gnn_bk, L1_gnn_Wv, L1_gnn_bv, L1_gnn_Ws, L1_gnn_bs, L1_gnn_Wg, L1_gnn_bg, L1_gnn_gamma, L1_gnn_beta, L1_gnn_alpha)
    h = jnp.maximum(_layernorm(x, axis=-1), 0.0)
    x = x + _L2_gnn_ref(h, edge_index, L2_gnn_W_l1, L2_gnn_W_r1, L2_gnn_b1, L2_gnn_W_l2, L2_gnn_W_r2, L2_gnn_b2)
    h = jnp.maximum(_layernorm(x, axis=-1), 0.0)
    x = x + _L3_gnn_ref(h, edge_index)
    return x

_drawn_inputs = setup_inputs


def setup_inputs(seed=0):
    import zlib

    import numpy as np

    out = dict(_drawn_inputs(seed))
    spreads = {'L0_gnn_mlp_b1': (0.0, 0.1),
     'L0_gnn_mlp_b2': (0.0, 0.1),
     'L0_gnn_lin2_b': (0.0, 0.1),
     'L0_gnn_lin_b': (0.0, 0.1),
     'L1_gnn_bq': (0.0, 0.8),
     'L1_gnn_bk': (0.0, 0.8),
     'L1_gnn_bv': (0.0, 0.1),
     'L1_gnn_bs': (0.0, 0.1),
     'L1_gnn_gamma': (1.0, 0.2),
     'L1_gnn_beta': (0.0, 0.1),
     'L2_gnn_b1': (0.0, 0.1),
     'L2_gnn_b2': (0.0, 0.1)}
    factors = {}
    for name, (base, spread) in spreads.items():
        noise = np.random.default_rng([zlib.crc32(name.encode()), seed]).standard_normal(out[name].shape)
        drawn = base * np.exp(spread * noise) if base else spread * noise
        out[name] = jnp.asarray(drawn.astype(out[name].dtype))
    for name, factor in factors.items():
        out[name] = (out[name] * factor).astype(out[name].dtype)
    return out
```

```python
import numpy as np
import concourse.bass as bass
from concourse import mybir
from contextlib import ExitStack, contextmanager

F32 = mybir.dt.float32
I32 = mybir.dt.int32
ALU = mybir.AluOpType
ACT = mybir.ActivationFunctionType
AX = mybir.AxisListType

P = 128
N = 6250
E = 100000
D = 128
H = 4
DH = D // H
NG = 50
G = -(-N // P)
GB = G + G % 2
NP = GB * P
C = -(-E // P)
U = 8
K = -(-(C + G - 1) // U) * U
IT = K // U
KT7 = -(-K // P)
KP = KT7 * P
MW = 132
FARAWAY = 1 << 20
EPS_LN = 1e-5
EPS_M = 1e-7
BIG = 1e30
LOG2 = float(np.log(2.0))


def build(nc, a, out, stop=None):
    dram = lambda name, shape, dt=F32: nc.dram_tensor(name, shape, dt, kind="Internal").ap()
    T0 = dram("T0", (NP, D))
    QV = dram("QV", (NP, 2 * D))
    VE = dram("VE", (K, P, D))
    SEQ = dram("SEQ", (H, KP * P))
    KEY = dram("KEY", (P + KP * P,))
    SEX = dram("SEX", (H, K * P))
    Y1 = dram("Y1", (NP, 64))
    H2 = dram("H2", (NP, 64))
    H3 = dram("H3", (NP, MW))
    MSG = dram("MSG", (K * P, MW))

    name_uses = {}

    def unique(name):
        name_uses[name] = name_uses.get(name, 0) + 1
        return name if name_uses[name] == 1 else f"{name}_{name_uses[name]}"

    def tile(name, shape, dt=F32):
        return nc.sbuf_tensor(unique(name), shape, dt)

    with ExitStack() as ctx:
        def sb(name, shape, dt=F32):
            return ctx.enter_context(tile(name, shape, dt))

        X = sb("X", [P, GB * D])
        AGG = sb("AGG", [P, GB * 136])
        TAB = sb("TAB", [P, GB * MW])
        Z = sb("Z", [P, GB * D])
        SCR = sb("SCR", [P, GB * D])
        srci = sb("srci", [P, KP], I32)
        drel = sb("drel", [P, KP])
        dkey = sb("dkey", [P, KP])
        cut = sb("cut", [P, KP])
        A = sb("A", [P, H, KP])
        gidx = sb("gidx", [1, KP], I32)
        cidx = sb("cidx", [1, KP], I32)
        ident = sb("ident", [P, P])
        iota = sb("iota", [P, P])
        ones = sb("ones", [P, P])
        cnt = sb("cnt", [P, GB])
        banks = [ctx.enter_context(nc.psum_tensor(f"bank{i}", [P, 512], F32)) for i in range(8)]

        gat = ctx.enter_context(nc.semaphore("gat"))
        gathered = [ctx.enter_context(nc.semaphore(f"gathered{j}")) for j in range(U)]
        passes = [0]

        def landed(it):
            return it * 16 + (16 + passes[0] * 16 * IT)

        @contextmanager
        def phase(names):
            with ExitStack() as st:
                sems = [st.enter_context(nc.semaphore(unique(n))) for n in names.split()]
                with nc.Block() as block:
                    yield block, sems
                nc.gpsimd.sem_clear(range(min(s.num for s in sems), max(s.num for s in sems) + 1))
                nc.all_engine_barrier()

        def scratch():
            return ExitStack()

        with scratch() as st:
            tb = lambda name, shape, dt=F32: st.enter_context(tile(name, shape, dt))
            lasti = tb("lasti", [P, C], I32)
            L = tb("L", [P, C])
            Lj = tb("Lj", [P, C])
            kcol = tb("kcol", [P, KT7])
            ccol = tb("ccol", [P, KT7])
            gcol = tb("gcol", [P, KT7])
            ccoli = tb("ccoli", [P, KT7], I32)
            rs = tb("rs", [P, KT7, P], I32)
            rd = tb("rd", [P, KT7, P], I32)
            re = tb("re", [P, KT7, P])
            rf = tb("rf", [P, 2, KT7, P])
            wide = tb("wide", [P, 2, P])
            half_pi = tb("half_pi", [P, 1])
            with phase("ld pool rowc tr evac dv sn") as (block, (ld, pool, rowc, tr, evac, dv, sn)):
                @block.sync
                def _(sp):
                    sp.dma_start(lasti[:, :], a["dst_last"].rearrange("(a n) -> a n", a=1).broadcast_to([P, C])).then_inc(ld, 16)
                    sp.dma_start(X[:, :].rearrange("p (g f) -> p g f", f=D), a["x"].rearrange("(g p) f -> p g f", p=P)).then_inc(ld, 16)

                @block.gpsimd
                def _(po):
                    po.memset(ident[:, :], 0.0).then_inc(pool, 1)
                    po.memset(ones[:, :], 1.0)
                    po.memset(half_pi[:, :], float(np.pi / 2))
                    po.memset(A[:, :, K:KP], 0.0)
                    po.iota(iota[:, :], [[1, P]], base=0, channel_multiplier=0, allow_small_or_imprecise_dtypes=True)
                    po.iota(L[:, :], [[1, C]], base=0, channel_multiplier=0, allow_small_or_imprecise_dtypes=True)
                    po.iota(kcol[:, :], [[P, KT7]], base=0, channel_multiplier=1, allow_small_or_imprecise_dtypes=True)
                    po.wait_ge(pool, 1)
                    po.affine_select(out=ident[:, :], in_=ident[:, :], compare_op=ALU.not_equal, fill=1.0, base=0,
                                     pattern=[[-1, P]], channel_multiplier=1).then_inc(pool, 1)
                    po.wait_ge(rowc, 1)
                    for t in range(KT7):
                        for dst, tab in ((rs, a["src2d"]), (rd, a["dst2d"]), (re, a["ew2d"])):
                            po.indirect_dma_start(out=dst[:, t, :], out_offset=None, in_=tab[:, :],
                                                  in_offset=bass.IndirectOffsetOnAxis(ap=ccoli[:, t:t + 1], axis=0)).then_inc(gat, 16)

                @block.vector
                def _(v):
                    n = [0]

                    def link(ins):
                        n[0] += 1
                        ins.then_inc(dv, 1)
                        v.wait_ge(dv, n[0])

                    v.wait_ge(ld, 32)
                    v.wait_ge(pool, 2)
                    link(v.tensor_scalar(lasti[:, :], lasti[:, :], 7, None, ALU.arith_shift_right))
                    link(v.tensor_scalar(Lj[:, :], lasti[:, :], float(G - 1), None, ALU.min))
                    link(v.tensor_tensor(L[:, :], L[:, :], Lj[:, :], ALU.add))
                    for t in range(KT7):
                        link(v.tensor_scalar(Lj[:, :], L[:, :], kcol[:, t:t + 1], 0.0, ALU.is_lt, ALU.add,
                                             accum_out=ccol[:, t:t + 1]))
                    link(v.tensor_tensor(gcol[:, :], kcol[:, :], ccol[:, :], ALU.subtract))
                    link(v.tensor_scalar(gcol[:, :], gcol[:, :], float(G - 1), None, ALU.min))
                    v.tensor_copy(ccoli[:, :], ccol[:, :]).then_inc(rowc, 1)
                    v.wait_ge(gat, 16 * 3 * KT7)
                    v.tensor_copy(rf[:, 0, :, :], rs[:, :, :])
                    link(v.tensor_copy(rf[:, 1, :, :], rd[:, :, :]))
                    for t in range(KT7):
                        cols = slice(t * P, (t + 1) * P)
                        if t:
                            v.wait_ge(tr, t)
                        v.tensor_copy(wide[:, 0, :], gcol[:, t:t + 1].broadcast_to([P, P]))
                        link(v.tensor_copy(wide[:, 1, :], ccol[:, t:t + 1].broadcast_to([P, P])))
                        v.sem_inc(rowc, 1)
                        v.wait_ge(tr, t + 1)
                        bk = banks[0]
                        v.tensor_copy(srci[:, cols], bk[:, 0:P])
                        v.tensor_copy(cut[:, cols], bk[:, 2 * P:3 * P])
                        link(v.tensor_copy(dkey[:, cols], bk[:, P:2 * P]))
                        v.scalar_tensor_tensor(drel[:, cols], banks[1][:, 0:P], -float(P), dkey[:, cols], ALU.mult, ALU.add)
                        v.tensor_copy(gidx[0:1, cols], banks[1][0:1, 0:P])
                        link(v.tensor_copy(cidx[0:1, cols], banks[1][0:1, P:2 * P]))
                        v.sem_inc(evac, 1)
                    w = cut[:, :]
                    s = SCR[:, 0:KP]
                    q = SCR[:, KP:2 * KP]
                    link(v.tensor_scalar(s, w, 10.0, None, ALU.is_le))
                    link(v.scalar_tensor_tensor(q, w, 0.0, s, ALU.is_ge, ALU.mult))
                    link(v.tensor_scalar(w, w, 0.0, 10.0, ALU.max, ALU.min))
                    v.sem_inc(evac, 1)
                    v.wait_ge(sn, 1)
                    link(v.tensor_scalar(w, w, 0.5, 0.5, ALU.mult, ALU.add))
                    link(v.tensor_tensor(w, w, q, ALU.mult))

                @block.tensor
                def _(pe):
                    pe.wait_ge(pool, 2)
                    for t in range(KT7):
                        pe.wait_ge(rowc, t + 2)
                        if t:
                            pe.wait_ge(evac, t)
                        pe.transpose(banks[0][:, 0:P], rf[:, 0, t, :], ident[:, :])
                        pe.transpose(banks[0][:, P:2 * P], rf[:, 1, t, :], ident[:, :])
                        pe.transpose(banks[0][:, 2 * P:3 * P], re[:, t, :], ident[:, :])
                        pe.matmul(banks[1][:, 0:P], wide[:, 0, :], ident[:, :], start=True, stop=True)
                        pe.matmul(banks[1][:, P:2 * P], wide[:, 1, :], ident[:, :], start=True, stop=True).then_inc(tr, 1)

                @block.scalar
                def _(ac):
                    ac.wait_ge(evac, KT7 + 1)
                    ac.activation(cut[:, :], cut[:, :], ACT.Sin, bias=half_pi[:, :], scale=-float(np.pi / 10)).then_inc(sn, 1)
        if stop == "items":
            with phase("o") as (block, (o,)):
                @block.sync
                def _(sp):
                    for i, t in enumerate((drel, dkey, cut)):
                        sp.dma_start(out[i * P:(i + 1) * P, :], t[:, 700:828]).then_inc(o, 16)
                    sp.wait_ge(o, 48)
            return

        weights = {}

        def load_weights(names):
            with phase("ld") as (block, (ld,)):
                @block.sync
                def _(sp):
                    for n in names:
                        sp.dma_start(weights[n][:, :], a[n]).then_inc(ld, 16)
                    sp.wait_ge(ld, 16 * len(names))

        def steps(eng, count, body):
            body(0, True)
            with eng.Fori(1, count) as it:
                body(it, False)

        Xg = X[:, :].rearrange("p (g f) -> p g f", f=D)
        SCRg = SCR[:, :].rearrange("p (g f) -> p g f", f=D)
        Zg = Z[:, :].rearrange("p (g f) -> p g f", f=D)
        stats = sb("stats", [P, 4, GB])
        rstd = stats[:, 3, :]

        def rsqrt_chain(link, v, ac_done, y, var, t):
            link(v.tensor_tensor(t, y, y, ALU.mult))
            link(v.tensor_tensor(t, t, var, ALU.mult))
            link(v.tensor_scalar(t, t, -0.5, 1.5, ALU.mult, ALU.add))
            link(v.tensor_tensor(y, y, t, ALU.mult))

        def normalise(src, squares):
            with phase("cen sq lnexp dv") as (block, (cen, sq, lnexp, dv)):
                @block.vector
                def _(v):
                    n = [0]

                    def link(ins):
                        n[0] += 1
                        ins.then_inc(dv, 1)
                        v.wait_ge(dv, n[0])

                    mean, ssq, tmp, y = (stats[:, j, :] for j in range(4))
                    link(v.tensor_reduce(mean, src, AX.X, ALU.add))
                    link(v.tensor_scalar(mean, mean, 1.0 / D, None, ALU.mult))
                    v.tensor_tensor(SCRg, src, mean.unsqueeze(2).broadcast_to([P, GB, D]), ALU.subtract).then_inc(cen, 1)
                    v.wait_ge(sq, 1)
                    link(v.tensor_reduce(ssq, squares.rearrange("p (g f) -> p g f", f=D), AX.X, ALU.add))
                    v.tensor_scalar(ssq, ssq, 1.0 / D, EPS_LN, ALU.mult, ALU.add).then_inc(cen, 1)
                    v.wait_ge(lnexp, 2)
                    rsqrt_chain(link, v, None, y, ssq, tmp)
                    rsqrt_chain(link, v, None, y, ssq, tmp)

                @block.scalar
                def _(ac):
                    ac.preload_act_table_set("natural_log_exp_and_others")
                    ac.wait_ge(cen, 1)
                    ac.activation(squares, SCR[:, :], ACT.Square).then_inc(sq, 1)
                    ac.wait_ge(cen, 2)
                    ac.activation(stats[:, 2, :], stats[:, 1, :], ACT.Ln).then_inc(lnexp, 1)
                    ac.wait_ge(lnexp, 1)
                    ac.activation(stats[:, 3, :], stats[:, 2, :], ACT.Exp, scale=-0.5).then_inc(lnexp, 1)

        def relu_norm_block(v, g, out_tile):
            return v.tensor_scalar(out_tile, SCR[:, bass.ds(g * D, D)], 0.0, stats[:, 3, bass.ds(g, 1)], ALU.max, ALU.mult)

        def node_products(fill, W, bias, take, taker, store=None, store_cols=0):
            width = W.shape[1]
            with scratch() as st:
                hb = st.enter_context(tile("hb", [P, 2, P], F32))
                hT = st.enter_context(tile("hT", [P, 2, P], F32))
                ob = st.enter_context(tile("ob", [P, 2, max(store_cols, 1)], F32))
                with phase("filled transposed copied product taken stored0 stored1 self") as (
                        block, (filled, transposed, copied, product, taken, stored0, stored1, own)):
                    stored = (stored0, stored1)

                    def taking(eng, it, b, first, pending):
                        g = it * 2 + b
                        eng.wait_ge(product, g + 1)
                        if store is not None and not first:
                            eng.wait_ge(stored[b], it * 16)
                        take(eng, g, banks[2 + b], ob[:, b, :]).then_inc(taken, 1)

                    @block.vector
                    def _(v):
                        def body(it, first):
                            for b in range(2):
                                if not first:
                                    v.wait_ge(transposed, it * 2 + b - 1)
                                fill(v, it * 2 + b, hb[:, b, :]).then_inc(filled, 1)
                            if taker == "vector":
                                for b in range(2):
                                    taking(v, it, b, first, None)
                        steps(v, GB // 2, body)

                    @block.tensor
                    def _(pe):
                        def body(it, first):
                            for b in range(2):
                                pe.wait_ge(filled, it * 2 + b + 1)
                                if not first:
                                    pe.wait_ge(copied, it * 2 + b - 1)
                                pe.transpose(banks[b][:, 0:P], hb[:, b, :], ident[:, :]).then_inc(transposed, 1)
                            for b in range(2):
                                pe.wait_ge(copied, it * 2 + b + 1)
                                if not first:
                                    pe.wait_ge(taken, it * 2 + b - 1)
                                po = banks[2 + b][:, 0:width]
                                pe.matmul(po, ones[0:1, :], bias[0:1, :], start=True, stop=False)
                                pe.matmul(po, hT[:, b, :], W[:, :], start=False, stop=True).then_inc(product, 1)
                        steps(pe, GB // 2, body)

                    @block.scalar
                    def _(ac):
                        def body(it, first):
                            for b in range(2):
                                ac.wait_ge(transposed, it * 2 + b + 1)
                                if not first:
                                    ac.wait_ge(product, it * 2 + b - 1)
                                ac.activation(hT[:, b, :], banks[b][:, 0:P], ACT.Copy).then_inc(copied, 1)
                            if taker == "scalar":
                                for b in range(2):
                                    taking(ac, it, b, first, None)
                        steps(ac, GB // 2, body)

                    if store is not None:
                        @block.sync
                        def _(sp):
                            def body(it, first):
                                for b in range(2):
                                    sp.wait_ge(taken, it * 2 + b + 1)
                                    sp.dma_start(store[bass.ds((it * 2 + b) * P, P), :], ob[:, b, :]).then_inc(stored[b], 16)
                            steps(sp, GB // 2, body)
                            for b in range(2):
                                sp.wait_ge(stored[b], 16 * (GB // 2))

        w = scratch()
        tbw = lambda name, shape: w.enter_context(tile(f"w_{name}", shape, F32))
        for n, shape in (("lin1", [D, D]), ("w1", [NG, D]), ("b1", [D, 1]), ("w2", [D, D]), ("b2", [1, D]), ("b2w", [1, 512])):
            weights[n] = tbw(n, shape)
        zero_row = tbw("zero_row", [1, D])
        b1m = tbw("b1m", [D, 1])
        load_weights(["lin1", "w1", "b1", "w2", "b2"])
        normalise(Xg, TAB[:, 0:GB * D])
        with phase("a b") as (block, (sa, sbb)):
            @block.tensor
            def _(pe):
                pe.matmul(banks[0][0:1, 0:D], ones[:, 0:1], weights["w2"][:, :], start=True, stop=True).then_inc(sa, 1)

            @block.vector
            def _(v):
                v.memset(zero_row[:, :], 0.0)
                v.tensor_scalar(b1m[:, :], weights["b1"][:, :], -30.0, None, ALU.add)
                v.wait_ge(sa, 1)
                for j in range(4):
                    v.scalar_tensor_tensor(weights["b2w"][:, j * D:(j + 1) * D], banks[0][0:1, 0:D], -LOG2, weights["b2"][:, :], ALU.mult, ALU.add)

        node_products(lambda v, g, t: relu_norm_block(v, g, t), weights["lin1"], zero_row,
                      lambda e, g, ps, t: e.activation(t, ps[:, 0:D], ACT.Copy), "scalar", T0, D)

        AGGT = AGG[:, 0:GB * P]
        with scratch() as st:
            tb = lambda name, shape, dt=F32: st.enter_context(tile(name, shape, dt))
            gb = tb("gb", [P, U, D])
            ab = tb("ab", [NG, U, P])
            ic = tb("ic", [P, 2, 4], I32)
            dc = tb("dc", [P, 2, U])
            xm = tb("xm", [P, 2, 512])
            rx = tb("rx", [P, 2, 512])
            ms = tb("ms", [P, 4, D])
            oh = tb("oh", [P, 4, P])
            with phase("at0 at1 at2 at3 at4 at5 at6 at7 icr mm1 xmr acr spr mm2 msr mm3 own") as (block, S):
                got, att = gathered, S[0:8]
                icr, mm1, xmr, acr, spr, mm2, msr, mm3, own = S[8:]

                @block.gpsimd
                def _(po):
                    def body(it, first):
                        for h in range(2):
                            if not first:
                                po.wait_ge(msr, (it - 1) * U + 4 * h + 4)
                            po.tensor_copy(ic[:, h, :], srci[:, bass.ds(it * U + 4 * h, 4)]).then_inc(icr, 1)
                            po.wait_ge(icr, it * 2 + h + 1)
                            po.nop(nofuse=True)
                            for j in range(4):
                                po.indirect_dma_start(out=gb[:, 4 * h + j, :], out_offset=None, in_=T0[:, :],
                                                      in_offset=bass.IndirectOffsetOnAxis(ap=ic[:, h, j:j + 1], axis=0)).then_inc(got[4 * h + j], 16)
                    steps(po, IT, body)

                @block.sync
                def _(sp):
                    regs = [sp.register(unique(f"chunk{j}")) for j in range(U)]
                    regs = [st.enter_context(r) for r in regs]

                    def body(it, first):
                        sp.load(regs, cidx[0:1, bass.ds(it * U, U)])
                        for j in range(U):
                            if not first and j % 4 == 0:
                                sp.wait_ge(mm1, (it - 1) * 2 + j // 4 + 1)
                            c = sp.snap(regs[j], min_val=0, max_val=C)
                            sp.dma_start(ab[:, j, :], a["attrT"][:, bass.ds(c * P, P)]).then_inc(att[j], 16)
                    steps(sp, IT, body)

                @block.tensor
                def _(pe):
                    def body(it, first):
                        for h in range(2):
                            hh = it * 2 + h
                            if not first:
                                pe.wait_ge(xmr, hh - 1)
                                pe.wait_ge(acr, (hh - 2) * 3 + 3)
                            for j in range(4):
                                pe.wait_ge(att[4 * h + j], it * 16 + 16)
                                last = pe.matmul(banks[h][:, j * P:(j + 1) * P], weights["w1"][:, :], ab[:, 4 * h + j, :], start=True, stop=True)
                            last.then_inc(mm1, 1)
                        for h in range(2):
                            hh = it * 2 + h
                            pe.wait_ge(spr, hh + 1)
                            if not first:
                                pe.wait_ge(msr, (hh - 2) * 4 + 4)
                            pe.matmul(banks[2 + h][:, 0:512], ones[0:1, :], weights["b2w"][0:1, :], start=True, stop=False)
                            for j in range(4):
                                last = pe.matmul(banks[2 + h][:, j * P:(j + 1) * P], rx[:, h, j * P:(j + 1) * P], weights["w2"][:, :],
                                                 start=False, stop=(j == 3))
                            last.then_inc(mm2, 1)
                            for j in range(4):
                                k = hh * 4 + j
                                pe.wait_ge(msr, k + 1)
                                pe.matmul(banks[4 + j][:, 0:P], ms[:, j, :], oh[:, j, :], start=True, stop=True).then_inc(mm3, 1)
                    steps(pe, IT, body)

                @block.scalar
                def _(ac):
                    def body(it, first):
                        for h in range(2):
                            hh = it * 2 + h
                            ac.wait_ge(xmr, hh + 1)
                            ac.activation(xm[:, h, :], xm[:, h, :], ACT.Exp).then_inc(acr, 1)
                            if not first:
                                ac.wait_ge(mm2, hh - 1)
                            ac.activation(rx[:, h, :], banks[h][:, 0:512], ACT.Relu, bias=b1m[:, :]).then_inc(acr, 1)
                            ac.wait_ge(acr, hh * 3 + 1)
                            ac.activation(xm[:, h, :], xm[:, h, :], ACT.Ln, bias=1.0).then_inc(acr, 1)
                    steps(ac, IT, body)

                @block.vector
                def _(v):
                    regs = [st.enter_context(v.register(unique(f"blk{j}"))) for j in range(U)]
                    v.memset(AGGT, 0.0).then_inc(own, 1)

                    def body(it, first):
                        v.load(regs, gidx[0:1, bass.ds(it * U, U)])
                        v.wait_ge(own, it * (U + 1) + 1)
                        v.tensor_copy(dc[:, 0, :], drel[:, bass.ds(it * U, U)])
                        v.tensor_copy(dc[:, 1, :], cut[:, bass.ds(it * U, U)]).then_inc(own, 1)
                        for h in range(2):
                            hh = it * 2 + h
                            v.wait_ge(mm1, hh + 1)
                            v.tensor_scalar(xm[:, h, :], banks[h][:, 0:512], weights["b1"][:, :], 30.0, ALU.add, ALU.min).then_inc(xmr, 1)
                        v.wait_ge(own, it * (U + 1) + 2)
                        for h in range(2):
                            hh = it * 2 + h
                            v.wait_ge(acr, hh * 3 + 3)
                            v.tensor_tensor(rx[:, h, :], rx[:, h, :], xm[:, h, :], ALU.add).then_inc(spr, 1)
                            for j in range(4):
                                k = hh * 4 + j
                                if j == 0:
                                    v.wait_ge(mm2, hh + 1)
                                v.wait_ge(got[4 * h + j], landed(it))
                                v.scalar_tensor_tensor(ms[:, j, :], banks[2 + h][:, j * P:(j + 1) * P], dc[:, 1, 4 * h + j:4 * h + j + 1],
                                                       gb[:, 4 * h + j, :], ALU.mult, ALU.mult)
                                v.tensor_scalar(oh[:, j, :], iota[:, :], dc[:, 0, 4 * h + j:4 * h + j + 1], None, ALU.is_equal).then_inc(msr, 1)
                            for j in range(4):
                                k = hh * 4 + j
                                g = v.snap(regs[4 * h + j], min_val=0, max_val=G - 1)
                                v.wait_ge(mm3, k + 1)
                                if h or j:
                                    v.wait_ge(own, it * (U + 1) + 2 + 4 * h + j)
                                acc = AGG[:, bass.ds(g * P, P)]
                                v.tensor_tensor(acc, acc, banks[4 + j][:, 0:P], ALU.add).then_inc(own, 1)
                    steps(v, IT, body)
        passes[0] += 1
        w.close()
        if stop == "l0":
            with phase("o") as (block, (o,)):
                @block.sync
                def _(sp):
                    for g in range(48):
                        sp.dma_start(out[g * P:(g + 1) * P, :], AGGT[:, g * P:(g + 1) * P]).then_inc(o, 16)
                    sp.wait_ge(o, 16 * 48)
            return

        w = scratch()
        for n, shape in (("lin2", [D, D]), ("lin2b", [D, 1]), ("lin", [D, D]), ("linb", [1, D])):
            weights[n] = tbw(n, shape)
        lin2bm = tbw("lin2bm", [D, 1])
        load_weights(["lin2", "lin2b", "lin", "linb"])
        with phase("a b") as (block, (sa, sbb)):
            @block.tensor
            def _(pe):
                pe.matmul(banks[0][0:1, 0:D], ones[:, 0:1], weights["lin"][:, :], start=True, stop=True).then_inc(sa, 1)

            @block.vector
            def _(v):
                v.tensor_scalar(lin2bm[:, :], weights["lin2b"][:, :], -30.0, None, ALU.add)
                v.wait_ge(sa, 1)
                v.scalar_tensor_tensor(weights["linb"][:, :], banks[0][0:1, 0:D], -LOG2, weights["linb"][:, :], ALU.mult, ALU.add)
        with scratch() as st:
            xm = st.enter_context(tile("xm", [P, 2, P], F32))
            rx = st.enter_context(tile("rx", [P, 2, P], F32))
            with phase("mm1 xmr acr spr mm2 added") as (block, (mm1, xmr, acr, spr, mm2, added)):
                @block.tensor
                def _(pe):
                    def body(it, first):
                        for b in range(2):
                            g = it * 2 + b
                            if not first:
                                pe.wait_ge(xmr, g - 1)
                                pe.wait_ge(acr, (g - 2) * 3 + 3)
                            pe.matmul(banks[b][:, 0:P], weights["lin2"][:, :], AGG[:, bass.ds(g * P, P)], start=True, stop=True).then_inc(mm1, 1)
                        for b in range(2):
                            g = it * 2 + b
                            pe.wait_ge(spr, g + 1)
                            if not first:
                                pe.wait_ge(added, g - 1)
                            pe.matmul(banks[2 + b][:, 0:D], ones[0:1, :], weights["linb"][0:1, :], start=True, stop=False)
                            pe.matmul(banks[2 + b][:, 0:D], rx[:, b, :], weights["lin"][:, :], start=False, stop=True).then_inc(mm2, 1)
                    steps(pe, GB // 2, body)

                @block.scalar
                def _(ac):
                    def body(it, first):
                        for b in range(2):
                            g = it * 2 + b
                            ac.wait_ge(xmr, g + 1)
                            ac.activation(xm[:, b, :], xm[:, b, :], ACT.Exp).then_inc(acr, 1)
                            if not first:
                                ac.wait_ge(mm2, g - 1)
                            ac.activation(rx[:, b, :], banks[b][:, 0:P], ACT.Relu, bias=lin2bm[:, :]).then_inc(acr, 1)
                            ac.wait_ge(acr, g * 3 + 1)
                            ac.activation(xm[:, b, :], xm[:, b, :], ACT.Ln, bias=1.0).then_inc(acr, 1)
                    steps(ac, GB // 2, body)

                @block.vector
                def _(v):
                    def body(it, first):
                        for b in range(2):
                            g = it * 2 + b
                            v.wait_ge(mm1, g + 1)
                            if not first:
                                v.wait_ge(spr, g - 1)
                            v.tensor_scalar(xm[:, b, :], banks[b][:, 0:P], weights["lin2b"][:, :], 30.0, ALU.add, ALU.min).then_inc(xmr, 1)
                        for b in range(2):
                            g = it * 2 + b
                            v.wait_ge(acr, g * 3 + 3)
                            v.tensor_tensor(rx[:, b, :], rx[:, b, :], xm[:, b, :], ALU.add).then_inc(spr, 1)
                        for b in range(2):
                            g = it * 2 + b
                            v.wait_ge(mm2, g + 1)
                            xb = X[:, bass.ds(g * D, D)]
                            v.tensor_tensor(xb, xb, banks[2 + b][:, 0:D], ALU.add).then_inc(added, 1)
                    steps(v, GB // 2, body)
        w.close()
        normalise(Xg, TAB[:, 0:GB * D])

        w = scratch()
        for n, shape in (("wqvks", [D, 4 * D]), ("bqvks", [1, 4 * D])):
            weights[n] = tbw(n, shape)
        load_weights(["wqvks", "bqvks"])

        def take_qvks(e, g, ps, t):
            e.activation(TAB[:, bass.ds(g * MW, D)], ps[:, 2 * D:3 * D], ACT.Copy)
            e.activation(Z[:, bass.ds(g * D, D)], ps[:, 3 * D:4 * D], ACT.Copy)
            return e.activation(t, ps[:, 0:2 * D], ACT.Copy)

        node_products(relu_norm_block, weights["wqvks"], weights["bqvks"], take_qvks, "scalar", QV, 2 * D)
        w.close()

        with scratch() as st:
            tb = lambda name, shape, dt=F32: st.enter_context(tile(name, shape, dt))
            gb = tb("gb", [P, U, 2 * D])
            ic = tb("ic", [P, 2, 4], I32)
            dc = tb("dc", [P, U])
            oh = tb("oh", [P, 2, 4, P])
            ot = tb("ot", [P, 2, 4, P])
            pr = tb("pr", [P, 2, 4, D])
            with phase("vs0 vs1 icr ohr tr otr kdr prr own") as (block, S):
                got, vst = gathered, S[0:2]
                icr, ohr, tr, otr, kdr, prr, own = S[2:]

                @block.gpsimd
                def _(po):
                    def body(it, first):
                        for h in range(2):
                            if not first:
                                po.wait_ge(prr, (it - 1) * 2 + h + 1)
                                po.wait_ge(vst[h], it * 16)
                            po.tensor_copy(ic[:, h, :], srci[:, bass.ds(it * U + 4 * h, 4)]).then_inc(icr, 1)
                            po.wait_ge(icr, it * 2 + h + 1)
                            po.nop(nofuse=True)
                            for j in range(4):
                                po.indirect_dma_start(out=gb[:, 4 * h + j, :], out_offset=None, in_=QV[:, :],
                                                      in_offset=bass.IndirectOffsetOnAxis(ap=ic[:, h, j:j + 1], axis=0)).then_inc(got[4 * h + j], 16)
                    steps(po, IT, body)

                @block.sync
                def _(sp):
                    def body(it, first):
                        for h in range(2):
                            for j in range(4):
                                sp.wait_ge(got[4 * h + j], landed(it))
                            sp.dma_start(VE[bass.ds(it * U + 4 * h, 4), :, :].rearrange("k p f -> p k f"),
                                         gb[:, 4 * h:4 * h + 4, D:2 * D]).then_inc(vst[h], 16)
                    steps(sp, IT, body)
                    for h in range(2):
                        sp.wait_ge(vst[h], 16 * IT)

                @block.vector
                def _(v):
                    def body(it, first):
                        if not first:
                            v.wait_ge(ohr, it * 2)
                        v.tensor_copy(dc[:, :], drel[:, bass.ds(it * U, U)]).then_inc(own, 1)
                        v.wait_ge(own, it + 1)
                        for h in range(2):
                            hh = it * 2 + h
                            if not first:
                                v.wait_ge(tr, hh - 1)
                            for j in range(4):
                                last = v.tensor_scalar(oh[:, h, j, :], iota[:, :], dc[:, 4 * h + j:4 * h + j + 1], None, ALU.is_equal)
                            last.then_inc(ohr, 1)
                        for h in range(2):
                            hh = it * 2 + h
                            for j in range(4):
                                v.wait_ge(got[4 * h + j], landed(it))
                            v.wait_ge(kdr, hh + 1)
                            v.tensor_tensor(pr[:, h, :, :], gb[:, 4 * h:4 * h + 4, 0:D],
                                            banks[2 + h][:, :].rearrange("p (j f) -> p j f", j=4), ALU.mult).then_inc(prr, 1)
                            v.wait_ge(prr, hh + 1)
                            v.tensor_reduce(A[:, :, bass.ds(hh * 4, 4)].rearrange("p h j -> p j h"),
                                            pr[:, h, :, :].rearrange("p j (h f) -> p j h f", h=H), AX.X, ALU.add)
                    steps(v, IT, body)

                @block.tensor
                def _(pe):
                    regs = [st.enter_context(pe.register(unique(f"pblk{j}"))) for j in range(U)]

                    def body(it, first):
                        pe.load(regs, gidx[0:1, bass.ds(it * U, U)])
                        for h in range(2):
                            hh = it * 2 + h
                            pe.wait_ge(ohr, hh + 1)
                            if not first:
                                pe.wait_ge(otr, hh - 1)
                            for j in range(4):
                                last = pe.transpose(banks[h][:, j * P:(j + 1) * P], oh[:, h, j, :], ident[:, :])
                            last.then_inc(tr, 1)
                        for h in range(2):
                            hh = it * 2 + h
                            pe.wait_ge(otr, hh + 1)
                            if not first:
                                pe.wait_ge(prr, hh - 1)
                            for j in range(4):
                                g = pe.snap(regs[4 * h + j], min_val=0, max_val=G - 1)
                                last = pe.matmul(banks[2 + h][:, j * D:(j + 1) * D], ot[:, h, j, :], TAB[:, bass.ds(g * MW, D)], start=True, stop=True)
                            last.then_inc(kdr, 1)
                    steps(pe, IT, body)

                @block.scalar
                def _(ac):
                    def body(it, first):
                        for h in range(2):
                            hh = it * 2 + h
                            ac.wait_ge(tr, hh + 1)
                            if not first:
                                ac.wait_ge(kdr, hh - 1)
                            ac.activation(ot[:, h, :, :].rearrange("p j n -> p (j n)"), banks[h][:, :], ACT.Copy).then_inc(otr, 1)
                    steps(ac, IT, body)

        passes[0] += 1

        LL = K * P // 32
        KC, FW = AGG[:, 0:LL], AGG[:, LL:2 * LL]
        BW, SC = SCR[:, 0:LL], TAB[:, 0:LL]
        with scratch() as st:
            tb = lambda name, shape, dt=F32: st.enter_context(tile(name, shape, dt))
            stage = TAB[:, 0:5 * KP].rearrange("p (t j e) -> p t j e", t=KT7, j=5)
            keyi = SCR[:, 0:KP]
            val = SCR[:, KP:2 * KP]
            pad = tb("pad", [1, P])
            cols = tb("cols", [P, 2])
            rows = tb("rows", [1, 4, P])
            cin = tb("cin", [P, 1])
            with phase("dv ready tr ev st") as (block, (dv, ready, tr, ev, sto)):
                @block.vector
                def _(v):
                    n = [0]

                    def link(ins):
                        n[0] += 1
                        ins.then_inc(dv, 1)
                        v.wait_ge(dv, n[0])

                    v.memset(pad[:, :], -2.0)
                    link(v.tensor_scalar(val, drel[:, :], 0.0, None, ALU.is_ge))
                    link(v.scalar_tensor_tensor(val, drel[:, :], float(P - 1), val, ALU.is_le, ALU.mult))
                    link(v.scalar_tensor_tensor(keyi, dkey[:, :], 1.0, val, ALU.add, ALU.mult))
                    link(v.tensor_scalar(keyi, keyi, -1.0, None, ALU.add))
                    v.sem_inc(ready, 1)
                    for t in range(KT7):
                        v.wait_ge(tr, t + 1)
                        v.tensor_copy(stage[:, t, 0:4, :], banks[2 * (t % 2)][:, :].rearrange("p (j e) -> p j e", j=4))
                        v.tensor_copy(stage[:, t, 4, :], banks[2 * (t % 2) + 1][:, 0:P]).then_inc(ev, 1)

                @block.tensor
                def _(pe):
                    pe.wait_ge(ready, 1)
                    for t in range(KT7):
                        if t >= 2:
                            pe.wait_ge(ev, t - 1)
                        for h in range(H):
                            pe.transpose(banks[2 * (t % 2)][:, h * P:(h + 1) * P], A[:, h, t * P:(t + 1) * P], ident[:, :])
                        pe.transpose(banks[2 * (t % 2) + 1][:, 0:P], keyi[:, t * P:(t + 1) * P], ident[:, :]).then_inc(tr, 1)

                @block.sync
                def _(sp):
                    sp.wait_ge(ready, 1)
                    sp.dma_start(KEY[0:P].rearrange("(a n) -> a n", a=1), pad[:, :]).then_inc(sto, 16)
                    for t in range(KT7):
                        sp.wait_ge(ev, t + 1)
                        sp.dma_start(SEQ[:, t * P * P:(t + 1) * P * P].rearrange("h (k e) -> k h e", e=P), stage[:, t, 0:4, :]).then_inc(sto, 16)
                        sp.dma_start(KEY[P + t * P * P:P + (t + 1) * P * P].rearrange("(k e) -> k e", e=P), stage[:, t, 4, :]).then_inc(sto, 16)
                    sp.wait_ge(sto, 16 * (2 * KT7 + 1))

            with phase("ld dv pe back ex sto") as (block, (ld, dv, pes, back, exd, sto)):
                @block.sync
                def _(sp):
                    for h in range(H):
                        part = slice(32 * h, 32 * h + 32)
                        sp.dma_start(SC[part, :], SEQ[h, 0:K * P].rearrange("(l j) -> l j", j=LL)).then_inc(ld, 16)
                        for dst, off in ((KC, 0), (FW, -1), (BW, 1)):
                            sp.dma_start(dst[part, :], KEY[P + off:P + off + K * P].rearrange("(l j) -> l j", j=LL)).then_inc(ld, 16)
                    sp.wait_ge(exd, 1)
                    sp.dma_start(SEX.rearrange("h (l j) -> (h l) j", j=LL), KC).then_inc(sto, 16)
                    sp.wait_ge(sto, 16)

                @block.vector
                def _(v):
                    n = [0]

                    def link(ins):
                        n[0] += 1
                        ins.then_inc(dv, 1)
                        v.wait_ge(dv, n[0])

                    def carries(i, last, flags, back_to_front):
                        v.tensor_copy(cols[:, 0:1], last)
                        link(v.tensor_reduce(cols[:, 1:2], flags, AX.X, ALU.add))
                        v.sem_inc(back, 1)
                        v.wait_ge(pes, 2 * i + 1)
                        v.memset(rows[:, 3, :], -BIG)
                        link(v.tensor_copy(rows[:, 0:2, :], banks[0][0:1, 0:2 * P].rearrange("p (j n) -> p j n", j=2)))
                        if back_to_front:
                            link(v.tensor_tensor_scan(rows[:, 2, ::-1], rows[:, 1, ::-1], rows[:, 0, ::-1], -BIG, ALU.add, ALU.max))
                            link(v.tensor_copy(rows[:, 3, 0:P - 1], rows[:, 2, 1:P]))
                        else:
                            link(v.tensor_tensor_scan(rows[:, 2, :], rows[:, 1, :], rows[:, 0, :], -BIG, ALU.add, ALU.max))
                            link(v.tensor_copy(rows[:, 3, 1:P], rows[:, 2, 0:P - 1]))
                        v.sem_inc(back, 1)
                        v.wait_ge(pes, 2 * i + 2)
                        link(v.tensor_copy(cin[:, :], banks[1][:, 0:1]))

                    v.wait_ge(ld, 16 * 16)
                    link(v.tensor_tensor(FW, FW, KC, ALU.not_equal))
                    link(v.tensor_tensor(BW, BW, KC, ALU.not_equal))
                    link(v.tensor_scalar(FW, FW, -BIG, None, ALU.mult))
                    link(v.tensor_scalar(BW, BW, -BIG, None, ALU.mult))
                    link(v.tensor_tensor_scan(KC, FW, SC, -BIG, ALU.add, ALU.max))
                    carries(0, KC[:, LL - 1:LL], FW, False)
                    link(v.tensor_tensor_scan(KC, FW, SC, cin[:, :], ALU.add, ALU.max))
                    link(v.tensor_tensor_scan(FW[:, ::-1], BW[:, ::-1], KC[:, ::-1], -BIG, ALU.add, ALU.max))
                    carries(1, FW[:, 0:1], BW, True)
                    link(v.tensor_tensor_scan(FW[:, ::-1], BW[:, ::-1], KC[:, ::-1], cin[:, :], ALU.add, ALU.max))
                    link(v.tensor_tensor(SC, SC, FW, ALU.subtract))
                    v.sem_inc(back, 1)

                @block.tensor
                def _(pe):
                    for i in range(2):
                        pe.wait_ge(back, 2 * i + 1)
                        pe.matmul(banks[0][0:1, 0:P], cols[:, 0:1], ident[:, :], start=True, stop=True)
                        pe.matmul(banks[0][0:1, P:2 * P], cols[:, 1:2], ident[:, :], start=True, stop=True).then_inc(pes, 1)
                        pe.wait_ge(back, 2 * i + 2)
                        pe.matmul(banks[1][:, 0:1], rows[0:1, 3, :], ones[0:1, 0:1], start=True, stop=True).then_inc(pes, 1)

                @block.scalar
                def _(ac):
                    ac.wait_ge(back, 5)
                    ac.activation(KC, SC, ACT.Exp, scale=float(DH) ** -0.5).then_inc(exd, 1)

            xs = TAB[:, 0:4 * KP].rearrange("p (t h e) -> p t h e", t=KT7, h=H)
            with phase("ld tr ev") as (block, (ld, tr, ev)):
                tiles = [(t, min(P, K - t * P)) for t in range(KT7)]

                @block.sync
                def _(sp):
                    for t, m in tiles:
                        sp.dma_start(xs[0:m, t, :, :], SEX[:, t * P * P:(t * P + m) * P].rearrange("h (k e) -> k h e", e=P)).then_inc(ld, 16)

                @block.tensor
                def _(pe):
                    pe.wait_ge(ld, 16 * KT7)
                    for t, m in tiles:
                        if t >= 2:
                            pe.wait_ge(ev, t - 1)
                        for h in range(H):
                            last = pe.transpose(banks[t % 2][:, h * P:h * P + m], xs[0:m, t, h, :], ident[0:m, 0:m])
                        last.then_inc(tr, 1)

                @block.vector
                def _(v):
                    for t, m in tiles:
                        v.wait_ge(tr, t + 1)
                        v.tensor_copy(A[:, :, t * P:t * P + m],
                                      banks[t % 2][:, :].rearrange("p (h k) -> p h k", h=H)[:, :, 0:m]).then_inc(ev, 1)

        AGGg = AGG[:, :].rearrange("p (g f) -> p g f", f=136)

        def edge_sum(width, table=None):
            with scratch() as st:
                tb = lambda name, shape, dt=F32: st.enter_context(tile(name, shape, dt))
                gw = 64 if table is not None else D
                gb = tb("gb", [P, U, gw])
                ic = tb("ic", [P, 2, 4], I32)
                dc = tb("dc", [P, U])
                ec = tb("ec", [P, U, H])
                ms = tb("ms", [P, 2, 4, 136])
                oh = tb("oh", [P, 2, 4, P])
                with phase("l0 l1 icr rdy mm own") as (block, S):
                    got = gathered if table is not None else S[0:2]
                    icr, rdy, mm, own = S[2:]

                    if table is not None:
                        @block.gpsimd
                        def _(po):
                            def body(it, first):
                                for h in range(2):
                                    if not first:
                                        po.wait_ge(mm, (it - 1) * U + 4 * h + 4)
                                    po.tensor_copy(ic[:, h, :], srci[:, bass.ds(it * U + 4 * h, 4)]).then_inc(icr, 1)
                                    po.wait_ge(icr, it * 2 + h + 1)
                                    po.nop(nofuse=True)
                                    for j in range(4):
                                        po.indirect_dma_start(out=gb[:, 4 * h + j, :], out_offset=None, in_=table[:, :],
                                                              in_offset=bass.IndirectOffsetOnAxis(ap=ic[:, h, j:j + 1], axis=0)).then_inc(got[4 * h + j], 16)
                            steps(po, IT, body)
                    else:
                        @block.sync
                        def _(sp):
                            def body(it, first):
                                for h in range(2):
                                    if not first:
                                        sp.wait_ge(rdy, (it - 1) * 2 + h + 1)
                                    sp.dma_start(gb[:, 4 * h:4 * h + 4, :],
                                                 VE[bass.ds(it * U + 4 * h, 4), :, :].rearrange("k p f -> p k f")).then_inc(got[h], 16)
                            steps(sp, IT, body)

                    @block.vector
                    def _(v):
                        regs = [st.enter_context(v.register(unique(f"eblk{j}"))) for j in range(U)]
                        v.memset(ms[:, :, :, 132:133], 1.0)
                        v.memset(AGG[:, :], 0.0).then_inc(own, 1)
                        per = U + 1

                        def body(it, first):
                            v.load(regs, gidx[0:1, bass.ds(it * U, U)])
                            v.wait_ge(own, it * per + 1)
                            if table is None:
                                v.tensor_copy(ec[:, :, :], A[:, :, bass.ds(it * U, U)].rearrange("p h j -> p j h"))
                            v.tensor_copy(dc[:, :], drel[:, bass.ds(it * U, U)]).then_inc(own, 1)
                            v.wait_ge(own, it * per + 2)
                            for h in range(2):
                                hh = it * 2 + h
                                if not first:
                                    v.wait_ge(mm, (hh - 2) * 4 + 4)
                                if table is None:
                                    v.wait_ge(got[h], it * 16 + 16)
                                    e4 = ec[:, 4 * h:4 * h + 4, :]
                                    v.tensor_tensor(ms[:, h, :, 0:D].rearrange("p j (h f) -> p j h f", h=H),
                                                    gb[:, 4 * h:4 * h + 4, :].rearrange("p j (h f) -> p j h f", h=H),
                                                    e4.unsqueeze(3).broadcast_to([P, 4, H, DH]), ALU.mult)
                                    v.tensor_copy(ms[:, h, :, D:D + H], e4)
                                for j in range(4):
                                    last = v.tensor_scalar(oh[:, h, j, :], iota[:, :], dc[:, 4 * h + j:4 * h + j + 1], None, ALU.is_equal)
                                last.then_inc(rdy, 1)
                            for h in range(2):
                                for j in range(4):
                                    k = (it * 2 + h) * 4 + j
                                    g = v.snap(regs[4 * h + j], min_val=0, max_val=G - 1)
                                    v.wait_ge(mm, k + 1)
                                    if h or j:
                                        v.wait_ge(own, it * per + 2 + 4 * h + j)
                                    acc = AGG[:, bass.ds(g * 136, width)]
                                    v.tensor_tensor(acc, acc, banks[4 * h + j][:, 0:width], ALU.add).then_inc(own, 1)
                        steps(v, IT, body)

                    @block.tensor
                    def _(pe):
                        def body(it, first):
                            for h in range(2):
                                pe.wait_ge(rdy, it * 2 + h + 1)
                                for j in range(4):
                                    k = (it * 2 + h) * 4 + j
                                    if not first:
                                        pe.wait_ge(own, (it - 1) * (U + 1) + 3 + 4 * h + j)
                                    if table is not None:
                                        pe.wait_ge(got[4 * h + j], landed(it))
                                        rhs = gb[:, 4 * h + j, :]
                                    else:
                                        rhs = ms[:, h, j, 0:width]
                                    pe.matmul(banks[4 * h + j][:, 0:width], oh[:, h, j, :], rhs, start=True, stop=True).then_inc(mm, 1)
                        steps(pe, IT, body)

            if table is not None:
                passes[0] += 1

        edge_sum(D + H + 1)

        w = scratch()
        row = lambda n, width: tbw(n, [P, width])
        wgb, gab, beb, bgb, alb = row("wgb", 3 * D), row("gab", D), row("beb", D), row("bgb", 1), row("alb", 1)
        rden = tbw("rden", [P, GB, H])
        with phase("ld dv sg sgr sq lx") as (block, (ld, dv, sg, sgr, sq, lx)):
            @block.sync
            def _(sp):
                for dst, n in ((wgb, "wg"), (gab, "gamma"), (beb, "beta"), (bgb, "bg"), (alb, "alpha")):
                    sp.dma_start(dst[:, :], a[n].broadcast_to([P, dst.shape[1]])).then_inc(ld, 16)

            @block.vector
            def _(v):
                n = [0]

                def link(ins):
                    n[0] += 1
                    ins.then_inc(dv, 1)
                    v.wait_ge(dv, n[0])

                spread = lambda col: col.unsqueeze(2).broadcast_to([P, GB, D])
                along = lambda r: r.unsqueeze(1).broadcast_to([P, GB, D])
                agg = AGGg[:, :, 0:D]
                v.wait_ge(ld, 16 * 5)
                den = AGGg[:, :, D:D + H]
                v.tensor_copy(cnt[:, :], AGG[:, D + H::136])
                link(v.scalar_tensor_tensor(rden[:, :, :], den, 0.0, den, ALU.is_le, ALU.add))
                link(v.reciprocal(rden[:, :, :], rden[:, :, :]))
                a4 = agg.rearrange("p g (h f) -> p g h f", h=H)
                for h in range(H):
                    link(v.tensor_tensor(agg[:, :, h * DH:(h + 1) * DH], agg[:, :, h * DH:(h + 1) * DH],
                                         rden[:, :, h:h + 1].broadcast_to([P, GB, DH]), ALU.mult))
                link(v.tensor_tensor(wgb[:, 0:D], wgb[:, 0:D], wgb[:, 2 * D:3 * D], ALU.add))
                link(v.tensor_tensor(wgb[:, D:2 * D], wgb[:, D:2 * D], wgb[:, 2 * D:3 * D], ALU.subtract))
                z0, z1, gate = (stats[:, j, :] for j in range(3))
                link(v.tensor_tensor(SCRg, Zg, along(wgb[:, 0:D]), ALU.mult))
                link(v.tensor_reduce(z0, SCRg, AX.X, ALU.add))
                link(v.tensor_tensor(SCRg, agg, along(wgb[:, D:2 * D]), ALU.mult))
                link(v.tensor_reduce(z1, SCRg, AX.X, ALU.add))
                link(v.scalar_tensor_tensor(z0, z0, bgb[:, 0:1], z1, ALU.add, ALU.add))
                link(v.tensor_scalar(z0, z0, -80.0, None, ALU.max))
                v.sem_inc(sg, 1)
                v.tensor_tensor(SCRg, Zg, agg, ALU.subtract)
                v.wait_ge(sgr, 1)
                link(v.tensor_scalar(gate, gate, 1.0, None, ALU.add))
                link(v.reciprocal(gate, gate))
                link(v.tensor_tensor(SCRg, SCRg, spread(gate), ALU.mult))
                link(v.tensor_tensor(SCRg, SCRg, agg, ALU.add))
                mean, ssq, tmp, y = (stats[:, j, :] for j in range(4))
                link(v.tensor_reduce(mean, SCRg, AX.X, ALU.add))
                link(v.tensor_scalar(mean, mean, 1.0 / D, None, ALU.mult))
                link(v.tensor_tensor(SCRg, SCRg, spread(mean), ALU.subtract))
                v.sem_inc(sg, 1)
                v.wait_ge(sq, 1)
                link(v.tensor_reduce(ssq, Zg, AX.X, ALU.add))
                link(v.tensor_scalar(ssq, ssq, 1.0 / D, EPS_LN, ALU.mult, ALU.add))
                v.sem_inc(sg, 1)
                v.wait_ge(lx, 2)
                rsqrt_chain(link, v, None, y, ssq, tmp)
                rsqrt_chain(link, v, None, y, ssq, tmp)
                link(v.tensor_tensor(SCRg, SCRg, spread(y), ALU.mult))
                link(v.tensor_tensor(SCRg, SCRg, along(gab[:, :]), ALU.mult))
                link(v.tensor_tensor(SCRg, SCRg, along(beb[:, :]), ALU.add))
                link(v.tensor_scalar(Z[:, :], SCR[:, :], 0.0, alb[:, 0:1], ALU.min, ALU.mult))
                link(v.scalar_tensor_tensor(SCR[:, :], SCR[:, :], 0.0, Z[:, :], ALU.max, ALU.add))
                link(v.tensor_tensor(X[:, :], X[:, :], SCR[:, :], ALU.add))

            @block.scalar
            def _(ac):
                ac.wait_ge(sg, 1)
                ac.activation(stats[:, 2, :], stats[:, 0, :], ACT.Exp, scale=-1.0).then_inc(sgr, 1)
                ac.wait_ge(sg, 2)
                ac.activation(Z[:, :], SCR[:, :], ACT.Square).then_inc(sq, 1)
                ac.wait_ge(sg, 3)
                ac.activation(stats[:, 2, :], stats[:, 1, :], ACT.Ln).then_inc(lx, 1)
                ac.wait_ge(lx, 1)
                ac.activation(stats[:, 3, :], stats[:, 2, :], ACT.Exp, scale=-0.5).then_inc(lx, 1)
        w.close()

        def show_x():
            with phase("o") as (block, (o,)):
                @block.sync
                def _(sp):
                    sp.dma_start(out.rearrange("(g p) f -> p g f", p=P), Xg).then_inc(o, 16)
                    sp.wait_ge(o, 16)

        if stop == "l1":
            show_x()
            return

        normalise(Xg, TAB[:, 0:GB * D])
        w = scratch()
        weights["wlr1"], weights["b21w"], weights["wlr2"], weights["b22"] = (
            tbw("wlr1", [D, D]), tbw("b21w", [1, D]), tbw("wlr2", [D, D]), tbw("b22", [1, D]))
        rdeg = tbw("rdeg", [P, GB])
        with phase("ld z") as (block, (ld, z)):
            @block.vector
            def _(v):
                v.memset(weights["b21w"][:, 0:64], 0.0).then_inc(z, 1)

            @block.sync
            def _(sp):
                sp.dma_start(weights["b21w"][:, 64:128], a["b21"]).then_inc(ld, 16)
                for n in ("wlr1", "wlr2", "b22"):
                    sp.dma_start(weights[n][:, :], a[n]).then_inc(ld, 16)
                sp.wait_ge(ld, 64)

        def take_yz(e, g, ps, t):
            e.activation(Z[:, bass.ds(g * D, 64)], ps[:, 64:128], ACT.Copy)
            return e.activation(t, ps[:, 0:64], ACT.Copy)

        node_products(relu_norm_block, weights["wlr1"], weights["b21w"], take_yz, "scalar", Y1, 64)
        edge_sum(64, Y1)
        with phase("dv r st") as (block, (dv, r, sto)):
            @block.vector
            def _(v):
                n = [0]

                def link(ins):
                    n[0] += 1
                    ins.then_inc(dv, 1)
                    v.wait_ge(dv, n[0])

                zz = Zg[:, :, 64:128]
                link(v.tensor_scalar(rdeg[:, :], cnt[:, :], 1.0, None, ALU.max))
                link(v.reciprocal(rdeg[:, :], rdeg[:, :]))
                link(v.tensor_tensor(zz, AGGg[:, :, 0:64], rdeg[:, :].unsqueeze(2).broadcast_to([P, GB, 64]), ALU.mult))
                link(v.tensor_tensor(zz, zz, Zg[:, :, 0:64], ALU.add))
                link(v.tensor_scalar(zz, zz, 0.0, None, ALU.max))
                v.sem_inc(r, 1)

            @block.sync
            def _(sp):
                sp.wait_ge(r, 1)
                sp.dma_start(H2.rearrange("(g p) f -> p g f", p=P), Zg[:, :, 64:128]).then_inc(sto, 16)
                sp.wait_ge(sto, 16)
        edge_sum(64, H2)
        with phase("dv") as (block, (dv,)):
            @block.vector
            def _(v):
                v.tensor_tensor(Zg[:, :, 0:64], AGGg[:, :, 0:64], rdeg[:, :].unsqueeze(2).broadcast_to([P, GB, 64]), ALU.mult)

        def add_x(e, g, ps, t):
            xb = X[:, bass.ds(g * D, D)]
            return e.tensor_tensor(xb, xb, ps[:, 0:D], ALU.add)

        node_products(lambda v, g, t: v.tensor_copy(t, Z[:, bass.ds(g * D, D)]), weights["wlr2"], weights["b22"], add_x, "vector")
        w.close()
        if stop == "l2":
            show_x()
            return

        normalise(Xg, TAB[:, 0:GB * D])
        TABg = TAB[:, :].rearrange("p (g f) -> p g f", f=MW)
        with phase("dv h sq st") as (block, (dv, hr, sq, sto)):
            @block.vector
            def _(v):
                v.memset(TABg[:, :, D:MW], 0.0).then_inc(dv, 1)
                v.scalar_tensor_tensor(TABg[:, :, 0:D], SCRg, 0.0, rstd.unsqueeze(2).broadcast_to([P, GB, D]), ALU.max, ALU.mult).then_inc(hr, 1)
                v.wait_ge(sq, 1)
                v.wait_ge(dv, 1)
                v.tensor_reduce(TABg[:, :, D], SCRg, AX.X, ALU.add).then_inc(hr, 1)

            @block.scalar
            def _(ac):
                ac.wait_ge(hr, 1)
                ac.activation(SCRg, TABg[:, :, 0:D], ACT.Square).then_inc(sq, 1)

            @block.sync
            def _(sp):
                sp.wait_ge(hr, 2)
                sp.dma_start(H3.rearrange("(g p) f -> p g f", p=P), TABg).then_inc(sto, 16)
                sp.wait_ge(sto, 16)

        with scratch() as st:
            tb = lambda name, shape, dt=F32: st.enter_context(tile(name, shape, dt))
            gb = tb("gb", [P, U, MW])
            ic = tb("ic", [P, 2, 4], I32)
            dc = tb("dc", [P, U])
            oh = tb("oh", [P, 2, 4, P])
            ot = tb("ot", [P, 2, 4, P])
            junk = tb("junk", [P, 2, 4, D])
            sc = tb("sc", [P, 2, 8, 4])
            tm = tb("tm", [P, 2, 4, D])
            mr = tb("mr", [P, 2, 4, MW])
            with phase("ms0 ms1 icr ohr tr otr hdr abr tmr mmr sqr rowr own") as (block, S):
                mst = S[0:2]
                icr, ohr, tr, otr, hdr, abr, tmr, mmr, sqr, rowr, own = S[2:]
                got = gathered

                @block.gpsimd
                def _(po):
                    def body(it, first):
                        for h in range(2):
                            if not first:
                                po.wait_ge(mmr, (it - 1) * U + 4 * h + 4)
                            po.tensor_copy(ic[:, h, :], srci[:, bass.ds(it * U + 4 * h, 4)]).then_inc(icr, 1)
                            po.wait_ge(icr, it * 2 + h + 1)
                            po.nop(nofuse=True)
                            for j in range(4):
                                po.indirect_dma_start(out=gb[:, 4 * h + j, :], out_offset=None, in_=H3[:, :],
                                                      in_offset=bass.IndirectOffsetOnAxis(ap=ic[:, h, j:j + 1], axis=0)).then_inc(got[4 * h + j], 16)
                    steps(po, IT, body)

                @block.vector
                def _(v):
                    LINKS = 7
                    per = 2 * LINKS + 1

                    def body(it, first):
                        if not first:
                            v.wait_ge(ohr, it * 2)
                        v.tensor_copy(dc[:, :], drel[:, bass.ds(it * U, U)]).then_inc(own, 1)
                        v.wait_ge(own, it * per + 1)
                        for h in range(2):
                            if not first:
                                v.wait_ge(tr, it * 2 + h - 1)
                            for j in range(4):
                                last = v.tensor_scalar(oh[:, h, j, :], iota[:, :], dc[:, 4 * h + j:4 * h + j + 1], None, ALU.is_equal)
                            last.then_inc(ohr, 1)
                        for h in range(2):
                            hh = it * 2 + h
                            n = [0]

                            def link(ins):
                                n[0] += 1
                                ins.then_inc(own, 1)
                                v.wait_ge(own, it * per + (1 + h * LINKS + n[0]))

                            sd, d2, p1, den, ca, cb, y2 = (sc[:, h, q, :] for q in range(7))
                            s2 = gb[:, 4 * h:4 * h + 4, D]
                            if not first:
                                v.wait_ge(tmr, hh * 4 - 4)
                            for j in range(4):
                                v.wait_ge(got[4 * h + j], landed(it))
                                v.wait_ge(hdr, hh * 2 + j // 2 + 1)
                                hd = banks[2 + 2 * h + j // 2][:, (j % 2) * 129:(j % 2) * 129 + 129]
                                v.tensor_copy(d2[:, j:j + 1], hd[:, D:D + 1])
                                last = v.tensor_tensor_reduce(junk[:, h, j, :], gb[:, 4 * h + j, 0:D], hd[:, 0:D], 1.0, 0.0, ALU.mult, ALU.add,
                                                              sd[:, j:j + 1])
                            link(last)
                            link(v.tensor_scalar(p1, sd, -2.0, 1.0, ALU.mult, ALU.add))
                            v.tensor_tensor(ca, p1, d2, ALU.add)
                            v.tensor_scalar(cb, s2, -1.0, 1.0, ALU.mult, ALU.add)
                            link(v.tensor_tensor(den, s2, d2, ALU.mult))
                            link(v.tensor_tensor(den, den, p1, ALU.add))
                            link(v.tensor_scalar(den, den, EPS_M, None, ALU.max))
                            link(v.reciprocal(den, den))
                            v.tensor_tensor(cb, cb, den, ALU.mult).then_inc(abr, 1)
                            link(v.tensor_tensor(ca, ca, den, ALU.mult))
                            assert n[0] == LINKS
                            if not first:
                                v.wait_ge(mst[h], it * 16)
                            for j in range(4):
                                v.wait_ge(tmr, hh * 4 + j + 1)
                                v.scalar_tensor_tensor(mr[:, h, j, 0:D], gb[:, 4 * h + j, 0:D], ca[:, j:j + 1], tm[:, h, j, :],
                                                       ALU.mult, ALU.subtract).then_inc(mmr, 1)
                        for h in range(2):
                            hh = it * 2 + h
                            y2 = sc[:, h, 6, :]
                            v.wait_ge(sqr, hh * 4 + 4)
                            for q, f in enumerate((-0.5, 0.5, 1.0, -1.0)):
                                last = v.tensor_scalar(mr[:, h, :, D + q], y2, f, None, ALU.mult)
                            last.then_inc(rowr, 1)
                    steps(v, IT, body)

                @block.tensor
                def _(pe):
                    regs = [st.enter_context(pe.register(unique(f"pblk{j}"))) for j in range(U)]

                    def body(it, first):
                        pe.load(regs, gidx[0:1, bass.ds(it * U, U)])
                        for h in range(2):
                            hh = it * 2 + h
                            pe.wait_ge(ohr, hh + 1)
                            if not first:
                                pe.wait_ge(otr, hh - 1)
                            for j in range(4):
                                last = pe.transpose(banks[h][:, j * P:(j + 1) * P], oh[:, h, j, :], ident[:, :])
                            last.then_inc(tr, 1)
                        for h in range(2):
                            hh = it * 2 + h
                            pe.wait_ge(otr, hh + 1)
                            if not first:
                                pe.wait_ge(tmr, hh * 4 - 4)
                            for j in range(4):
                                g = pe.snap(regs[4 * h + j], min_val=0, max_val=G - 1)
                                o = (j % 2) * 129
                                last = pe.matmul(banks[2 + 2 * h + j // 2][:, o:o + 129], ot[:, h, j, :], TAB[:, bass.ds(g * MW, 129)],
                                                 start=True, stop=True)
                                if j % 2:
                                    last.then_inc(hdr, 1)
                    steps(pe, IT, body)

                @block.scalar
                def _(ac):
                    def body(it, first):
                        for h in range(2):
                            hh = it * 2 + h
                            ac.wait_ge(tr, hh + 1)
                            if not first:
                                ac.wait_ge(hdr, hh * 2 - 2)
                            ac.activation(ot[:, h, :, :].rearrange("p j n -> p (j n)"), banks[h][:, :], ACT.Copy).then_inc(otr, 1)
                        for h in range(2):
                            hh = it * 2 + h
                            ac.wait_ge(abr, hh + 1)
                            if not first:
                                ac.wait_ge(mmr, hh * 4 - 4)
                            for j in range(4):
                                hd = banks[2 + 2 * h + j // 2][:, (j % 2) * 129:(j % 2) * 129 + D]
                                ac.activation(tm[:, h, j, :], hd, ACT.Copy, scale=sc[:, h, 5, j:j + 1]).then_inc(tmr, 1)
                            for j in range(4):
                                ac.wait_ge(mmr, hh * 4 + j + 1)
                                if j == 0 and not first:
                                    ac.wait_ge(rowr, hh - 1)
                                ac.activation(tm[:, h, j, :], mr[:, h, j, 0:D], ACT.Square, accum_out=sc[:, h, 6, j:j + 1]).then_inc(sqr, 1)
                    steps(ac, IT, body)

                @block.sync
                def _(sp):
                    rows = MSG.rearrange("(k p) c -> k p c", p=P)

                    def body(it, first):
                        for h in range(2):
                            sp.wait_ge(rowr, it * 2 + h + 1)
                            sp.dma_start(rows[bass.ds(it * U + 4 * h, 4), :, :].rearrange("k p c -> p k c"), mr[:, h, :, :]).then_inc(mst[h], 16)
                    steps(sp, IT, body)
                    for h in range(2):
                        sp.wait_ge(mst[h], 16 * IT)
        passes[0] += 1

        w = scratch()
        WR = 2
        wfirst, woff, weff = tbw("wfirst", [P, GB]), tbw("woff", [P, GB]), tbw("weff", [P, GB])
        tcount = tbw("tcount", [1, GB + 2])
        tcounti = w.enter_context(tile("tcounti", [1, GB + 2], I32))
        with scratch() as st:
            tb = lambda name, shape, dt=F32: st.enter_context(tile(name, shape, dt))
            before = tb("before", [P, P])
            gpos = tb("gpos", [P, GB])
            tot, pos, nw, fr = tb("tot", [P, GB]), tb("pos", [P, GB]), tb("nw", [P, GB]), tb("fr", [P, GB])
            ii = tb("ii", [P, GB], I32)
            mx = tb("mx", [GB, 1])
            with phase("pr pe1 dv nwr pe2 mxr pe3") as (block, (pr, pe1, dv, nwr, pe2, mxr, pe3)):
                @block.gpsimd
                def _(po):
                    po.memset(before[:, :], 1.0).then_inc(pr, 1)
                    po.iota(gpos[:, :], [[P, GB]], base=0, channel_multiplier=0, allow_small_or_imprecise_dtypes=True)
                    po.wait_ge(pr, 1)
                    po.affine_select(out=before[:, :], in_=before[:, :], compare_op=ALU.is_gt, fill=0.0, base=0,
                                     pattern=[[1, P]], channel_multiplier=-1).then_inc(pr, 1)

                @block.tensor
                def _(pe):
                    pe.wait_ge(pr, 2)
                    pe.matmul(banks[0][:, 0:GB], before[:, :], cnt[:, :], start=True, stop=True)
                    pe.matmul(banks[0][:, GB:2 * GB], ones[:, :], cnt[:, :], start=True, stop=True).then_inc(pe1, 1)
                    pe.wait_ge(nwr, 1)
                    pe.transpose(banks[1][0:GB, 0:P], nw[:, :], ident[:, :]).then_inc(pe2, 1)
                    pe.wait_ge(mxr, 1)
                    pe.matmul(banks[2][0:1, 0:GB], mx[:, :], ident[0:GB, 0:GB], start=True, stop=True).then_inc(pe3, 1)

                @block.vector
                def _(v):
                    n = [0]

                    def link(ins):
                        n[0] += 1
                        ins.then_inc(dv, 1)
                        v.wait_ge(dv, n[0])

                    v.wait_ge(pr, 2)
                    v.wait_ge(pe1, 1)
                    link(v.tensor_copy(tot[:, :], banks[0][:, GB:2 * GB]))
                    link(v.memset(fr[:, :], 0.0))
                    link(v.tensor_tensor_scan(nw[:, :], tot[:, :], fr[:, :], 0.0, ALU.add, ALU.add))
                    link(v.tensor_tensor(pos[:, :], nw[:, :], tot[:, :], ALU.subtract))
                    link(v.tensor_tensor(pos[:, :], pos[:, :], banks[0][:, 0:GB], ALU.add))
                    link(v.tensor_tensor(pos[:, :], pos[:, :], gpos[:, :], ALU.add))
                    link(v.tensor_copy(ii[:, :], pos[:, :]))
                    link(v.tensor_scalar(ii[:, :], ii[:, :], 1, None, ALU.arith_shift_right))
                    link(v.tensor_copy(wfirst[:, :], ii[:, :]))
                    link(v.scalar_tensor_tensor(woff[:, :], wfirst[:, :], -float(WR), pos[:, :], ALU.mult, ALU.add))
                    link(v.tensor_tensor(weff[:, :], woff[:, :], cnt[:, :], ALU.add))
                    link(v.tensor_scalar(nw[:, :], weff[:, :], float(2 * WR - 1), None, ALU.add))
                    link(v.tensor_copy(ii[:, :], nw[:, :]))
                    link(v.tensor_scalar(ii[:, :], ii[:, :], 2, None, ALU.arith_shift_right))
                    link(v.tensor_copy(nw[:, :], ii[:, :]))
                    link(v.scalar_tensor_tensor(nw[:, :], cnt[:, :], 0.0, nw[:, :], ALU.is_gt, ALU.mult))
                    v.sem_inc(nwr, 1)
                    v.wait_ge(pe2, 1)
                    link(v.tensor_reduce(mx[:, :], banks[1][0:GB, 0:P], AX.X, ALU.max))
                    v.sem_inc(mxr, 1)
                    v.wait_ge(pe3, 1)
                    link(v.tensor_scalar(tcount[:, 0:GB], banks[2][0:1, 0:GB], 1.0, None, ALU.max))
                    link(v.tensor_reduce(tcount[:, GB:GB + 1], tcount[:, 1:GB], AX.X, ALU.add))
                    link(v.tensor_tensor(tcount[:, GB + 1:GB + 2], tcount[:, 0:1], tcount[:, GB:GB + 1], ALU.subtract))
                    link(v.tensor_scalar(tcount[:, GB + 1:GB + 2], tcount[:, GB + 1:GB + 2], 1.0, None, ALU.max))
                    v.tensor_copy(tcounti[:, :], tcount[:, :])

        LAST = K * P // WR - 1
        MAXT = E // (2 * WR) + 2 * GB
        with scratch() as st:
            tb = lambda name, shape, dt=F32: st.enter_context(tile(name, shape, dt))
            S2 = tb("S2", [P, 2, MW])
            mw = tb("mw", [P, 2, 2, WR, MW])
            mk = tb("mk", [P, 2, 2, WR, MW])
            wrow = tb("wrow", [P, 2, 2 * WR])
            wlen = tb("wlen", [P, 2])
            widx = tb("widx", [P, 2])
            wi = tb("wi", [P, 2, 2], I32)
            m0 = tb("m0", [P, 2, 2 * WR])
            msk = tb("msk", [P, 2, 2 * WR])
            woff1 = tb("woff1", [P, 1])
            jrow = tb("jrow", [P, 2 * WR])
            jk = tb("jk", [P, 2, 130])
            wv = tb("wv", [P, 2, D])
            den, rdn, be, t2 = tb("den", [P, 2]), tb("rdn", [P, 2]), tb("be", [P, 2]), tb("t2", [P, 2])
            wgat = [[st.enter_context(nc.semaphore(unique(f"wgat{b}{s}"))) for s in range(2)] for b in range(2)]
            windows = MSG.rearrange("(w r) c -> w (r c)", r=WR)

            def turns(eng, begin_block, turn):
                done = st.enter_context(eng.register(unique("done")))
                left = st.enter_context(eng.register(unique("left")))
                eng.reg_mov(done, 0)

                def one(g):
                    turn(g, eng.snap(done, min_val=0, max_val=MAXT))
                    eng.reg_add(done, done, 1)

                with eng.Fori(1, GB) as g:
                    begin_block(g, eng.snap(done, min_val=0, max_val=MAXT))
                    eng.load(left, tcounti[0:1, bass.ds(g, 1)])
                    with eng.Fori(0, eng.snap(left, min_val=1, max_val=MAXT)) as _:
                        one(g)
                eng.load(left, tcounti[0:1, GB + 1:GB + 2])
                with eng.Fori(0, eng.snap(left, min_val=1, max_val=MAXT)) as _:
                    one(GB - 1)

            with phase("pown masked used own") as (block, (pown, masked, used, own)):
                @block.gpsimd
                def _(po):
                    PT, PB, P0 = 8, 4, 4
                    po.iota(jrow[:, :], [[1, 2 * WR]], base=0, channel_multiplier=0, allow_small_or_imprecise_dtypes=True).then_inc(pown, 1)
                    po.wait_ge(pown, 1)
                    po.tensor_copy(widx[:, 0:1], wfirst[:, 0:1]).then_inc(pown, 1)
                    po.tensor_copy(wlen[:, 0:1], cnt[:, 0:1]).then_inc(pown, 1)
                    po.tensor_scalar(wrow[:, 0, :], jrow[:, :], woff[:, 0:1], None, ALU.subtract).then_inc(pown, 1)

                    def begin_block(g, t):
                        po.wait_ge(pown, t * PT + (g * PB + (P0 - PB)))
                        po.tensor_copy(widx[:, 1:2], wfirst[:, bass.ds(g, 1)]).then_inc(pown, 1)
                        po.tensor_copy(wlen[:, 1:2], cnt[:, bass.ds(g, 1)]).then_inc(pown, 1)
                        po.tensor_copy(woff1[:, :], woff[:, bass.ds(g, 1)]).then_inc(pown, 1)
                        po.wait_ge(pown, t * PT + (g * PB + (P0 - PB + 3)))
                        po.nop(nofuse=True)
                        po.tensor_scalar(wrow[:, 1, :], jrow[:, :], woff1[:, :], None, ALU.subtract).then_inc(pown, 1)

                    def turn(g, t):
                        n = [0]

                        def link(ins):
                            n[0] += 1
                            ins.then_inc(pown, 1)
                            po.wait_ge(pown, t * PT + (g * PB + (P0 + n[0])))
                            po.nop(nofuse=True)

                        po.wait_ge(pown, t * PT + (g * PB + P0))
                        po.wait_ge(masked, t * 2 + 2)
                        po.nop(nofuse=True)
                        link(po.tensor_scalar(wi[:, 0, :], widx[:, :], float(LAST), None, ALU.min))
                        link(po.tensor_scalar(wi[:, 1, :], widx[:, :], 1.0, float(LAST), ALU.add, ALU.min))
                        link(po.tensor_scalar(widx[:, :], widx[:, :], 2.0, None, ALU.add))
                        link(po.tensor_tensor(m0[:, :, :], wlen[:, :].unsqueeze(2).broadcast_to([P, 2, 2 * WR]), wrow[:, :, :], ALU.subtract))
                        link(po.tensor_scalar(m0[:, :, :], m0[:, :, :], 0.0, None, ALU.is_gt))
                        link(po.tensor_scalar(msk[:, :, :], wrow[:, :, :], 0.0, None, ALU.is_ge))
                        link(po.tensor_tensor(msk[:, :, :], msk[:, :, :], m0[:, :, :], ALU.mult))
                        link(po.tensor_scalar(wrow[:, :, :], wrow[:, :, :], 2.0 * WR, None, ALU.add))
                        assert n[0] == PT
                        po.nop(nofuse=True)
                        for b in range(2):
                            for s in range(2):
                                po.indirect_dma_start(out=mw[:, b, s, :, :].rearrange("p r c -> p (r c)"), out_offset=None, in_=windows[:, :],
                                                      in_offset=bass.IndirectOffsetOnAxis(ap=wi[:, b, s:s + 1], axis=0)).then_inc(wgat[b][s], 16)
                    turns(po, begin_block, turn)

                @block.scalar
                def _(ac):
                    ac.sem_inc(masked, 2)

                    def turn(g, t):
                        for b in range(2):
                            ac.wait_ge(used, t * 2 + (b + 1))
                            for s in range(2):
                                ac.wait_ge(wgat[b][s], t * 16 + 16)
                                for r in range(WR):
                                    last = ac.activation(mk[:, b, s, r, :], mw[:, b, s, r, :], ACT.Copy, scale=msk[:, s, WR * b + r:WR * b + r + 1])
                            last.then_inc(masked, 1)
                    turns(ac, lambda g, t: None, turn)

                @block.vector
                def _(v):
                    OPS = 11
                    DT, DB, D0 = 2 * WR * OPS, 3, 2
                    v.sem_inc(used, 2)
                    v.memset(S2[:, :, 0:D], 0.0).then_inc(own, 1)
                    v.memset(S2[:, :, D:D + 2], 1.0).then_inc(own, 1)

                    def begin_block(g, t):
                        v.wait_ge(own, t * DT + (g * DB + (D0 - DB)))
                        v.tensor_copy(AGG[:, bass.ds(g * 136 - 136, D)], S2[:, 1, 0:D]).then_inc(own, 1)
                        v.wait_ge(own, t * DT + (g * DB + (D0 - DB + 1)))
                        v.memset(S2[:, 1, 0:D], 0.0).then_inc(own, 1)
                        v.memset(S2[:, 1, D:D + 2], 1.0).then_inc(own, 1)

                    def turn(g, t):
                        n = [0]

                        def ops_done(m):
                            v.wait_ge(own, t * DT + (g * DB + (D0 + m)))

                        def do(ins):
                            n[0] += 1
                            ins.then_inc(own, 1)
                            return n[0]

                        sum_done = [0, 0]
                        d_done = 0
                        for b in range(2):
                            v.wait_ge(masked, t * 2 + (b + 3))
                            for r in range(WR):
                                M = mk[:, b, :, r, :]
                                ops_done(max(d_done, sum_done[0]))
                                do(v.tensor_tensor_reduce(jk[:, 0, :], S2[:, 0, 0:130], M[:, 0, 0:130], 2.0, 1.0, ALU.mult, ALU.add, den[:, 0:1]))
                                ops_done(sum_done[1])
                                dd = do(v.tensor_tensor_reduce(jk[:, 1, :], S2[:, 1, 0:130], M[:, 1, 0:130], 2.0, 1.0, ALU.mult, ALU.add, den[:, 1:2]))
                                for s in range(2):
                                    do(v.scalar_tensor_tensor(wv[:, s, :], S2[:, s, 0:D], M[:, s, D + 2:D + 3], M[:, s, 0:D], ALU.mult, ALU.add))
                                ops_done(dd)
                                ops_done(do(v.tensor_scalar(den[:, :], den[:, :], EPS_M, None, ALU.max)))
                                ops_done(do(v.reciprocal(rdn[:, :], den[:, :])))
                                ops_done(do(v.tensor_tensor(be[:, :], S2[:, :, D], rdn[:, :], ALU.mult)))
                                tt = do(v.tensor_tensor(t2[:, :], be[:, :], M[:, :, D + 3], ALU.mult))
                                sum_done[0] = do(v.scalar_tensor_tensor(S2[:, 0, 0:D], wv[:, 0, :], be[:, 0:1], S2[:, 0, 0:D], ALU.mult, ALU.add))
                                ops_done(tt)
                                d_done = do(v.tensor_tensor(S2[:, :, D], be[:, :], t2[:, :], ALU.add))
                                last = v.scalar_tensor_tensor(S2[:, 1, 0:D], wv[:, 1, :], be[:, 1:2], S2[:, 1, 0:D], ALU.mult, ALU.add)
                                sum_done[1] = do(last)
                            ops_done(sum_done[1])
                            v.sem_inc(used, 1)
                        assert n[0] == DT
                    turns(v, begin_block, turn)
                    v.tensor_copy(AGG[:, (GB - 1) * 136:(GB - 1) * 136 + D], S2[:, 1, 0:D])
                    v.tensor_copy(AGG[:, 0:D], S2[:, 0, 0:D])

        with scratch() as st:
            tb = lambda name, shape, dt=F32: st.enter_context(tile(name, shape, dt))
            small = tb("small", [P, 10, GB])
            with phase("dv go acd st") as (block, (dv, go, acd, sto)):
                n2, nn, nr, q0, q1, sc_, xy, q2, q3, f = (small[:, j, :] for j in range(10))
                sums = AGGg[:, :, 0:D]
                hs = TABg[:, :, 0:D]
                spread = lambda col: col.unsqueeze(2).broadcast_to([P, GB, D])

                @block.vector
                def _(v):
                    n = [0]

                    def link(ins):
                        n[0] += 1
                        ins.then_inc(dv, 1)
                        v.wait_ge(dv, n[0])

                    link(v.tensor_tensor(SCRg, sums, sums, ALU.mult))
                    link(v.tensor_reduce(n2, SCRg, AX.X, ALU.add))
                    link(v.tensor_scalar(q0, n2, 1e-30, None, ALU.max))
                    v.sem_inc(go, 1)
                    link(v.tensor_tensor(SCRg, sums, hs, ALU.mult))
                    link(v.tensor_reduce(xy, SCRg, AX.X, ALU.add))
                    link(v.tensor_scalar(sc_, cnt[:, :], 1.0, None, ALU.max))
                    link(v.reciprocal(sc_, sc_))
                    v.wait_ge(acd, 1)
                    link(v.reciprocal(nr, nn))
                    link(v.tensor_tensor(nr, nr, q0, ALU.mult))
                    link(v.tensor_tensor(nn, nn, nr, ALU.add))
                    link(v.tensor_scalar(nn, nn, 0.5, None, ALU.mult))
                    link(v.tensor_scalar(nr, nn, EPS_M, float(np.float32(1.0) - np.float32(EPS_M)), ALU.max, ALU.min))
                    link(v.tensor_scalar(q0, nr, -1.0, 1.0, ALU.mult, ALU.add))
                    link(v.reciprocal(q0, q0))
                    link(v.tensor_scalar(q1, nr, 1.0, None, ALU.add))
                    link(v.tensor_tensor(q0, q0, q1, ALU.mult))
                    v.sem_inc(go, 1)
                    link(v.tensor_tensor(q2, nr, nr, ALU.mult))
                    link(v.tensor_scalar(q3, q2, 1.0 / 9, 1.0 / 7, ALU.mult, ALU.add))
                    for c in (1.0 / 5, 1.0 / 3, 1.0):
                        link(v.tensor_tensor(q3, q3, q2, ALU.mult))
                        link(v.tensor_scalar(q3, q3, c, None, ALU.add))
                    link(v.tensor_tensor(q3, q3, nr, ALU.mult))
                    link(v.tensor_scalar(q2, nr, 0.15, None, ALU.is_lt))
                    v.wait_ge(acd, 2)
                    link(v.tensor_scalar(f, f, 0.5, None, ALU.mult))
                    link(v.tensor_tensor(q3, q3, f, ALU.subtract))
                    link(v.tensor_tensor(q3, q3, q2, ALU.mult))
                    link(v.tensor_tensor(f, f, q3, ALU.add))
                    link(v.tensor_tensor(f, f, sc_, ALU.mult))
                    v.sem_inc(go, 1)
                    v.wait_ge(acd, 3)
                    link(v.reciprocal(q0, nr))
                    link(v.tensor_tensor(f, f, q0, ALU.mult))
                    link(v.scalar_tensor_tensor(f, nn, EPS_M, f, ALU.is_gt, ALU.mult))
                    x2 = TABg[:, :, D]
                    link(v.tensor_tensor(xy, xy, f, ALU.mult))
                    link(v.tensor_tensor(n2, n2, f, ALU.mult))
                    link(v.tensor_tensor(n2, n2, f, ALU.mult))
                    link(v.tensor_scalar(q0, xy, 2.0, 1.0, ALU.mult, ALU.add))
                    link(v.tensor_tensor(q1, x2, n2, ALU.mult))
                    link(v.tensor_tensor(q1, q1, q0, ALU.add))
                    link(v.tensor_scalar(q1, q1, EPS_M, None, ALU.max))
                    link(v.reciprocal(q1, q1))
                    link(v.tensor_tensor(q0, q0, n2, ALU.add))
                    link(v.tensor_tensor(q0, q0, q1, ALU.mult))
                    link(v.tensor_scalar(q2, x2, -1.0, 1.0, ALU.mult, ALU.add))
                    link(v.tensor_tensor(q2, q2, f, ALU.mult))
                    link(v.tensor_tensor(q2, q2, q1, ALU.mult))
                    link(v.tensor_tensor(SCRg, hs, spread(q0), ALU.mult))
                    link(v.tensor_tensor(X[:, :], X[:, :], SCR[:, :], ALU.add))
                    link(v.tensor_tensor(SCRg, sums, spread(q2), ALU.mult))
                    link(v.tensor_tensor(X[:, :], X[:, :], SCR[:, :], ALU.add))
                    v.sem_inc(go, 1)

                @block.scalar
                def _(ac):
                    ac.wait_ge(go, 1)
                    ac.activation(nn, q0, ACT.Sqrt).then_inc(acd, 1)
                    ac.wait_ge(go, 2)
                    ac.activation(f, q0, ACT.Ln).then_inc(acd, 1)
                    ac.wait_ge(go, 3)
                    ac.activation(f, f, ACT.Tanh).then_inc(acd, 1)

                @block.sync
                def _(sp):
                    sp.wait_ge(go, 4)
                    sp.dma_start(out.rearrange("(g p) f -> p g f", p=P), Xg).then_inc(sto, 16)
                    sp.wait_ge(sto, 16)
        w.close()


def layout(inputs):
    i = {k: np.asarray(v) for k, v in inputs.items()}
    pad = (C + 1) * P - E
    one = lambda n: np.ascontiguousarray(i[n].reshape(1, -1))
    col = lambda n: np.ascontiguousarray(i[n].reshape(-1, 1))
    dst2d = np.concatenate([i["dst"], np.full(pad, FARAWAY, np.int32)]).reshape(C + 1, P)
    return {
        "x": np.concatenate([i["x"], np.zeros((NP - N, D), np.float32)]),
        "src2d": np.concatenate([i["src"], np.zeros(pad, np.int32)]).reshape(C + 1, P),
        "dst2d": dst2d,
        "dst_last": np.ascontiguousarray(dst2d[:C, P - 1]),
        "ew2d": np.concatenate([i["edge_weight"], np.zeros(pad, np.float32)]).reshape(C + 1, P),
        "attrT": np.ascontiguousarray(np.concatenate([i["edge_attr_50"], np.zeros((pad, NG), np.float32)]).T),
        "w1": i["L0_gnn_mlp_w1"], "b1": col("L0_gnn_mlp_b1"), "w2": i["L0_gnn_mlp_w2"], "b2": one("L0_gnn_mlp_b2"),
        "lin1": i["L0_gnn_lin1_w"], "lin2": i["L0_gnn_lin2_w"], "lin2b": col("L0_gnn_lin2_b"),
        "lin": i["L0_gnn_lin_w"], "linb": one("L0_gnn_lin_b"),
        "wqvks": np.concatenate([i["L1_gnn_Wq"], i["L1_gnn_Wv"], i["L1_gnn_Wk"], i["L1_gnn_Ws"]], 1),
        "bqvks": np.concatenate([i["L1_gnn_bq"], i["L1_gnn_bv"], i["L1_gnn_bk"], i["L1_gnn_bs"]]).reshape(1, -1),
        "wg": i["L1_gnn_Wg"].reshape(1, 3 * D), "bg": i["L1_gnn_bg"].reshape(1, 1),
        "gamma": one("L1_gnn_gamma"), "beta": one("L1_gnn_beta"), "alpha": i["L1_gnn_alpha"].reshape(1, 1),
        "wlr1": np.concatenate([i["L2_gnn_W_l1"].T, i["L2_gnn_W_r1"].T], 1),
        "b21": one("L2_gnn_b1"),
        "wlr2": np.concatenate([i["L2_gnn_W_l2"].T, i["L2_gnn_W_r2"].T], 0),
        "b22": one("L2_gnn_b2"),
    }


STOP = None


def kernel(**inputs):
    import concourse.bacc as _bacc
    from concourse.bass_utils import run_bass_kernel_spmd as _run

    nc = _bacc.Bacc("TRN2", target_bir_lowering=False, num_devices=1)
    arrays = {f"in_{k}": np.ascontiguousarray(v) for k, v in layout(inputs).items()}
    aps = {n[3:]: nc.dram_tensor(n, v.shape, mybir.dt.from_np(v.dtype), kind="ExternalInput").ap() for n, v in arrays.items()}
    out = nc.dram_tensor("out", (NP, D), F32, kind="ExternalOutput").ap()
    build(nc, aps, out, STOP)
    r = _run(nc, [arrays], core_ids=[0])
    return r.results[0]["out"][:N]
```

```python
import numpy as np
import concourse.bass as bass
from concourse import mybir
from contextlib import ExitStack, contextmanager

F32 = mybir.dt.float32
BF16 = mybir.dt.bfloat16
I32 = mybir.dt.int32
ALU = mybir.AluOpType
ACT = mybir.ActivationFunctionType
AX = mybir.AxisListType

P = 128
N = 6250
E = 100000
D = 128
H = 4
DH = D // H
NG = 50
G = -(-N // P)
GB = G + G % 2
NP = GB * P
C = -(-E // P)
U = 8
K = -(-(C + G - 1) // U) * U
IT = K // U
KT7 = -(-K // P)
KP = KT7 * P
MW = 132
FARAWAY = 1 << 20
EPS_LN = 1e-5
EPS_M = 1e-7
BIG = 1e30
LOG2 = float(np.log(2.0))


def build(nc, a, out, stop=None):
    dram = lambda name, shape, dt=F32: nc.dram_tensor(name, shape, dt, kind="Internal").ap()
    T0 = dram("T0", (NP, D))
    QV = dram("QV", (NP, 2 * D))
    VE = dram("VE", (K, P, D))
    SEQ = dram("SEQ", (H, KP * P))
    KEY = dram("KEY", (P + KP * P,))
    SEX = dram("SEX", (H, K * P))
    Y1 = dram("Y1", (NP, 64))
    H2 = dram("H2", (NP, 64))
    H3 = dram("H3", (NP, MW))
    MSG = dram("MSG", (K * P, MW))

    name_uses = {}

    def unique(name):
        name_uses[name] = name_uses.get(name, 0) + 1
        return name if name_uses[name] == 1 else f"{name}_{name_uses[name]}"

    def tile(name, shape, dt=F32):
        return nc.sbuf_tensor(unique(name), shape, dt)

    with ExitStack() as ctx:
        def sb(name, shape, dt=F32):
            return ctx.enter_context(tile(name, shape, dt))

        X = sb("X", [P, GB * D])
        AGG = sb("AGG", [P, GB * 136])
        TAB = sb("TAB", [P, GB * MW])
        Z = sb("Z", [P, GB * D])
        SCR = sb("SCR", [P, GB * D])
        srci = sb("srci", [P, KP], I32)
        drel = sb("drel", [P, KP])
        dkey = sb("dkey", [P, KP])
        cut = sb("cut", [P, KP])
        A = sb("A", [P, H, KP])
        gidx = sb("gidx", [1, KP], I32)
        cidx = sb("cidx", [1, KP], I32)
        ident = sb("ident", [P, P])
        iota = sb("iota", [P, P])
        ones = sb("ones", [P, P])
        cnt = sb("cnt", [P, GB])
        banks = [ctx.enter_context(nc.psum_tensor(f"bank{i}", [P, 512], F32)) for i in range(8)]

        gat = ctx.enter_context(nc.semaphore("gat"))
        gathered = [ctx.enter_context(nc.semaphore(f"gathered{j}")) for j in range(U)]
        passes = [0]

        def landed(it):
            return it * 16 + (16 + passes[0] * 16 * IT)

        @contextmanager
        def phase(names):
            with ExitStack() as st:
                sems = [st.enter_context(nc.semaphore(unique(n))) for n in names.split()]
                with nc.Block() as block:
                    yield block, sems
                nc.gpsimd.sem_clear(range(min(s.num for s in sems), max(s.num for s in sems) + 1))
                nc.all_engine_barrier()

        def scratch():
            return ExitStack()

        with scratch() as st:
            tb = lambda name, shape, dt=F32: st.enter_context(tile(name, shape, dt))
            lasti = tb("lasti", [P, C], I32)
            L = tb("L", [P, C])
            Lj = tb("Lj", [P, C])
            kcol = tb("kcol", [P, KT7])
            ccol = tb("ccol", [P, KT7])
            gcol = tb("gcol", [P, KT7])
            ccoli = tb("ccoli", [P, KT7], I32)
            rs = tb("rs", [P, KT7, P], I32)
            rd = tb("rd", [P, KT7, P], I32)
            re = tb("re", [P, KT7, P])
            rf = tb("rf", [P, 2, KT7, P])
            wide = tb("wide", [P, 2, P])
            half_pi = tb("half_pi", [P, 1])
            with phase("ld pool rowc tr evac dv sn") as (block, (ld, pool, rowc, tr, evac, dv, sn)):
                @block.sync
                def _(sp):
                    sp.dma_start(lasti[:, :], a["dst_last"].rearrange("(a n) -> a n", a=1).broadcast_to([P, C])).then_inc(ld, 16)
                    sp.dma_start(X[:, :].rearrange("p (g f) -> p g f", f=D), a["x"].rearrange("(g p) f -> p g f", p=P)).then_inc(ld, 16)

                @block.gpsimd
                def _(po):
                    po.memset(ident[:, :], 0.0).then_inc(pool, 1)
                    po.memset(ones[:, :], 1.0)
                    po.memset(half_pi[:, :], float(np.pi / 2))
                    po.memset(A[:, :, K:KP], 0.0)
                    po.iota(iota[:, :], [[1, P]], base=0, channel_multiplier=0, allow_small_or_imprecise_dtypes=True)
                    po.iota(L[:, :], [[1, C]], base=0, channel_multiplier=0, allow_small_or_imprecise_dtypes=True)
                    po.iota(kcol[:, :], [[P, KT7]], base=0, channel_multiplier=1, allow_small_or_imprecise_dtypes=True)
                    po.wait_ge(pool, 1)
                    po.affine_select(out=ident[:, :], in_=ident[:, :], compare_op=ALU.not_equal, fill=1.0, base=0,
                                     pattern=[[-1, P]], channel_multiplier=1).then_inc(pool, 1)
                    po.wait_ge(rowc, 1)
                    for t in range(KT7):
                        for dst, tab in ((rs, a["src2d"]), (rd, a["dst2d"]), (re, a["ew2d"])):
                            po.indirect_dma_start(out=dst[:, t, :], out_offset=None, in_=tab[:, :],
                                                  in_offset=bass.IndirectOffsetOnAxis(ap=ccoli[:, t:t + 1], axis=0)).then_inc(gat, 16)

                @block.vector
                def _(v):
                    n = [0]

                    def link(ins):
                        n[0] += 1
                        ins.then_inc(dv, 1)
                        v.wait_ge(dv, n[0])

                    v.wait_ge(ld, 32)
                    v.wait_ge(pool, 2)
                    link(v.tensor_scalar(lasti[:, :], lasti[:, :], 7, None, ALU.arith_shift_right))
                    link(v.tensor_scalar(Lj[:, :], lasti[:, :], float(G - 1), None, ALU.min))
                    link(v.tensor_tensor(L[:, :], L[:, :], Lj[:, :], ALU.add))
                    for t in range(KT7):
                        link(v.tensor_scalar(Lj[:, :], L[:, :], kcol[:, t:t + 1], 0.0, ALU.is_lt, ALU.add,
                                             accum_out=ccol[:, t:t + 1]))
                    link(v.tensor_tensor(gcol[:, :], kcol[:, :], ccol[:, :], ALU.subtract))
                    link(v.tensor_scalar(gcol[:, :], gcol[:, :], float(G - 1), None, ALU.min))
                    v.tensor_copy(ccoli[:, :], ccol[:, :]).then_inc(rowc, 1)
                    v.wait_ge(gat, 16 * 3 * KT7)
                    v.tensor_copy(rf[:, 0, :, :], rs[:, :, :])
                    link(v.tensor_copy(rf[:, 1, :, :], rd[:, :, :]))
                    for t in range(KT7):
                        cols = slice(t * P, (t + 1) * P)
                        if t:
                            v.wait_ge(tr, t)
                        v.tensor_copy(wide[:, 0, :], gcol[:, t:t + 1].broadcast_to([P, P]))
                        link(v.tensor_copy(wide[:, 1, :], ccol[:, t:t + 1].broadcast_to([P, P])))
                        v.sem_inc(rowc, 1)
                        v.wait_ge(tr, t + 1)
                        bk = banks[0]
                        v.tensor_copy(srci[:, cols], bk[:, 0:P])
                        v.tensor_copy(cut[:, cols], bk[:, 2 * P:3 * P])
                        link(v.tensor_copy(dkey[:, cols], bk[:, P:2 * P]))
                        v.scalar_tensor_tensor(drel[:, cols], banks[1][:, 0:P], -float(P), dkey[:, cols], ALU.mult, ALU.add)
                        v.tensor_copy(gidx[0:1, cols], banks[1][0:1, 0:P])
                        link(v.tensor_copy(cidx[0:1, cols], banks[1][0:1, P:2 * P]))
                        v.sem_inc(evac, 1)
                    w = cut[:, :]
                    s = SCR[:, 0:KP]
                    q = SCR[:, KP:2 * KP]
                    link(v.tensor_scalar(s, w, 10.0, None, ALU.is_le))
                    link(v.scalar_tensor_tensor(q, w, 0.0, s, ALU.is_ge, ALU.mult))
                    link(v.tensor_scalar(w, w, 0.0, 10.0, ALU.max, ALU.min))
                    v.sem_inc(evac, 1)
                    v.wait_ge(sn, 1)
                    link(v.tensor_scalar(w, w, 0.5, 0.5, ALU.mult, ALU.add))
                    link(v.tensor_tensor(w, w, q, ALU.mult))

                @block.tensor
                def _(pe):
                    pe.wait_ge(pool, 2)
                    for t in range(KT7):
                        pe.wait_ge(rowc, t + 2)
                        if t:
                            pe.wait_ge(evac, t)
                        pe.transpose(banks[0][:, 0:P], rf[:, 0, t, :], ident[:, :])
                        pe.transpose(banks[0][:, P:2 * P], rf[:, 1, t, :], ident[:, :])
                        pe.transpose(banks[0][:, 2 * P:3 * P], re[:, t, :], ident[:, :])
                        pe.matmul(banks[1][:, 0:P], wide[:, 0, :], ident[:, :], start=True, stop=True)
                        pe.matmul(banks[1][:, P:2 * P], wide[:, 1, :], ident[:, :], start=True, stop=True).then_inc(tr, 1)

                @block.scalar
                def _(ac):
                    ac.wait_ge(evac, KT7 + 1)
                    ac.activation(cut[:, :], cut[:, :], ACT.Sin, bias=half_pi[:, :], scale=-float(np.pi / 10)).then_inc(sn, 1)
        if stop == "items":
            with phase("o") as (block, (o,)):
                @block.sync
                def _(sp):
                    for i, t in enumerate((drel, dkey, cut)):
                        sp.dma_start(out[i * P:(i + 1) * P, :], t[:, 700:828]).then_inc(o, 16)
                    sp.wait_ge(o, 48)
            return

        weights = {}

        def load_weights(names):
            with phase("ld") as (block, (ld,)):
                @block.sync
                def _(sp):
                    for n in names:
                        sp.dma_start(weights[n][:, :], a[n]).then_inc(ld, 16)
                    sp.wait_ge(ld, 16 * len(names))

        def steps(eng, count, body):
            body(0, True)
            with eng.Fori(1, count) as it:
                body(it, False)

        def pipeline(eng, count, body):
            body(0, True, 2)
            with eng.Fori(1, count - 2) as it:
                body(it, False, 2)
            body(count - 2, False, 1)
            body(count - 1, False, 0)

        Xg = X[:, :].rearrange("p (g f) -> p g f", f=D)
        SCRg = SCR[:, :].rearrange("p (g f) -> p g f", f=D)
        Zg = Z[:, :].rearrange("p (g f) -> p g f", f=D)
        stats = sb("stats", [P, 4, GB])
        rstd = stats[:, 3, :]

        def rsqrt_chain(link, v, ac_done, y, var, t):
            link(v.tensor_tensor(t, y, y, ALU.mult))
            link(v.tensor_tensor(t, t, var, ALU.mult))
            link(v.tensor_scalar(t, t, -0.5, 1.5, ALU.mult, ALU.add))
            link(v.tensor_tensor(y, y, t, ALU.mult))

        def normalise(src, squares):
            with phase("cen sq lnexp dv") as (block, (cen, sq, lnexp, dv)):
                @block.vector
                def _(v):
                    n = [0]

                    def link(ins):
                        n[0] += 1
                        ins.then_inc(dv, 1)
                        v.wait_ge(dv, n[0])

                    mean, ssq, tmp, y = (stats[:, j, :] for j in range(4))
                    link(v.tensor_reduce(mean, src, AX.X, ALU.add))
                    link(v.tensor_scalar(mean, mean, 1.0 / D, None, ALU.mult))
                    v.tensor_tensor(SCRg, src, mean.unsqueeze(2).broadcast_to([P, GB, D]), ALU.subtract).then_inc(cen, 1)
                    v.wait_ge(sq, 1)
                    link(v.tensor_reduce(ssq, squares.rearrange("p (g f) -> p g f", f=D), AX.X, ALU.add))
                    v.tensor_scalar(ssq, ssq, 1.0 / D, EPS_LN, ALU.mult, ALU.add).then_inc(cen, 1)
                    v.wait_ge(lnexp, 2)
                    rsqrt_chain(link, v, None, y, ssq, tmp)
                    rsqrt_chain(link, v, None, y, ssq, tmp)

                @block.scalar
                def _(ac):
                    ac.preload_act_table_set("natural_log_exp_and_others")
                    ac.wait_ge(cen, 1)
                    ac.activation(squares, SCR[:, :], ACT.Square).then_inc(sq, 1)
                    ac.wait_ge(cen, 2)
                    ac.activation(stats[:, 2, :], stats[:, 1, :], ACT.Ln).then_inc(lnexp, 1)
                    ac.wait_ge(lnexp, 1)
                    ac.activation(stats[:, 3, :], stats[:, 2, :], ACT.Exp, scale=-0.5).then_inc(lnexp, 1)

        def relu_norm_block(v, g, out_tile):
            return v.tensor_scalar(out_tile, SCR[:, bass.ds(g * D, D)], 0.0, stats[:, 3, bass.ds(g, 1)], ALU.max, ALU.mult)

        ones3 = sb("ones3", [3, P], BF16)

        def split_row(row, parts3):
            n = row.shape[1]
            with scratch() as st:
                pt = st.enter_context(tile("pt", [1, 3, n], BF16))
                hi = st.enter_context(tile("hi", [1, n], F32))
                rest = st.enter_context(tile("rest", [1, n], F32))
                with phase("dv parts ld") as (block, (dv, parts, ld)):
                    @block.vector
                    def _(v):
                        m = [0]

                        def link(ins):
                            m[0] += 1
                            ins.then_inc(dv, 1)
                            v.wait_ge(dv, m[0])

                        link(v.tensor_copy(rest[:, :], row))
                        for k in range(3):
                            link(v.tensor_copy(pt[:, k, :], rest[:, :]))
                            link(v.tensor_copy(hi[:, :], pt[:, k, :]))
                            link(v.tensor_tensor(rest[:, :], rest[:, :], hi[:, :], ALU.subtract))
                        v.memset(ones3[:, :], 1.0)
                        v.sem_inc(parts, 1)

                    @block.sync
                    def _(sp):
                        sp.wait_ge(parts, 1)
                        for k in range(3):
                            sp.dma_start(parts3[k:k + 1, :], pt[:, k, :]).then_inc(ld, 16)
                        sp.wait_ge(ld, 48)

        def node_products(fill, W, bias, take, taker, store=None, store_cols=0):
            width = W.shape[1]
            with scratch() as st:
                hb = st.enter_context(tile("hb", [P, 2, P], F32))
                hT = st.enter_context(tile("hT", [P, 2, P], F32))
                ob = st.enter_context(tile("ob", [P, 2, max(store_cols, 1)], F32))
                with phase("filled transposed copied product taken stored0 stored1 self") as (
                        block, (filled, transposed, copied, product, taken, stored0, stored1, own)):
                    stored = (stored0, stored1)

                    def taking(eng, it, b, first, pending):
                        g = it * 2 + b
                        eng.wait_ge(product, g + 1)
                        if store is not None and not first:
                            eng.wait_ge(stored[b], it * 16)
                        take(eng, g, banks[2 + b], ob[:, b, :]).then_inc(taken, 1)

                    @block.vector
                    def _(v):
                        def body(it, first):
                            for b in range(2):
                                if not first:
                                    v.wait_ge(transposed, it * 2 + b - 1)
                                fill(v, it * 2 + b, hb[:, b, :]).then_inc(filled, 1)
                            if taker == "vector":
                                for b in range(2):
                                    taking(v, it, b, first, None)
                        steps(v, GB // 2, body)

                    @block.tensor
                    def _(pe):
                        def body(it, first):
                            for b in range(2):
                                pe.wait_ge(filled, it * 2 + b + 1)
                                if not first:
                                    pe.wait_ge(copied, it * 2 + b - 1)
                                pe.transpose(banks[b][:, 0:P], hb[:, b, :], ident[:, :]).then_inc(transposed, 1)
                            for b in range(2):
                                pe.wait_ge(copied, it * 2 + b + 1)
                                if not first:
                                    pe.wait_ge(taken, it * 2 + b - 1)
                                po = banks[2 + b][:, 0:width]
                                pe.matmul(po, ones[0:1, :], bias[0:1, :], start=True, stop=False)
                                pe.matmul(po, hT[:, b, :], W[:, :], start=False, stop=True).then_inc(product, 1)
                        steps(pe, GB // 2, body)

                    @block.scalar
                    def _(ac):
                        def body(it, first):
                            for b in range(2):
                                ac.wait_ge(transposed, it * 2 + b + 1)
                                if not first:
                                    ac.wait_ge(product, it * 2 + b - 1)
                                ac.activation(hT[:, b, :], banks[b][:, 0:P], ACT.Copy).then_inc(copied, 1)
                            if taker == "scalar":
                                for b in range(2):
                                    taking(ac, it, b, first, None)
                        steps(ac, GB // 2, body)

                    if store is not None:
                        @block.sync
                        def _(sp):
                            def body(it, first):
                                for b in range(2):
                                    sp.wait_ge(taken, it * 2 + b + 1)
                                    sp.dma_start(store[bass.ds((it * 2 + b) * P, P), :], ob[:, b, :]).then_inc(stored[b], 16)
                            steps(sp, GB // 2, body)
                            for b in range(2):
                                sp.wait_ge(stored[b], 16 * (GB // 2))

        w = scratch()
        tbw = lambda name, shape: w.enter_context(tile(f"w_{name}", shape, F32))
        for n, shape in (("lin1", [D, D]), ("w1", [NG, D]), ("b1", [D, 1]), ("w2", [D, D]), ("b2", [1, D]), ("b2w", [1, 512])):
            weights[n] = tbw(n, shape)
        zero_row = tbw("zero_row", [1, D])
        b1m = tbw("b1m", [D, 1])
        load_weights(["lin1", "w1", "b1", "w2", "b2"])
        normalise(Xg, TAB[:, 0:GB * D])
        with phase("a b") as (block, (sa, sbb)):
            @block.tensor
            def _(pe):
                pe.matmul(banks[0][0:1, 0:D], ones[:, 0:1], weights["w2"][:, :], start=True, stop=True).then_inc(sa, 1)

            @block.vector
            def _(v):
                v.memset(zero_row[:, :], 0.0)
                v.tensor_scalar(b1m[:, :], weights["b1"][:, :], -30.0, None, ALU.add)
                v.wait_ge(sa, 1)
                for j in range(4):
                    v.scalar_tensor_tensor(weights["b2w"][:, j * D:(j + 1) * D], banks[0][0:1, 0:D], -LOG2, weights["b2"][:, :], ALU.mult, ALU.add)

        b2parts = w.enter_context(tile("b2parts", [3, 512], BF16))
        split_row(weights["b2w"][:, :], b2parts)
        node_products(lambda v, g, t: relu_norm_block(v, g, t), weights["lin1"], zero_row,
                      lambda e, g, ps, t: e.activation(t, ps[:, 0:D], ACT.Copy), "scalar", T0, D)

        AGGT = AGG[:, 0:GB * P]
        with scratch() as st:
            tb = lambda name, shape, dt=F32: st.enter_context(tile(name, shape, dt))
            gb = tb("gb", [P, U, D])
            ab = tb("ab", [NG, U, P])
            ic = tb("ic", [P, 2, 4], I32)
            dc = tb("dc", [P, 2, U])
            xm = tb("xm", [P, 2, 512])
            rx = tb("rx", [P, 2, 512])
            ms = tb("ms", [P, 2, 4, D])
            oh = tb("oh", [P, 2, 4, P])
            with phase("at0 at1 at2 at3 at4 at5 at6 at7 icr mm1 xmr acr spr mm2 msr mm3 dcr accd") as (block, S):
                got, att = gathered, S[0:8]
                icr, mm1, xmr, acr, spr, mm2, msr, mm3, dcr, accd = S[8:]

                @block.gpsimd
                def _(po):
                    def body(it, first):
                        for h in range(2):
                            if not first:
                                po.wait_ge(msr, (it - 1) * U + 4 * h + 4)
                            po.tensor_copy(ic[:, h, :], srci[:, bass.ds(it * U + 4 * h, 4)]).then_inc(icr, 1)
                            po.wait_ge(icr, it * 2 + h + 1)
                            po.nop(nofuse=True)
                            for j in range(4):
                                po.indirect_dma_start(out=gb[:, 4 * h + j, :], out_offset=None, in_=T0[:, :],
                                                      in_offset=bass.IndirectOffsetOnAxis(ap=ic[:, h, j:j + 1], axis=0)).then_inc(got[4 * h + j], 16)
                    steps(po, IT, body)

                @block.sync
                def _(sp):
                    regs = [sp.register(unique(f"chunk{j}")) for j in range(U)]
                    regs = [st.enter_context(r) for r in regs]

                    def body(it, first):
                        sp.load(regs, cidx[0:1, bass.ds(it * U, U)])
                        for j in range(U):
                            if not first and j % 4 == 0:
                                sp.wait_ge(mm1, (it - 1) * 2 + j // 4 + 1)
                            c = sp.snap(regs[j], min_val=0, max_val=C)
                            sp.dma_start(ab[:, j, :], a["attrT"][:, bass.ds(c * P, P)]).then_inc(att[j], 16)
                    steps(sp, IT, body)

                @block.tensor
                def _(pe):
                    def filter1(it, h):
                        for j in range(4):
                            pe.wait_ge(att[4 * h + j], it * 16 + 16)
                        pe.matmul(banks[h][:, :], weights["w1"][:, :], ab[:, 4 * h:4 * h + 4, :].rearrange("p j e -> p (j e)"),
                                  start=True, stop=True).then_inc(mm1, 1)

                    def filter2(it, h):
                        pe.wait_ge(spr, it * 2 + h + 1)
                        pe.matmul(banks[2 + h][:, 0:512], ones3[:, :], b2parts[:, :], start=True, stop=False)
                        for j in range(4):
                            last = pe.matmul(banks[2 + h][:, j * P:(j + 1) * P], rx[:, h, j * P:(j + 1) * P], weights["w2"][:, :],
                                             start=False, stop=(j == 3))
                        last.then_inc(mm2, 1)

                    def body(it, first, ahead):
                        for h in range(2):
                            u = it * 2 + h
                            if h == 0 or ahead > 0:
                                filter2(it + h, 1 - h)
                            if ahead > h:
                                filter1(it + 1 + h, 1 - h)
                            for j in range(4):
                                if not first and j % 2 == 0:
                                    pe.wait_ge(accd, u * 4 + (2 * (j // 2) - 5))
                                pe.wait_ge(msr, u * 4 + j + 1)
                                pe.matmul(banks[4 + 2 * h + j // 2][:, (j % 2) * P:(j % 2 + 1) * P], ms[:, h, j, :], oh[:, h, j, :],
                                          start=True, stop=True).then_inc(mm3, 1)

                    filter1(0, 0)
                    filter1(0, 1)
                    filter2(0, 0)
                    filter1(1, 0)
                    pipeline(pe, IT, body)

                @block.scalar
                def _(ac):
                    def body(it, first):
                        for h in range(2):
                            hh = it * 2 + h
                            ac.wait_ge(xmr, hh + 1)
                            ac.activation(xm[:, h, :], xm[:, h, :], ACT.Exp).then_inc(acr, 1)
                            if not first:
                                ac.wait_ge(mm2, hh - 1)
                            ac.activation(rx[:, h, :], banks[h][:, 0:512], ACT.Relu, bias=b1m[:, :]).then_inc(acr, 1)
                            ac.wait_ge(acr, hh * 3 + 1)
                            ac.activation(xm[:, h, :], xm[:, h, :], ACT.Ln, bias=1.0).then_inc(acr, 1)
                    steps(ac, IT, body)

                @block.vector
                def _(v):
                    regs = [st.enter_context(v.register(unique(f"blk{j}"))) for j in range(4)]
                    v.memset(AGGT, 0.0).then_inc(accd, 1)

                    def clamp(it, h):
                        v.wait_ge(mm1, it * 2 + h + 1)
                        v.tensor_scalar(xm[:, h, :], banks[h][:, 0:512], weights["b1"][:, :], 30.0, ALU.add, ALU.min).then_inc(xmr, 1)

                    def softplus(it, h):
                        v.wait_ge(acr, (it * 2 + h) * 3 + 3)
                        v.tensor_tensor(rx[:, h, :], rx[:, h, :], xm[:, h, :], ALU.add).then_inc(spr, 1)

                    def add_sum(u, h, j):
                        g = v.snap(regs[j], min_val=0, max_val=G - 1)
                        if j % 2 == 0:
                            v.wait_ge(mm3, u * 4 + (j + 2))
                        v.wait_ge(accd, u * 4 + (j + 1))
                        acc = AGG[:, bass.ds(g * P, P)]
                        v.tensor_tensor(acc, acc, banks[4 + 2 * h + j // 2][:, (j % 2) * P:(j % 2 + 1) * P], ALU.add).then_inc(accd, 1)

                    def body(it, first, ahead):
                        if not first:
                            v.wait_ge(msr, it * U)
                        v.tensor_copy(dc[:, 0, :], drel[:, bass.ds(it * U, U)])
                        v.tensor_copy(dc[:, 1, :], cut[:, bass.ds(it * U, U)]).then_inc(dcr, 1)
                        for h in range(2):
                            u = it * 2 + h
                            adds = not (first and h == 0)
                            if adds:
                                v.load(regs, gidx[0:1, bass.ds(it * U + (4 * h - 4), 4)])
                            if ahead > 0:
                                clamp(it + 1, h)
                            if h == 0 or ahead > 0:
                                softplus(it + h, 1 - h)
                            if h == 0:
                                v.wait_ge(dcr, it + 1)
                            v.wait_ge(mm2, u + 1)
                            for j in range(4):
                                v.wait_ge(got[4 * h + j], landed(it))
                                v.scalar_tensor_tensor(ms[:, h, j, :], banks[2 + h][:, j * P:(j + 1) * P], dc[:, 1, 4 * h + j:4 * h + j + 1],
                                                       gb[:, 4 * h + j, :], ALU.mult, ALU.mult)
                                v.tensor_scalar(oh[:, h, j, :], iota[:, :], dc[:, 0, 4 * h + j:4 * h + j + 1], None, ALU.is_equal).then_inc(msr, 1)
                                if adds:
                                    add_sum(u - 1, 1 - h, j)
                    clamp(0, 0)
                    clamp(0, 1)
                    softplus(0, 0)
                    pipeline(v, IT, body)
                    v.load(regs, gidx[0:1, IT * U - 4:IT * U])
                    for j in range(4):
                        add_sum(IT * 2 - 1, 1, j)
        passes[0] += 1
        w.close()
        if stop == "l0":
            with phase("o") as (block, (o,)):
                @block.sync
                def _(sp):
                    for g in range(48):
                        sp.dma_start(out[g * P:(g + 1) * P, :], AGGT[:, g * P:(g + 1) * P]).then_inc(o, 16)
                    sp.wait_ge(o, 16 * 48)
            return

        w = scratch()
        for n, shape in (("lin2", [D, D]), ("lin2b", [D, 1]), ("lin", [D, D]), ("linb", [1, D])):
            weights[n] = tbw(n, shape)
        lin2bm = tbw("lin2bm", [D, 1])
        load_weights(["lin2", "lin2b", "lin", "linb"])
        with phase("a b") as (block, (sa, sbb)):
            @block.tensor
            def _(pe):
                pe.matmul(banks[0][0:1, 0:D], ones[:, 0:1], weights["lin"][:, :], start=True, stop=True).then_inc(sa, 1)

            @block.vector
            def _(v):
                v.tensor_scalar(lin2bm[:, :], weights["lin2b"][:, :], -30.0, None, ALU.add)
                v.wait_ge(sa, 1)
                v.scalar_tensor_tensor(weights["linb"][:, :], banks[0][0:1, 0:D], -LOG2, weights["linb"][:, :], ALU.mult, ALU.add)
        with scratch() as st:
            xm = st.enter_context(tile("xm", [P, 2, P], F32))
            rx = st.enter_context(tile("rx", [P, 2, P], F32))
            with phase("mm1 xmr acr spr mm2 added") as (block, (mm1, xmr, acr, spr, mm2, added)):
                @block.tensor
                def _(pe):
                    def body(it, first):
                        for b in range(2):
                            g = it * 2 + b
                            if not first:
                                pe.wait_ge(xmr, g - 1)
                                pe.wait_ge(acr, (g - 2) * 3 + 3)
                            pe.matmul(banks[b][:, 0:P], weights["lin2"][:, :], AGG[:, bass.ds(g * P, P)], start=True, stop=True).then_inc(mm1, 1)
                        for b in range(2):
                            g = it * 2 + b
                            pe.wait_ge(spr, g + 1)
                            if not first:
                                pe.wait_ge(added, g - 1)
                            pe.matmul(banks[2 + b][:, 0:D], ones[0:1, :], weights["linb"][0:1, :], start=True, stop=False)
                            pe.matmul(banks[2 + b][:, 0:D], rx[:, b, :], weights["lin"][:, :], start=False, stop=True).then_inc(mm2, 1)
                    steps(pe, GB // 2, body)

                @block.scalar
                def _(ac):
                    def body(it, first):
                        for b in range(2):
                            g = it * 2 + b
                            ac.wait_ge(xmr, g + 1)
                            ac.activation(xm[:, b, :], xm[:, b, :], ACT.Exp).then_inc(acr, 1)
                            if not first:
                                ac.wait_ge(mm2, g - 1)
                            ac.activation(rx[:, b, :], banks[b][:, 0:P], ACT.Relu, bias=lin2bm[:, :]).then_inc(acr, 1)
                            ac.wait_ge(acr, g * 3 + 1)
                            ac.activation(xm[:, b, :], xm[:, b, :], ACT.Ln, bias=1.0).then_inc(acr, 1)
                    steps(ac, GB // 2, body)

                @block.vector
                def _(v):
                    def body(it, first):
                        for b in range(2):
                            g = it * 2 + b
                            v.wait_ge(mm1, g + 1)
                            if not first:
                                v.wait_ge(spr, g - 1)
                            v.tensor_scalar(xm[:, b, :], banks[b][:, 0:P], weights["lin2b"][:, :], 30.0, ALU.add, ALU.min).then_inc(xmr, 1)
                        for b in range(2):
                            g = it * 2 + b
                            v.wait_ge(acr, g * 3 + 3)
                            v.tensor_tensor(rx[:, b, :], rx[:, b, :], xm[:, b, :], ALU.add).then_inc(spr, 1)
                        for b in range(2):
                            g = it * 2 + b
                            v.wait_ge(mm2, g + 1)
                            xb = X[:, bass.ds(g * D, D)]
                            v.tensor_tensor(xb, xb, banks[2 + b][:, 0:D], ALU.add).then_inc(added, 1)
                    steps(v, GB // 2, body)
        w.close()
        normalise(Xg, TAB[:, 0:GB * D])

        w = scratch()
        for n, shape in (("wqvks", [D, 4 * D]), ("bqvks", [1, 4 * D])):
            weights[n] = tbw(n, shape)
        load_weights(["wqvks", "bqvks"])

        def take_qvks(e, g, ps, t):
            e.activation(TAB[:, bass.ds(g * MW, D)], ps[:, 2 * D:3 * D], ACT.Copy)
            e.activation(Z[:, bass.ds(g * D, D)], ps[:, 3 * D:4 * D], ACT.Copy)
            return e.activation(t, ps[:, 0:2 * D], ACT.Copy)

        node_products(relu_norm_block, weights["wqvks"], weights["bqvks"], take_qvks, "scalar", QV, 2 * D)
        w.close()

        with scratch() as st:
            tb = lambda name, shape, dt=F32: st.enter_context(tile(name, shape, dt))
            gb = tb("gb", [P, U, 2 * D])
            ic = tb("ic", [P, 2, 4], I32)
            dc = tb("dc", [P, U])
            oh = tb("oh", [P, 2, 4, P])
            ot = tb("ot", [P, 2, 4, P])
            pr = tb("pr", [P, 2, 4, D])
            with phase("vs0 vs1 icr ohr tr otr kdr prr own") as (block, S):
                got, vst = gathered, S[0:2]
                icr, ohr, tr, otr, kdr, prr, own = S[2:]

                @block.gpsimd
                def _(po):
                    def body(it, first):
                        for h in range(2):
                            if not first:
                                po.wait_ge(prr, (it - 1) * 2 + h + 1)
                                po.wait_ge(vst[h], it * 16)
                            po.tensor_copy(ic[:, h, :], srci[:, bass.ds(it * U + 4 * h, 4)]).then_inc(icr, 1)
                            po.wait_ge(icr, it * 2 + h + 1)
                            po.nop(nofuse=True)
                            for j in range(4):
                                po.indirect_dma_start(out=gb[:, 4 * h + j, :], out_offset=None, in_=QV[:, :],
                                                      in_offset=bass.IndirectOffsetOnAxis(ap=ic[:, h, j:j + 1], axis=0)).then_inc(got[4 * h + j], 16)
                    steps(po, IT, body)

                @block.sync
                def _(sp):
                    def body(it, first):
                        for h in range(2):
                            for j in range(4):
                                sp.wait_ge(got[4 * h + j], landed(it))
                            sp.dma_start(VE[bass.ds(it * U + 4 * h, 4), :, :].rearrange("k p f -> p k f"),
                                         gb[:, 4 * h:4 * h + 4, D:2 * D]).then_inc(vst[h], 16)
                    steps(sp, IT, body)
                    for h in range(2):
                        sp.wait_ge(vst[h], 16 * IT)

                @block.vector
                def _(v):
                    def body(it, first):
                        if not first:
                            v.wait_ge(ohr, it * 2)
                        v.tensor_copy(dc[:, :], drel[:, bass.ds(it * U, U)]).then_inc(own, 1)
                        v.wait_ge(own, it + 1)
                        for h in range(2):
                            hh = it * 2 + h
                            if not first:
                                v.wait_ge(tr, hh - 1)
                            for j in range(4):
                                last = v.tensor_scalar(oh[:, h, j, :], iota[:, :], dc[:, 4 * h + j:4 * h + j + 1], None, ALU.is_equal)
                            last.then_inc(ohr, 1)
                        for h in range(2):
                            hh = it * 2 + h
                            for j in range(4):
                                v.wait_ge(got[4 * h + j], landed(it))
                            v.wait_ge(kdr, hh + 1)
                            v.tensor_tensor(pr[:, h, :, :], gb[:, 4 * h:4 * h + 4, 0:D],
                                            banks[2 + h][:, :].rearrange("p (j f) -> p j f", j=4), ALU.mult).then_inc(prr, 1)
                            v.wait_ge(prr, hh + 1)
                            v.tensor_reduce(A[:, :, bass.ds(hh * 4, 4)].rearrange("p h j -> p j h"),
                                            pr[:, h, :, :].rearrange("p j (h f) -> p j h f", h=H), AX.X, ALU.add)
                    steps(v, IT, body)

                @block.tensor
                def _(pe):
                    regs = [st.enter_context(pe.register(unique(f"pblk{j}"))) for j in range(U)]

                    def body(it, first):
                        pe.load(regs, gidx[0:1, bass.ds(it * U, U)])
                        for h in range(2):
                            hh = it * 2 + h
                            pe.wait_ge(ohr, hh + 1)
                            if not first:
                                pe.wait_ge(otr, hh - 1)
                            for j in range(4):
                                last = pe.transpose(banks[h][:, j * P:(j + 1) * P], oh[:, h, j, :], ident[:, :])
                            last.then_inc(tr, 1)
                        for h in range(2):
                            hh = it * 2 + h
                            pe.wait_ge(otr, hh + 1)
                            if not first:
                                pe.wait_ge(prr, hh - 1)
                            for j in range(4):
                                g = pe.snap(regs[4 * h + j], min_val=0, max_val=G - 1)
                                last = pe.matmul(banks[2 + h][:, j * D:(j + 1) * D], ot[:, h, j, :], TAB[:, bass.ds(g * MW, D)], start=True, stop=True)
                            last.then_inc(kdr, 1)
                    steps(pe, IT, body)

                @block.scalar
                def _(ac):
                    def body(it, first):
                        for h in range(2):
                            hh = it * 2 + h
                            ac.wait_ge(tr, hh + 1)
                            if not first:
                                ac.wait_ge(kdr, hh - 1)
                            ac.activation(ot[:, h, :, :].rearrange("p j n -> p (j n)"), banks[h][:, :], ACT.Copy).then_inc(otr, 1)
                    steps(ac, IT, body)

        passes[0] += 1

        LL = K * P // 32
        KC, FW = AGG[:, 0:LL], AGG[:, LL:2 * LL]
        BW, SC = SCR[:, 0:LL], TAB[:, 0:LL]
        with scratch() as st:
            tb = lambda name, shape, dt=F32: st.enter_context(tile(name, shape, dt))
            stage = TAB[:, 0:5 * KP].rearrange("p (t j e) -> p t j e", t=KT7, j=5)
            keyi = SCR[:, 0:KP]
            val = SCR[:, KP:2 * KP]
            pad = tb("pad", [1, P])
            cols = tb("cols", [P, 2])
            rows = tb("rows", [1, 4, P])
            cin = tb("cin", [P, 1])
            with phase("dv ready tr ev st") as (block, (dv, ready, tr, ev, sto)):
                @block.vector
                def _(v):
                    n = [0]

                    def link(ins):
                        n[0] += 1
                        ins.then_inc(dv, 1)
                        v.wait_ge(dv, n[0])

                    v.memset(pad[:, :], -2.0)
                    link(v.tensor_scalar(val, drel[:, :], 0.0, None, ALU.is_ge))
                    link(v.scalar_tensor_tensor(val, drel[:, :], float(P - 1), val, ALU.is_le, ALU.mult))
                    link(v.scalar_tensor_tensor(keyi, dkey[:, :], 1.0, val, ALU.add, ALU.mult))
                    link(v.tensor_scalar(keyi, keyi, -1.0, None, ALU.add))
                    v.sem_inc(ready, 1)
                    for t in range(KT7):
                        v.wait_ge(tr, t + 1)
                        v.tensor_copy(stage[:, t, 0:4, :], banks[2 * (t % 2)][:, :].rearrange("p (j e) -> p j e", j=4))
                        v.tensor_copy(stage[:, t, 4, :], banks[2 * (t % 2) + 1][:, 0:P]).then_inc(ev, 1)

                @block.tensor
                def _(pe):
                    pe.wait_ge(ready, 1)
                    for t in range(KT7):
                        if t >= 2:
                            pe.wait_ge(ev, t - 1)
                        for h in range(H):
                            pe.transpose(banks[2 * (t % 2)][:, h * P:(h + 1) * P], A[:, h, t * P:(t + 1) * P], ident[:, :])
                        pe.transpose(banks[2 * (t % 2) + 1][:, 0:P], keyi[:, t * P:(t + 1) * P], ident[:, :]).then_inc(tr, 1)

                @block.sync
                def _(sp):
                    sp.wait_ge(ready, 1)
                    sp.dma_start(KEY[0:P].rearrange("(a n) -> a n", a=1), pad[:, :]).then_inc(sto, 16)
                    for t in range(KT7):
                        sp.wait_ge(ev, t + 1)
                        sp.dma_start(SEQ[:, t * P * P:(t + 1) * P * P].rearrange("h (k e) -> k h e", e=P), stage[:, t, 0:4, :]).then_inc(sto, 16)
                        sp.dma_start(KEY[P + t * P * P:P + (t + 1) * P * P].rearrange("(k e) -> k e", e=P), stage[:, t, 4, :]).then_inc(sto, 16)
                    sp.wait_ge(sto, 16 * (2 * KT7 + 1))

            with phase("ld dv pe back ex sto") as (block, (ld, dv, pes, back, exd, sto)):
                @block.sync
                def _(sp):
                    for h in range(H):
                        part = slice(32 * h, 32 * h + 32)
                        sp.dma_start(SC[part, :], SEQ[h, 0:K * P].rearrange("(l j) -> l j", j=LL)).then_inc(ld, 16)
                        for dst, off in ((KC, 0), (FW, -1), (BW, 1)):
                            sp.dma_start(dst[part, :], KEY[P + off:P + off + K * P].rearrange("(l j) -> l j", j=LL)).then_inc(ld, 16)
                    sp.wait_ge(exd, 1)
                    sp.dma_start(SEX.rearrange("h (l j) -> (h l) j", j=LL), KC).then_inc(sto, 16)
                    sp.wait_ge(sto, 16)

                @block.vector
                def _(v):
                    n = [0]

                    def link(ins):
                        n[0] += 1
                        ins.then_inc(dv, 1)
                        v.wait_ge(dv, n[0])

                    def carries(i, last, flags, back_to_front):
                        v.tensor_copy(cols[:, 0:1], last)
                        link(v.tensor_reduce(cols[:, 1:2], flags, AX.X, ALU.add))
                        v.sem_inc(back, 1)
                        v.wait_ge(pes, 2 * i + 1)
                        v.memset(rows[:, 3, :], -BIG)
                        link(v.tensor_copy(rows[:, 0:2, :], banks[0][0:1, 0:2 * P].rearrange("p (j n) -> p j n", j=2)))
                        if back_to_front:
                            link(v.tensor_tensor_scan(rows[:, 2, ::-1], rows[:, 1, ::-1], rows[:, 0, ::-1], -BIG, ALU.add, ALU.max))
                            link(v.tensor_copy(rows[:, 3, 0:P - 1], rows[:, 2, 1:P]))
                        else:
                            link(v.tensor_tensor_scan(rows[:, 2, :], rows[:, 1, :], rows[:, 0, :], -BIG, ALU.add, ALU.max))
                            link(v.tensor_copy(rows[:, 3, 1:P], rows[:, 2, 0:P - 1]))
                        v.sem_inc(back, 1)
                        v.wait_ge(pes, 2 * i + 2)
                        link(v.tensor_copy(cin[:, :], banks[1][:, 0:1]))

                    v.wait_ge(ld, 16 * 16)
                    link(v.tensor_tensor(FW, FW, KC, ALU.not_equal))
                    link(v.tensor_tensor(BW, BW, KC, ALU.not_equal))
                    link(v.tensor_scalar(FW, FW, -BIG, None, ALU.mult))
                    link(v.tensor_scalar(BW, BW, -BIG, None, ALU.mult))
                    link(v.tensor_tensor_scan(KC, FW, SC, -BIG, ALU.add, ALU.max))
                    carries(0, KC[:, LL - 1:LL], FW, False)
                    link(v.tensor_tensor_scan(KC, FW, SC, cin[:, :], ALU.add, ALU.max))
                    link(v.tensor_tensor_scan(FW[:, ::-1], BW[:, ::-1], KC[:, ::-1], -BIG, ALU.add, ALU.max))
                    carries(1, FW[:, 0:1], BW, True)
                    link(v.tensor_tensor_scan(FW[:, ::-1], BW[:, ::-1], KC[:, ::-1], cin[:, :], ALU.add, ALU.max))
                    link(v.tensor_tensor(SC, SC, FW, ALU.subtract))
                    v.sem_inc(back, 1)

                @block.tensor
                def _(pe):
                    for i in range(2):
                        pe.wait_ge(back, 2 * i + 1)
                        pe.matmul(banks[0][0:1, 0:P], cols[:, 0:1], ident[:, :], start=True, stop=True)
                        pe.matmul(banks[0][0:1, P:2 * P], cols[:, 1:2], ident[:, :], start=True, stop=True).then_inc(pes, 1)
                        pe.wait_ge(back, 2 * i + 2)
                        pe.matmul(banks[1][:, 0:1], rows[0:1, 3, :], ones[0:1, 0:1], start=True, stop=True).then_inc(pes, 1)

                @block.scalar
                def _(ac):
                    ac.wait_ge(back, 5)
                    ac.activation(KC, SC, ACT.Exp, scale=float(DH) ** -0.5).then_inc(exd, 1)

            xs = TAB[:, 0:4 * KP].rearrange("p (t h e) -> p t h e", t=KT7, h=H)
            with phase("ld tr ev") as (block, (ld, tr, ev)):
                tiles = [(t, min(P, K - t * P)) for t in range(KT7)]

                @block.sync
                def _(sp):
                    for t, m in tiles:
                        sp.dma_start(xs[0:m, t, :, :], SEX[:, t * P * P:(t * P + m) * P].rearrange("h (k e) -> k h e", e=P)).then_inc(ld, 16)

                @block.tensor
                def _(pe):
                    pe.wait_ge(ld, 16 * KT7)
                    for t, m in tiles:
                        if t >= 2:
                            pe.wait_ge(ev, t - 1)
                        for h in range(H):
                            last = pe.transpose(banks[t % 2][:, h * P:h * P + m], xs[0:m, t, h, :], ident[0:m, 0:m])
                        last.then_inc(tr, 1)

                @block.vector
                def _(v):
                    for t, m in tiles:
                        v.wait_ge(tr, t + 1)
                        v.tensor_copy(A[:, :, t * P:t * P + m],
                                      banks[t % 2][:, :].rearrange("p (h k) -> p h k", h=H)[:, :, 0:m]).then_inc(ev, 1)

        AGGg = AGG[:, :].rearrange("p (g f) -> p g f", f=136)

        def edge_sum(width, table=None):
            with scratch() as st:
                tb = lambda name, shape, dt=F32: st.enter_context(tile(name, shape, dt))
                gw = 64 if table is not None else D
                gb = tb("gb", [P, U, gw])
                ic = tb("ic", [P, 2, 4], I32)
                dc = tb("dc", [P, U])
                ec = tb("ec", [P, U, H])
                ms = tb("ms", [P, 2, 4, 136])
                oh = tb("oh", [P, 2, 4, P])
                with phase("l0 l1 icr rdy mm own") as (block, S):
                    got = gathered if table is not None else S[0:2]
                    icr, rdy, mm, own = S[2:]

                    if table is not None:
                        @block.gpsimd
                        def _(po):
                            def body(it, first):
                                for h in range(2):
                                    if not first:
                                        po.wait_ge(mm, (it - 1) * U + 4 * h + 4)
                                    po.tensor_copy(ic[:, h, :], srci[:, bass.ds(it * U + 4 * h, 4)]).then_inc(icr, 1)
                                    po.wait_ge(icr, it * 2 + h + 1)
                                    po.nop(nofuse=True)
                                    for j in range(4):
                                        po.indirect_dma_start(out=gb[:, 4 * h + j, :], out_offset=None, in_=table[:, :],
                                                              in_offset=bass.IndirectOffsetOnAxis(ap=ic[:, h, j:j + 1], axis=0)).then_inc(got[4 * h + j], 16)
                            steps(po, IT, body)
                    else:
                        @block.sync
                        def _(sp):
                            def body(it, first):
                                for h in range(2):
                                    if not first:
                                        sp.wait_ge(rdy, (it - 1) * 2 + h + 1)
                                    sp.dma_start(gb[:, 4 * h:4 * h + 4, :],
                                                 VE[bass.ds(it * U + 4 * h, 4), :, :].rearrange("k p f -> p k f")).then_inc(got[h], 16)
                            steps(sp, IT, body)

                    @block.vector
                    def _(v):
                        regs = [st.enter_context(v.register(unique(f"eblk{j}"))) for j in range(U)]
                        v.memset(ms[:, :, :, 132:133], 1.0)
                        v.memset(AGG[:, :], 0.0).then_inc(own, 1)
                        per = U + 1

                        def body(it, first):
                            v.load(regs, gidx[0:1, bass.ds(it * U, U)])
                            v.wait_ge(own, it * per + 1)
                            if table is None:
                                v.tensor_copy(ec[:, :, :], A[:, :, bass.ds(it * U, U)].rearrange("p h j -> p j h"))
                            v.tensor_copy(dc[:, :], drel[:, bass.ds(it * U, U)]).then_inc(own, 1)
                            v.wait_ge(own, it * per + 2)
                            for h in range(2):
                                hh = it * 2 + h
                                if not first:
                                    v.wait_ge(mm, (hh - 2) * 4 + 4)
                                if table is None:
                                    v.wait_ge(got[h], it * 16 + 16)
                                    e4 = ec[:, 4 * h:4 * h + 4, :]
                                    v.tensor_tensor(ms[:, h, :, 0:D].rearrange("p j (h f) -> p j h f", h=H),
                                                    gb[:, 4 * h:4 * h + 4, :].rearrange("p j (h f) -> p j h f", h=H),
                                                    e4.unsqueeze(3).broadcast_to([P, 4, H, DH]), ALU.mult)
                                    v.tensor_copy(ms[:, h, :, D:D + H], e4)
                                for j in range(4):
                                    last = v.tensor_scalar(oh[:, h, j, :], iota[:, :], dc[:, 4 * h + j:4 * h + j + 1], None, ALU.is_equal)
                                last.then_inc(rdy, 1)
                            for h in range(2):
                                for j in range(4):
                                    k = (it * 2 + h) * 4 + j
                                    g = v.snap(regs[4 * h + j], min_val=0, max_val=G - 1)
                                    v.wait_ge(mm, k + 1)
                                    if h or j:
                                        v.wait_ge(own, it * per + 2 + 4 * h + j)
                                    acc = AGG[:, bass.ds(g * 136, width)]
                                    v.tensor_tensor(acc, acc, banks[4 * h + j][:, 0:width], ALU.add).then_inc(own, 1)
                        steps(v, IT, body)

                    @block.tensor
                    def _(pe):
                        def body(it, first):
                            for h in range(2):
                                pe.wait_ge(rdy, it * 2 + h + 1)
                                for j in range(4):
                                    k = (it * 2 + h) * 4 + j
                                    if not first:
                                        pe.wait_ge(own, (it - 1) * (U + 1) + 3 + 4 * h + j)
                                    if table is not None:
                                        pe.wait_ge(got[4 * h + j], landed(it))
                                        rhs = gb[:, 4 * h + j, :]
                                    else:
                                        rhs = ms[:, h, j, 0:width]
                                    pe.matmul(banks[4 * h + j][:, 0:width], oh[:, h, j, :], rhs, start=True, stop=True).then_inc(mm, 1)
                        steps(pe, IT, body)

            if table is not None:
                passes[0] += 1

        edge_sum(D + H + 1)

        w = scratch()
        row = lambda n, width: tbw(n, [P, width])
        wgb, gab, beb, bgb, alb = row("wgb", 3 * D), row("gab", D), row("beb", D), row("bgb", 1), row("alb", 1)
        rden = tbw("rden", [P, GB, H])
        with phase("ld dv sg sgr sq lx") as (block, (ld, dv, sg, sgr, sq, lx)):
            @block.sync
            def _(sp):
                for dst, n in ((wgb, "wg"), (gab, "gamma"), (beb, "beta"), (bgb, "bg"), (alb, "alpha")):
                    sp.dma_start(dst[:, :], a[n].broadcast_to([P, dst.shape[1]])).then_inc(ld, 16)

            @block.vector
            def _(v):
                n = [0]

                def link(ins):
                    n[0] += 1
                    ins.then_inc(dv, 1)
                    v.wait_ge(dv, n[0])

                spread = lambda col: col.unsqueeze(2).broadcast_to([P, GB, D])
                along = lambda r: r.unsqueeze(1).broadcast_to([P, GB, D])
                agg = AGGg[:, :, 0:D]
                v.wait_ge(ld, 16 * 5)
                den = AGGg[:, :, D:D + H]
                v.tensor_copy(cnt[:, :], AGG[:, D + H::136])
                link(v.scalar_tensor_tensor(rden[:, :, :], den, 0.0, den, ALU.is_le, ALU.add))
                link(v.reciprocal(rden[:, :, :], rden[:, :, :]))
                a4 = agg.rearrange("p g (h f) -> p g h f", h=H)
                for h in range(H):
                    link(v.tensor_tensor(agg[:, :, h * DH:(h + 1) * DH], agg[:, :, h * DH:(h + 1) * DH],
                                         rden[:, :, h:h + 1].broadcast_to([P, GB, DH]), ALU.mult))
                link(v.tensor_tensor(wgb[:, 0:D], wgb[:, 0:D], wgb[:, 2 * D:3 * D], ALU.add))
                link(v.tensor_tensor(wgb[:, D:2 * D], wgb[:, D:2 * D], wgb[:, 2 * D:3 * D], ALU.subtract))
                z0, z1, gate = (stats[:, j, :] for j in range(3))
                link(v.tensor_tensor(SCRg, Zg, along(wgb[:, 0:D]), ALU.mult))
                link(v.tensor_reduce(z0, SCRg, AX.X, ALU.add))
                link(v.tensor_tensor(SCRg, agg, along(wgb[:, D:2 * D]), ALU.mult))
                link(v.tensor_reduce(z1, SCRg, AX.X, ALU.add))
                link(v.scalar_tensor_tensor(z0, z0, bgb[:, 0:1], z1, ALU.add, ALU.add))
                link(v.tensor_scalar(z0, z0, -80.0, None, ALU.max))
                v.sem_inc(sg, 1)
                v.tensor_tensor(SCRg, Zg, agg, ALU.subtract)
                v.wait_ge(sgr, 1)
                link(v.tensor_scalar(gate, gate, 1.0, None, ALU.add))
                link(v.reciprocal(gate, gate))
                link(v.tensor_tensor(SCRg, SCRg, spread(gate), ALU.mult))
                link(v.tensor_tensor(SCRg, SCRg, agg, ALU.add))
                mean, ssq, tmp, y = (stats[:, j, :] for j in range(4))
                link(v.tensor_reduce(mean, SCRg, AX.X, ALU.add))
                link(v.tensor_scalar(mean, mean, 1.0 / D, None, ALU.mult))
                link(v.tensor_tensor(SCRg, SCRg, spread(mean), ALU.subtract))
                v.sem_inc(sg, 1)
                v.wait_ge(sq, 1)
                link(v.tensor_reduce(ssq, Zg, AX.X, ALU.add))
                link(v.tensor_scalar(ssq, ssq, 1.0 / D, EPS_LN, ALU.mult, ALU.add))
                v.sem_inc(sg, 1)
                v.wait_ge(lx, 2)
                rsqrt_chain(link, v, None, y, ssq, tmp)
                rsqrt_chain(link, v, None, y, ssq, tmp)
                link(v.tensor_tensor(SCRg, SCRg, spread(y), ALU.mult))
                link(v.tensor_tensor(SCRg, SCRg, along(gab[:, :]), ALU.mult))
                link(v.tensor_tensor(SCRg, SCRg, along(beb[:, :]), ALU.add))
                link(v.tensor_scalar(Z[:, :], SCR[:, :], 0.0, alb[:, 0:1], ALU.min, ALU.mult))
                link(v.scalar_tensor_tensor(SCR[:, :], SCR[:, :], 0.0, Z[:, :], ALU.max, ALU.add))
                link(v.tensor_tensor(X[:, :], X[:, :], SCR[:, :], ALU.add))

            @block.scalar
            def _(ac):
                ac.wait_ge(sg, 1)
                ac.activation(stats[:, 2, :], stats[:, 0, :], ACT.Exp, scale=-1.0).then_inc(sgr, 1)
                ac.wait_ge(sg, 2)
                ac.activation(Z[:, :], SCR[:, :], ACT.Square).then_inc(sq, 1)
                ac.wait_ge(sg, 3)
                ac.activation(stats[:, 2, :], stats[:, 1, :], ACT.Ln).then_inc(lx, 1)
                ac.wait_ge(lx, 1)
                ac.activation(stats[:, 3, :], stats[:, 2, :], ACT.Exp, scale=-0.5).then_inc(lx, 1)
        w.close()

        def show_x():
            with phase("o") as (block, (o,)):
                @block.sync
                def _(sp):
                    sp.dma_start(out.rearrange("(g p) f -> p g f", p=P), Xg).then_inc(o, 16)
                    sp.wait_ge(o, 16)

        if stop == "l1":
            show_x()
            return

        normalise(Xg, TAB[:, 0:GB * D])
        w = scratch()
        weights["wlr1"], weights["b21w"], weights["wlr2"], weights["b22"] = (
            tbw("wlr1", [D, D]), tbw("b21w", [1, D]), tbw("wlr2", [D, D]), tbw("b22", [1, D]))
        rdeg = tbw("rdeg", [P, GB])
        with phase("ld z") as (block, (ld, z)):
            @block.vector
            def _(v):
                v.memset(weights["b21w"][:, 0:64], 0.0).then_inc(z, 1)

            @block.sync
            def _(sp):
                sp.dma_start(weights["b21w"][:, 64:128], a["b21"]).then_inc(ld, 16)
                for n in ("wlr1", "wlr2", "b22"):
                    sp.dma_start(weights[n][:, :], a[n]).then_inc(ld, 16)
                sp.wait_ge(ld, 64)

        def take_yz(e, g, ps, t):
            e.activation(Z[:, bass.ds(g * D, 64)], ps[:, 64:128], ACT.Copy)
            return e.activation(t, ps[:, 0:64], ACT.Copy)

        node_products(relu_norm_block, weights["wlr1"], weights["b21w"], take_yz, "scalar", Y1, 64)
        edge_sum(64, Y1)
        with phase("dv r st") as (block, (dv, r, sto)):
            @block.vector
            def _(v):
                n = [0]

                def link(ins):
                    n[0] += 1
                    ins.then_inc(dv, 1)
                    v.wait_ge(dv, n[0])

                zz = Zg[:, :, 64:128]
                link(v.tensor_scalar(rdeg[:, :], cnt[:, :], 1.0, None, ALU.max))
                link(v.reciprocal(rdeg[:, :], rdeg[:, :]))
                link(v.tensor_tensor(zz, AGGg[:, :, 0:64], rdeg[:, :].unsqueeze(2).broadcast_to([P, GB, 64]), ALU.mult))
                link(v.tensor_tensor(zz, zz, Zg[:, :, 0:64], ALU.add))
                link(v.tensor_scalar(zz, zz, 0.0, None, ALU.max))
                v.sem_inc(r, 1)

            @block.sync
            def _(sp):
                sp.wait_ge(r, 1)
                sp.dma_start(H2.rearrange("(g p) f -> p g f", p=P), Zg[:, :, 64:128]).then_inc(sto, 16)
                sp.wait_ge(sto, 16)
        edge_sum(64, H2)
        with phase("dv") as (block, (dv,)):
            @block.vector
            def _(v):
                v.tensor_tensor(Zg[:, :, 0:64], AGGg[:, :, 0:64], rdeg[:, :].unsqueeze(2).broadcast_to([P, GB, 64]), ALU.mult)

        def add_x(e, g, ps, t):
            xb = X[:, bass.ds(g * D, D)]
            return e.tensor_tensor(xb, xb, ps[:, 0:D], ALU.add)

        node_products(lambda v, g, t: v.tensor_copy(t, Z[:, bass.ds(g * D, D)]), weights["wlr2"], weights["b22"], add_x, "vector")
        w.close()
        if stop == "l2":
            show_x()
            return

        normalise(Xg, TAB[:, 0:GB * D])
        TABg = TAB[:, :].rearrange("p (g f) -> p g f", f=MW)
        with phase("dv h sq st") as (block, (dv, hr, sq, sto)):
            @block.vector
            def _(v):
                v.memset(TABg[:, :, D:MW], 0.0).then_inc(dv, 1)
                v.scalar_tensor_tensor(TABg[:, :, 0:D], SCRg, 0.0, rstd.unsqueeze(2).broadcast_to([P, GB, D]), ALU.max, ALU.mult).then_inc(hr, 1)
                v.wait_ge(sq, 1)
                v.wait_ge(dv, 1)
                v.tensor_reduce(TABg[:, :, D], SCRg, AX.X, ALU.add).then_inc(hr, 1)

            @block.scalar
            def _(ac):
                ac.wait_ge(hr, 1)
                ac.activation(SCRg, TABg[:, :, 0:D], ACT.Square).then_inc(sq, 1)

            @block.sync
            def _(sp):
                sp.wait_ge(hr, 2)
                sp.dma_start(H3.rearrange("(g p) f -> p g f", p=P), TABg).then_inc(sto, 16)
                sp.wait_ge(sto, 16)

        Q = 4
        STEPS = K // (4 * Q)
        with scratch() as st:
            tb = lambda name, shape, dt=F32: st.enter_context(tile(name, shape, dt))
            gb = tb("gb", [P, Q, 4, MW])
            ic = tb("ic", [P, Q, 4], I32)
            dc = tb("dc", [P, Q, 4])
            oh = tb("oh", [P, 2, 4, P])
            ot = tb("ot", [P, 2, 4, P])
            junk = tb("junk", [P, 4, D])
            junk2 = tb("junk2", [P, 4, D])
            sc = tb("sc", [P, Q, 7, 4])
            tm = tb("tm", [P, 2, 4, D])
            mr = tb("mr", [P, Q, 4, MW])
            got = [st.enter_context(nc.semaphore(unique(f"got3_{i}"))) for i in range(4 * Q)]

            def units(unit):
                every = 10 * Q

                def run(it, q, lo, hi):
                    unit(it, q, lambda d: lo <= q + d < hi)

                def whole(eng):
                    for q in range(1, Q):
                        run(-1, q, Q, every)
                    for q in range(Q):
                        run(0, q, 0, every)
                    with eng.Fori(1, STEPS - 1) as it:
                        for q in range(Q):
                            run(it, q, -every, every)
                    for q in range(Q):
                        run(STEPS - 1, q, -every, Q)
                    for q in range(2):
                        run(STEPS, q, -every, 0)
                return whole

            with phase("ms0 ms1 ms2 ms3 icr dcr ohr tr otr hdr abr tmr mmr sqr rowr own") as (block, S):
                mst = S[0:4]
                icr, dcr, ohr, tr, otr, hdr, abr, tmr, mmr, sqr, rowr, own = S[4:]

                @block.gpsimd
                def _(po):
                    def body(it, first):
                        for q in range(Q):
                            if not first:
                                po.wait_ge(mmr, it * (4 * Q) + (4 * q - 12))
                            po.tensor_copy(ic[:, q, :], srci[:, bass.ds(it * (4 * Q) + 4 * q, 4)]).then_inc(icr, 1)
                            po.wait_ge(icr, it * Q + (q + 1))
                            po.nop(nofuse=True)
                            for j in range(4):
                                po.indirect_dma_start(out=gb[:, q, j, :], out_offset=None, in_=H3[:, :],
                                                      in_offset=bass.IndirectOffsetOnAxis(ap=ic[:, q, j:j + 1], axis=0)).then_inc(got[4 * q + j], 16)
                    steps(po, STEPS, body)

                @block.vector
                def _(v):
                    LINKS = 7

                    def unit(it, q, ok):
                        u = it * Q + q
                        h = q % 2

                        def one_hot():
                            if ok(0):
                                v.wait_ge(tr, u + 1)
                            v.wait_ge(dcr, u + 3)
                            for j in range(4):
                                last = v.tensor_scalar(oh[:, h, j, :], iota[:, :], dc[:, (q + 2) % Q, j:j + 1], None, ALU.is_equal)
                            last.then_inc(ohr, 1)

                        def columns():
                            if ok(-1):
                                v.wait_ge(ohr, u)
                            v.tensor_copy(dc[:, (q + 3) % Q, :], drel[:, bass.ds(u * 4 + 12, 4)]).then_inc(dcr, 1)

                        n = [0]

                        def link(ins):
                            n[0] += 1
                            ins.then_inc(own, 1)
                            return n[0]

                        def linked(m):
                            v.wait_ge(own, u * LINKS + m)

                        def message(j):
                            if ok(-1):
                                if j == 0:
                                    if ok(-1 - Q):
                                        v.wait_ge(mst[(q - 1) % Q], (it + (q - 1) // Q) * 16)
                                    v.wait_ge(own, u * LINKS)
                                v.wait_ge(tmr, u * 4 + (j - 3))
                                v.scalar_tensor_tensor(mr[:, (q - 1) % Q, j, 0:D], gb[:, (q - 1) % Q, j, 0:D], sc[:, (q - 1) % Q, 4, j:j + 1],
                                                       tm[:, 1 - h, j, :], ALU.mult, ALU.subtract).then_inc(mmr, 1)

                        def norms():
                            if ok(-2):
                                v.wait_ge(sqr, u * 4 - 4)
                                y2 = sc[:, (q - 2) % Q, 6, :]
                                for k, f in enumerate((-0.5, 0.5, 1.0, -1.0)):
                                    last = v.tensor_scalar(mr[:, (q - 2) % Q, :, D + k], y2, f, None, ALU.mult)
                                last.then_inc(rowr, 1)

                        if ok(2):
                            one_hot()
                        if ok(3):
                            columns()
                        if not ok(0):
                            for j in range(4):
                                message(j)
                            norms()
                            return
                        sd, d2, p1, den, ca, cb = (sc[:, q, k, :] for k in range(6))
                        s2 = gb[:, q, :, D]
                        for j in range(4):
                            v.wait_ge(got[4 * q + j], it * 16 + 16)
                            if j % 2 == 0:
                                v.wait_ge(hdr, u * 2 + (j // 2 + 1))
                                v.tensor_copy(d2[:, j:j + 2], banks[2 + 2 * h + j // 2][:, 0:258].rearrange("p (j c) -> p j c", j=2)[:, :, D])
                            hd = banks[2 + 2 * h + j // 2][:, (j % 2) * 129:(j % 2) * 129 + D]
                            last = v.tensor_tensor_reduce(junk[:, j, :], gb[:, q, j, 0:D], hd, 1.0, 0.0, ALU.mult, ALU.add, sd[:, j:j + 1])
                        dots = link(last)
                        message(0)
                        linked(dots)
                        one = link(v.tensor_scalar(p1, sd, -2.0, 1.0, ALU.mult, ALU.add))
                        v.tensor_scalar(cb, s2, -1.0, 1.0, ALU.mult, ALU.add)
                        prod = link(v.tensor_tensor(den, s2, d2, ALU.mult))
                        message(1)
                        linked(prod)
                        v.tensor_tensor(ca, p1, d2, ALU.add)
                        ds_ = link(v.tensor_tensor(den, den, p1, ALU.add))
                        message(2)
                        linked(ds_)
                        mx = link(v.tensor_scalar(den, den, EPS_M, None, ALU.max))
                        message(3)
                        linked(mx)
                        rc = link(v.reciprocal(den, den))
                        norms()
                        linked(rc)
                        v.tensor_tensor(cb, cb, den, ALU.mult).then_inc(abr, 1)
                        link(v.tensor_tensor(ca, ca, den, ALU.mult))
                        assert n[0] == LINKS
                    units(unit)(v)

                @block.tensor
                def _(pe):
                    regs = [st.enter_context(pe.register(unique(f"pblk{j}"))) for j in range(4)]

                    def unit(it, q, ok):
                        u = it * Q + q
                        h = q % 2
                        if ok(1):
                            pe.load(regs, gidx[0:1, bass.ds(u * 4 + 4, 4)])
                        if ok(2):
                            pe.wait_ge(ohr, u + 3)
                            if ok(0):
                                pe.wait_ge(otr, u + 1)
                            for j in range(4):
                                last = pe.transpose(banks[h][:, j * P:(j + 1) * P], oh[:, h, j, :], ident[:, :])
                            last.then_inc(tr, 1)
                        if ok(1):
                            pe.wait_ge(otr, u + 2)
                            if ok(-1):
                                pe.wait_ge(tmr, u * 4)
                            for j in range(4):
                                g = pe.snap(regs[j], min_val=0, max_val=G - 1)
                                o = (j % 2) * 129
                                last = pe.matmul(banks[2 + 2 * (1 - h) + j // 2][:, o:o + 129], ot[:, 1 - h, j, :], TAB[:, bass.ds(g * MW, 129)],
                                                 start=True, stop=True)
                                if j % 2:
                                    last.then_inc(hdr, 1)
                    units(unit)(pe)

                @block.scalar
                def _(ac):
                    def unit(it, q, ok):
                        u = it * Q + q
                        h = q % 2
                        if ok(2):
                            ac.wait_ge(tr, u + 3)
                            if ok(0):
                                ac.wait_ge(hdr, u * 2 + 2)
                            ac.activation(ot[:, h, :, :].rearrange("p j n -> p (j n)"), banks[h][:, :], ACT.Copy).then_inc(otr, 1)
                        if ok(-1):
                            for j in range(4):
                                ac.wait_ge(mmr, u * 4 + (j - 3))
                                ac.activation(junk2[:, j, :], mr[:, (q - 1) % Q, j, 0:D], ACT.Square,
                                              accum_out=sc[:, (q - 1) % Q, 6, j:j + 1]).then_inc(sqr, 1)
                        if ok(0):
                            ac.wait_ge(abr, u + 1)
                            for j in range(4):
                                hd = banks[2 + 2 * h + j // 2][:, (j % 2) * 129:(j % 2) * 129 + D]
                                ac.activation(tm[:, h, j, :], hd, ACT.Copy, scale=sc[:, q, 5, j:j + 1]).then_inc(tmr, 1)
                    units(unit)(ac)

                @block.sync
                def _(sp):
                    rows = MSG.rearrange("(k p) c -> k p c", p=P)

                    def body(it, first):
                        for q in range(Q):
                            sp.wait_ge(rowr, it * Q + (q + 1))
                            sp.dma_start(rows[bass.ds(it * (4 * Q) + 4 * q, 4), :, :].rearrange("k p c -> p k c"), mr[:, q, :, :]).then_inc(mst[q], 16)
                    steps(sp, STEPS, body)
                    for q in range(Q):
                        sp.wait_ge(mst[q], 16 * STEPS)

        w = scratch()
        WR = 2
        wfirst, woff, weff = tbw("wfirst", [P, GB]), tbw("woff", [P, GB]), tbw("weff", [P, GB])
        tcount = tbw("tcount", [1, GB + 2])
        tcounti = w.enter_context(tile("tcounti", [1, GB + 2], I32))
        with scratch() as st:
            tb = lambda name, shape, dt=F32: st.enter_context(tile(name, shape, dt))
            before = tb("before", [P, P])
            gpos = tb("gpos", [P, GB])
            tot, pos, nw, fr = tb("tot", [P, GB]), tb("pos", [P, GB]), tb("nw", [P, GB]), tb("fr", [P, GB])
            ii = tb("ii", [P, GB], I32)
            mx = tb("mx", [GB, 1])
            with phase("pr pe1 dv nwr pe2 mxr pe3") as (block, (pr, pe1, dv, nwr, pe2, mxr, pe3)):
                @block.gpsimd
                def _(po):
                    po.memset(before[:, :], 1.0).then_inc(pr, 1)
                    po.iota(gpos[:, :], [[P, GB]], base=0, channel_multiplier=0, allow_small_or_imprecise_dtypes=True)
                    po.wait_ge(pr, 1)
                    po.affine_select(out=before[:, :], in_=before[:, :], compare_op=ALU.is_gt, fill=0.0, base=0,
                                     pattern=[[1, P]], channel_multiplier=-1).then_inc(pr, 1)

                @block.tensor
                def _(pe):
                    pe.wait_ge(pr, 2)
                    pe.matmul(banks[0][:, 0:GB], before[:, :], cnt[:, :], start=True, stop=True)
                    pe.matmul(banks[0][:, GB:2 * GB], ones[:, :], cnt[:, :], start=True, stop=True).then_inc(pe1, 1)
                    pe.wait_ge(nwr, 1)
                    pe.transpose(banks[1][0:GB, 0:P], nw[:, :], ident[:, :]).then_inc(pe2, 1)
                    pe.wait_ge(mxr, 1)
                    pe.matmul(banks[2][0:1, 0:GB], mx[:, :], ident[0:GB, 0:GB], start=True, stop=True).then_inc(pe3, 1)

                @block.vector
                def _(v):
                    n = [0]

                    def link(ins):
                        n[0] += 1
                        ins.then_inc(dv, 1)
                        v.wait_ge(dv, n[0])

                    v.wait_ge(pr, 2)
                    v.wait_ge(pe1, 1)
                    link(v.tensor_copy(tot[:, :], banks[0][:, GB:2 * GB]))
                    link(v.memset(fr[:, :], 0.0))
                    link(v.tensor_tensor_scan(nw[:, :], tot[:, :], fr[:, :], 0.0, ALU.add, ALU.add))
                    link(v.tensor_tensor(pos[:, :], nw[:, :], tot[:, :], ALU.subtract))
                    link(v.tensor_tensor(pos[:, :], pos[:, :], banks[0][:, 0:GB], ALU.add))
                    link(v.tensor_tensor(pos[:, :], pos[:, :], gpos[:, :], ALU.add))
                    link(v.tensor_copy(ii[:, :], pos[:, :]))
                    link(v.tensor_scalar(ii[:, :], ii[:, :], 1, None, ALU.arith_shift_right))
                    link(v.tensor_copy(wfirst[:, :], ii[:, :]))
                    link(v.scalar_tensor_tensor(woff[:, :], wfirst[:, :], -float(WR), pos[:, :], ALU.mult, ALU.add))
                    link(v.tensor_tensor(weff[:, :], woff[:, :], cnt[:, :], ALU.add))
                    link(v.tensor_scalar(nw[:, :], weff[:, :], float(2 * WR - 1), None, ALU.add))
                    link(v.tensor_copy(ii[:, :], nw[:, :]))
                    link(v.tensor_scalar(ii[:, :], ii[:, :], 2, None, ALU.arith_shift_right))
                    link(v.tensor_copy(nw[:, :], ii[:, :]))
                    link(v.scalar_tensor_tensor(nw[:, :], cnt[:, :], 0.0, nw[:, :], ALU.is_gt, ALU.mult))
                    v.sem_inc(nwr, 1)
                    v.wait_ge(pe2, 1)
                    link(v.tensor_reduce(mx[:, :], banks[1][0:GB, 0:P], AX.X, ALU.max))
                    v.sem_inc(mxr, 1)
                    v.wait_ge(pe3, 1)
                    link(v.tensor_scalar(tcount[:, 0:GB], banks[2][0:1, 0:GB], 1.0, None, ALU.max))
                    link(v.tensor_reduce(tcount[:, GB:GB + 1], tcount[:, 1:GB], AX.X, ALU.add))
                    link(v.tensor_tensor(tcount[:, GB + 1:GB + 2], tcount[:, 0:1], tcount[:, GB:GB + 1], ALU.subtract))
                    link(v.tensor_scalar(tcount[:, GB + 1:GB + 2], tcount[:, GB + 1:GB + 2], 1.0, None, ALU.max))
                    v.tensor_copy(tcounti[:, :], tcount[:, :])

        LAST = K * P // WR - 1
        MAXT = E // (2 * WR) + 2 * GB
        with scratch() as st:
            tb = lambda name, shape, dt=F32: st.enter_context(tile(name, shape, dt))
            S2 = tb("S2", [P, 2, MW])
            mw = tb("mw", [P, 2, 2, WR, MW])
            mk = tb("mk", [P, 2, 2, WR, MW])
            wrow = tb("wrow", [P, 2, 2 * WR])
            wlen = tb("wlen", [P, 2])
            widx = tb("widx", [P, 2])
            wi = tb("wi", [P, 2, 2], I32)
            m0 = tb("m0", [P, 2, 2 * WR])
            msk = tb("msk", [P, 2, 2 * WR])
            woff1 = tb("woff1", [P, 1])
            jrow = tb("jrow", [P, 2 * WR])
            jk = tb("jk", [P, 2, 130])
            wv = tb("wv", [P, 2, D])
            den, rdn, be, t2 = tb("den", [P, 2]), tb("rdn", [P, 2]), tb("be", [P, 2]), tb("t2", [P, 2])
            wgat = [[st.enter_context(nc.semaphore(unique(f"wgat{b}{s}"))) for s in range(2)] for b in range(2)]
            windows = MSG.rearrange("(w r) c -> w (r c)", r=WR)

            def turns(eng, begin_block, turn):
                done = st.enter_context(eng.register(unique("done")))
                left = st.enter_context(eng.register(unique("left")))
                eng.reg_mov(done, 0)

                def one(g):
                    turn(g, eng.snap(done, min_val=0, max_val=MAXT))
                    eng.reg_add(done, done, 1)

                with eng.Fori(1, GB) as g:
                    begin_block(g, eng.snap(done, min_val=0, max_val=MAXT))
                    eng.load(left, tcounti[0:1, bass.ds(g, 1)])
                    with eng.Fori(0, eng.snap(left, min_val=1, max_val=MAXT)) as _:
                        one(g)
                eng.load(left, tcounti[0:1, GB + 1:GB + 2])
                with eng.Fori(0, eng.snap(left, min_val=1, max_val=MAXT)) as _:
                    one(GB - 1)

            with phase("pown masked used own") as (block, (pown, masked, used, own)):
                @block.gpsimd
                def _(po):
                    PT, PB, P0 = 8, 4, 4
                    po.iota(jrow[:, :], [[1, 2 * WR]], base=0, channel_multiplier=0, allow_small_or_imprecise_dtypes=True).then_inc(pown, 1)
                    po.wait_ge(pown, 1)
                    po.tensor_copy(widx[:, 0:1], wfirst[:, 0:1]).then_inc(pown, 1)
                    po.tensor_copy(wlen[:, 0:1], cnt[:, 0:1]).then_inc(pown, 1)
                    po.tensor_scalar(wrow[:, 0, :], jrow[:, :], woff[:, 0:1], None, ALU.subtract).then_inc(pown, 1)

                    def begin_block(g, t):
                        po.wait_ge(pown, t * PT + (g * PB + (P0 - PB)))
                        po.tensor_copy(widx[:, 1:2], wfirst[:, bass.ds(g, 1)]).then_inc(pown, 1)
                        po.tensor_copy(wlen[:, 1:2], cnt[:, bass.ds(g, 1)]).then_inc(pown, 1)
                        po.tensor_copy(woff1[:, :], woff[:, bass.ds(g, 1)]).then_inc(pown, 1)
                        po.wait_ge(pown, t * PT + (g * PB + (P0 - PB + 3)))
                        po.nop(nofuse=True)
                        po.tensor_scalar(wrow[:, 1, :], jrow[:, :], woff1[:, :], None, ALU.subtract).then_inc(pown, 1)

                    def turn(g, t):
                        n = [0]

                        def link(ins):
                            n[0] += 1
                            ins.then_inc(pown, 1)
                            po.wait_ge(pown, t * PT + (g * PB + (P0 + n[0])))
                            po.nop(nofuse=True)

                        po.wait_ge(pown, t * PT + (g * PB + P0))
                        po.wait_ge(masked, t * 2 + 2)
                        po.nop(nofuse=True)
                        link(po.tensor_scalar(wi[:, 0, :], widx[:, :], float(LAST), None, ALU.min))
                        link(po.tensor_scalar(wi[:, 1, :], widx[:, :], 1.0, float(LAST), ALU.add, ALU.min))
                        link(po.tensor_scalar(widx[:, :], widx[:, :], 2.0, None, ALU.add))
                        link(po.tensor_tensor(m0[:, :, :], wlen[:, :].unsqueeze(2).broadcast_to([P, 2, 2 * WR]), wrow[:, :, :], ALU.subtract))
                        link(po.tensor_scalar(m0[:, :, :], m0[:, :, :], 0.0, None, ALU.is_gt))
                        link(po.tensor_scalar(msk[:, :, :], wrow[:, :, :], 0.0, None, ALU.is_ge))
                        link(po.tensor_tensor(msk[:, :, :], msk[:, :, :], m0[:, :, :], ALU.mult))
                        link(po.tensor_scalar(wrow[:, :, :], wrow[:, :, :], 2.0 * WR, None, ALU.add))
                        assert n[0] == PT
                        po.nop(nofuse=True)
                        for b in range(2):
                            for s in range(2):
                                po.indirect_dma_start(out=mw[:, b, s, :, :].rearrange("p r c -> p (r c)"), out_offset=None, in_=windows[:, :],
                                                      in_offset=bass.IndirectOffsetOnAxis(ap=wi[:, b, s:s + 1], axis=0)).then_inc(wgat[b][s], 16)
                    turns(po, begin_block, turn)

                @block.scalar
                def _(ac):
                    ac.sem_inc(masked, 2)

                    def turn(g, t):
                        for b in range(2):
                            ac.wait_ge(used, t * 2 + (b + 1))
                            for s in range(2):
                                ac.wait_ge(wgat[b][s], t * 16 + 16)
                                for r in range(WR):
                                    last = ac.activation(mk[:, b, s, r, :], mw[:, b, s, r, :], ACT.Copy, scale=msk[:, s, WR * b + r:WR * b + r + 1])
                            last.then_inc(masked, 1)
                    turns(ac, lambda g, t: None, turn)

                @block.vector
                def _(v):
                    OPS = 11
                    DT, DB, D0 = 2 * WR * OPS, 3, 2
                    v.sem_inc(used, 2)
                    v.memset(S2[:, :, 0:D], 0.0).then_inc(own, 1)
                    v.memset(S2[:, :, D:D + 2], 1.0).then_inc(own, 1)

                    def begin_block(g, t):
                        v.wait_ge(own, t * DT + (g * DB + (D0 - DB)))
                        v.tensor_copy(AGG[:, bass.ds(g * 136 - 136, D)], S2[:, 1, 0:D]).then_inc(own, 1)
                        v.wait_ge(own, t * DT + (g * DB + (D0 - DB + 1)))
                        v.memset(S2[:, 1, 0:D], 0.0).then_inc(own, 1)
                        v.memset(S2[:, 1, D:D + 2], 1.0).then_inc(own, 1)

                    def turn(g, t):
                        n = [0]

                        def ops_done(m):
                            v.wait_ge(own, t * DT + (g * DB + (D0 + m)))

                        def do(ins):
                            n[0] += 1
                            ins.then_inc(own, 1)
                            return n[0]

                        sum_done = [0, 0]
                        d_done = 0
                        for b in range(2):
                            v.wait_ge(masked, t * 2 + (b + 3))
                            for r in range(WR):
                                M = mk[:, b, :, r, :]
                                ops_done(max(d_done, sum_done[0]))
                                do(v.tensor_tensor_reduce(jk[:, 0, :], S2[:, 0, 0:130], M[:, 0, 0:130], 2.0, 1.0, ALU.mult, ALU.add, den[:, 0:1]))
                                ops_done(sum_done[1])
                                dd = do(v.tensor_tensor_reduce(jk[:, 1, :], S2[:, 1, 0:130], M[:, 1, 0:130], 2.0, 1.0, ALU.mult, ALU.add, den[:, 1:2]))
                                for s in range(2):
                                    do(v.scalar_tensor_tensor(wv[:, s, :], S2[:, s, 0:D], M[:, s, D + 2:D + 3], M[:, s, 0:D], ALU.mult, ALU.add))
                                ops_done(dd)
                                ops_done(do(v.tensor_scalar(den[:, :], den[:, :], EPS_M, None, ALU.max)))
                                ops_done(do(v.reciprocal(rdn[:, :], den[:, :])))
                                ops_done(do(v.tensor_tensor(be[:, :], S2[:, :, D], rdn[:, :], ALU.mult)))
                                tt = do(v.tensor_tensor(t2[:, :], be[:, :], M[:, :, D + 3], ALU.mult))
                                sum_done[0] = do(v.scalar_tensor_tensor(S2[:, 0, 0:D], wv[:, 0, :], be[:, 0:1], S2[:, 0, 0:D], ALU.mult, ALU.add))
                                ops_done(tt)
                                d_done = do(v.tensor_tensor(S2[:, :, D], be[:, :], t2[:, :], ALU.add))
                                last = v.scalar_tensor_tensor(S2[:, 1, 0:D], wv[:, 1, :], be[:, 1:2], S2[:, 1, 0:D], ALU.mult, ALU.add)
                                sum_done[1] = do(last)
                            ops_done(sum_done[1])
                            v.sem_inc(used, 1)
                        assert n[0] == DT
                    turns(v, begin_block, turn)
                    v.tensor_copy(AGG[:, (GB - 1) * 136:(GB - 1) * 136 + D], S2[:, 1, 0:D])
                    v.tensor_copy(AGG[:, 0:D], S2[:, 0, 0:D])

        with scratch() as st:
            tb = lambda name, shape, dt=F32: st.enter_context(tile(name, shape, dt))
            small = tb("small", [P, 10, GB])
            with phase("dv go acd st") as (block, (dv, go, acd, sto)):
                n2, nn, nr, q0, q1, sc_, xy, q2, q3, f = (small[:, j, :] for j in range(10))
                sums = AGGg[:, :, 0:D]
                hs = TABg[:, :, 0:D]
                spread = lambda col: col.unsqueeze(2).broadcast_to([P, GB, D])

                @block.vector
                def _(v):
                    n = [0]

                    def link(ins):
                        n[0] += 1
                        ins.then_inc(dv, 1)
                        v.wait_ge(dv, n[0])

                    link(v.tensor_tensor(SCRg, sums, sums, ALU.mult))
                    link(v.tensor_reduce(n2, SCRg, AX.X, ALU.add))
                    link(v.tensor_scalar(q0, n2, 1e-30, None, ALU.max))
                    v.sem_inc(go, 1)
                    link(v.tensor_tensor(SCRg, sums, hs, ALU.mult))
                    link(v.tensor_reduce(xy, SCRg, AX.X, ALU.add))
                    link(v.tensor_scalar(sc_, cnt[:, :], 1.0, None, ALU.max))
                    link(v.reciprocal(sc_, sc_))
                    v.wait_ge(acd, 1)
                    link(v.reciprocal(nr, nn))
                    link(v.tensor_tensor(nr, nr, q0, ALU.mult))
                    link(v.tensor_tensor(nn, nn, nr, ALU.add))
                    link(v.tensor_scalar(nn, nn, 0.5, None, ALU.mult))
                    link(v.tensor_scalar(nr, nn, EPS_M, float(np.float32(1.0) - np.float32(EPS_M)), ALU.max, ALU.min))
                    link(v.tensor_scalar(q0, nr, -1.0, 1.0, ALU.mult, ALU.add))
                    link(v.reciprocal(q0, q0))
                    link(v.tensor_scalar(q1, nr, 1.0, None, ALU.add))
                    link(v.tensor_tensor(q0, q0, q1, ALU.mult))
                    v.sem_inc(go, 1)
                    link(v.tensor_tensor(q2, nr, nr, ALU.mult))
                    link(v.tensor_scalar(q3, q2, 1.0 / 9, 1.0 / 7, ALU.mult, ALU.add))
                    for c in (1.0 / 5, 1.0 / 3, 1.0):
                        link(v.tensor_tensor(q3, q3, q2, ALU.mult))
                        link(v.tensor_scalar(q3, q3, c, None, ALU.add))
                    link(v.tensor_tensor(q3, q3, nr, ALU.mult))
                    link(v.tensor_scalar(q2, nr, 0.15, None, ALU.is_lt))
                    v.wait_ge(acd, 2)
                    link(v.tensor_scalar(f, f, 0.5, None, ALU.mult))
                    link(v.tensor_tensor(q3, q3, f, ALU.subtract))
                    link(v.tensor_tensor(q3, q3, q2, ALU.mult))
                    link(v.tensor_tensor(f, f, q3, ALU.add))
                    link(v.tensor_tensor(f, f, sc_, ALU.mult))
                    v.sem_inc(go, 1)
                    v.wait_ge(acd, 3)
                    link(v.reciprocal(q0, nr))
                    link(v.tensor_tensor(f, f, q0, ALU.mult))
                    link(v.scalar_tensor_tensor(f, nn, EPS_M, f, ALU.is_gt, ALU.mult))
                    x2 = TABg[:, :, D]
                    link(v.tensor_tensor(xy, xy, f, ALU.mult))
                    link(v.tensor_tensor(n2, n2, f, ALU.mult))
                    link(v.tensor_tensor(n2, n2, f, ALU.mult))
                    link(v.tensor_scalar(q0, xy, 2.0, 1.0, ALU.mult, ALU.add))
                    link(v.tensor_tensor(q1, x2, n2, ALU.mult))
                    link(v.tensor_tensor(q1, q1, q0, ALU.add))
                    link(v.tensor_scalar(q1, q1, EPS_M, None, ALU.max))
                    link(v.reciprocal(q1, q1))
                    link(v.tensor_tensor(q0, q0, n2, ALU.add))
                    link(v.tensor_tensor(q0, q0, q1, ALU.mult))
                    link(v.tensor_scalar(q2, x2, -1.0, 1.0, ALU.mult, ALU.add))
                    link(v.tensor_tensor(q2, q2, f, ALU.mult))
                    link(v.tensor_tensor(q2, q2, q1, ALU.mult))
                    link(v.tensor_tensor(SCRg, hs, spread(q0), ALU.mult))
                    link(v.tensor_tensor(X[:, :], X[:, :], SCR[:, :], ALU.add))
                    link(v.tensor_tensor(SCRg, sums, spread(q2), ALU.mult))
                    link(v.tensor_tensor(X[:, :], X[:, :], SCR[:, :], ALU.add))
                    v.sem_inc(go, 1)

                @block.scalar
                def _(ac):
                    ac.wait_ge(go, 1)
                    ac.activation(nn, q0, ACT.Sqrt).then_inc(acd, 1)
                    ac.wait_ge(go, 2)
                    ac.activation(f, q0, ACT.Ln).then_inc(acd, 1)
                    ac.wait_ge(go, 3)
                    ac.activation(f, f, ACT.Tanh).then_inc(acd, 1)

                @block.sync
                def _(sp):
                    sp.wait_ge(go, 4)
                    sp.dma_start(out.rearrange("(g p) f -> p g f", p=P), Xg).then_inc(sto, 16)
                    sp.wait_ge(sto, 16)
        w.close()


def layout(inputs):
    i = {k: np.asarray(v) for k, v in inputs.items()}
    pad = (C + 1) * P - E
    one = lambda n: np.ascontiguousarray(i[n].reshape(1, -1))
    col = lambda n: np.ascontiguousarray(i[n].reshape(-1, 1))
    dst2d = np.concatenate([i["dst"], np.full(pad, FARAWAY, np.int32)]).reshape(C + 1, P)
    return {
        "x": np.concatenate([i["x"], np.zeros((NP - N, D), np.float32)]),
        "src2d": np.concatenate([i["src"], np.zeros(pad, np.int32)]).reshape(C + 1, P),
        "dst2d": dst2d,
        "dst_last": np.ascontiguousarray(dst2d[:C, P - 1]),
        "ew2d": np.concatenate([i["edge_weight"], np.zeros(pad, np.float32)]).reshape(C + 1, P),
        "attrT": np.ascontiguousarray(np.concatenate([i["edge_attr_50"], np.zeros((pad, NG), np.float32)]).T),
        "w1": i["L0_gnn_mlp_w1"], "b1": col("L0_gnn_mlp_b1"), "w2": i["L0_gnn_mlp_w2"], "b2": one("L0_gnn_mlp_b2"),
        "lin1": i["L0_gnn_lin1_w"], "lin2": i["L0_gnn_lin2_w"], "lin2b": col("L0_gnn_lin2_b"),
        "lin": i["L0_gnn_lin_w"], "linb": one("L0_gnn_lin_b"),
        "wqvks": np.concatenate([i["L1_gnn_Wq"], i["L1_gnn_Wv"], i["L1_gnn_Wk"], i["L1_gnn_Ws"]], 1),
        "bqvks": np.concatenate([i["L1_gnn_bq"], i["L1_gnn_bv"], i["L1_gnn_bk"], i["L1_gnn_bs"]]).reshape(1, -1),
        "wg": i["L1_gnn_Wg"].reshape(1, 3 * D), "bg": i["L1_gnn_bg"].reshape(1, 1),
        "gamma": one("L1_gnn_gamma"), "beta": one("L1_gnn_beta"), "alpha": i["L1_gnn_alpha"].reshape(1, 1),
        "wlr1": np.concatenate([i["L2_gnn_W_l1"].T, i["L2_gnn_W_r1"].T], 1),
        "b21": one("L2_gnn_b1"),
        "wlr2": np.concatenate([i["L2_gnn_W_l2"].T, i["L2_gnn_W_r2"].T], 0),
        "b22": one("L2_gnn_b2"),
    }


STOP = None


def kernel(**inputs):
    import concourse.bacc as _bacc
    from concourse.bass_utils import run_bass_kernel_spmd as _run

    nc = _bacc.Bacc("TRN2", target_bir_lowering=False, num_devices=1)
    arrays = {f"in_{k}": np.ascontiguousarray(v) for k, v in layout(inputs).items()}
    aps = {n[3:]: nc.dram_tensor(n, v.shape, mybir.dt.from_np(v.dtype), kind="ExternalInput").ap() for n, v in arrays.items()}
    out = nc.dram_tensor("out", (NP, D), F32, kind="ExternalOutput").ap()
    build(nc, aps, out, STOP)
    r = _run(nc, [arrays], core_ids=[0])
    return r.results[0]["out"][:N]
```

```python
import numpy as np
import concourse.bass as bass
from concourse import mybir
from contextlib import ExitStack, contextmanager

F32 = mybir.dt.float32
BF16 = mybir.dt.bfloat16
I32 = mybir.dt.int32
ALU = mybir.AluOpType
ACT = mybir.ActivationFunctionType
AX = mybir.AxisListType

P = 128
N = 6250
E = 100000
D = 128
H = 4
DH = D // H
NG = 50
G = -(-N // P)
GB = G + G % 2
NP = GB * P
C = -(-E // P)
U = 8
K = -(-(C + G - 1) // (4 * U)) * 4 * U
IT = K // U
Q = 4
STEPS = K // (4 * Q)
KT7 = -(-K // P)
KP = KT7 * P
MW = 132
FARAWAY = 1 << 20
EPS_LN = 1e-5
EPS_M = 1e-7
BIG = 1e30
LOG2 = float(np.log(2.0))


def build(nc, a, out):
    dram = lambda name, shape, dt=F32: nc.dram_tensor(name, shape, dt, kind="Internal").ap()
    T0 = dram("T0", (NP, D))
    QV = dram("QV", (NP, 2 * D))
    VE = dram("VE", (K, P, D))
    SEQ = dram("SEQ", (H, KP * P))
    KEY = dram("KEY", (P + KP * P,))
    SEX = dram("SEX", (H, K * P))
    Y1 = dram("Y1", (NP, 64))
    H2 = dram("H2", (NP, 64))
    H3 = dram("H3", (NP, MW))
    MSG = dram("MSG", (K * P, MW))

    name_uses = {}

    def unique(name):
        name_uses[name] = name_uses.get(name, 0) + 1
        return name if name_uses[name] == 1 else f"{name}_{name_uses[name]}"

    def tile(name, shape, dt=F32):
        return nc.sbuf_tensor(unique(name), shape, dt)

    with ExitStack() as ctx:
        def sb(name, shape, dt=F32):
            return ctx.enter_context(tile(name, shape, dt))

        X = sb("X", [P, GB * D])
        AGG = sb("AGG", [P, GB * 136])
        TAB = sb("TAB", [P, GB * MW])
        Z = sb("Z", [P, GB * D])
        SCR = sb("SCR", [P, GB * D])
        srci = sb("srci", [P, KP], I32)
        drel = sb("drel", [P, KP])
        dkey = sb("dkey", [P, KP])
        cut = sb("cut", [P, KP])
        A = sb("A", [P, H, KP])
        gidx = sb("gidx", [1, KP], I32)
        cidx = sb("cidx", [1, KP], I32)
        ident = sb("ident", [P, P])
        iota = sb("iota", [P, P])
        ones = sb("ones", [P, P])
        cnt = sb("cnt", [P, GB])
        banks = [ctx.enter_context(nc.psum_tensor(f"bank{i}", [P, 512], F32)) for i in range(8)]

        gat = ctx.enter_context(nc.semaphore("gat"))
        gathered = [ctx.enter_context(nc.semaphore(f"gathered{j}")) for j in range(U)]
        passes = [0]

        def landed(it):
            return it * 16 + (16 + passes[0] * 16 * IT)

        gathered4 = [ctx.enter_context(nc.semaphore(f"gathered4_{j}")) for j in range(4 * Q)]
        passes4 = [0]

        def landed4(it):
            return it * 16 + (16 + passes4[0] * 16 * STEPS)

        @contextmanager
        def phase(names):
            with ExitStack() as st:
                sems = [st.enter_context(nc.semaphore(unique(n))) for n in names.split()]
                with nc.Block() as block:
                    yield block, sems
                nc.gpsimd.sem_clear(range(min(s.num for s in sems), max(s.num for s in sems) + 1))
                nc.all_engine_barrier()

        def scratch():
            return ExitStack()

        with scratch() as st:
            tb = lambda name, shape, dt=F32: st.enter_context(tile(name, shape, dt))
            lasti = tb("lasti", [P, C], I32)
            L = tb("L", [P, C])
            Lj = tb("Lj", [P, C])
            kcol = tb("kcol", [P, KT7])
            ccol = tb("ccol", [P, KT7])
            gcol = tb("gcol", [P, KT7])
            ccoli = tb("ccoli", [P, KT7], I32)
            rs = tb("rs", [P, KT7, P], I32)
            rd = tb("rd", [P, KT7, P], I32)
            re = tb("re", [P, KT7, P])
            rf = tb("rf", [P, 2, KT7, P])
            wide = tb("wide", [P, 2, P])
            half_pi = tb("half_pi", [P, 1])
            with phase("ld pool rowc transposed evac dv sn") as (block, (ld, pool, rowc, transposed, evac, dv, sn)):
                @block.sync
                def _(sp):
                    sp.dma_start(lasti[:, :], a["dst_last"].rearrange("(a n) -> a n", a=1).broadcast_to([P, C])).then_inc(ld, 16)
                    sp.dma_start(X[:, :].rearrange("p (g f) -> p g f", f=D), a["x"].rearrange("(g p) f -> p g f", p=P)).then_inc(ld, 16)

                @block.gpsimd
                def _(po):
                    po.memset(ident[:, :], 0.0).then_inc(pool, 1)
                    po.memset(ones[:, :], 1.0)
                    po.memset(half_pi[:, :], float(np.pi / 2))
                    po.memset(A[:, :, K:KP], 0.0)
                    po.iota(iota[:, :], [[1, P]], base=0, channel_multiplier=0, allow_small_or_imprecise_dtypes=True)
                    po.iota(L[:, :], [[1, C]], base=0, channel_multiplier=0, allow_small_or_imprecise_dtypes=True)
                    po.iota(kcol[:, :], [[P, KT7]], base=0, channel_multiplier=1, allow_small_or_imprecise_dtypes=True)
                    po.wait_ge(pool, 1)
                    po.affine_select(out=ident[:, :], in_=ident[:, :], compare_op=ALU.not_equal, fill=1.0, base=0,
                                     pattern=[[-1, P]], channel_multiplier=1).then_inc(pool, 1)
                    po.wait_ge(rowc, 1)
                    for t in range(KT7):
                        for dst, tab in ((rs, a["src2d"]), (rd, a["dst2d"]), (re, a["ew2d"])):
                            po.indirect_dma_start(out=dst[:, t, :], out_offset=None, in_=tab[:, :],
                                                  in_offset=bass.IndirectOffsetOnAxis(ap=ccoli[:, t:t + 1], axis=0)).then_inc(gat, 16)

                @block.vector
                def _(v):
                    n = [0]

                    def link(ins):
                        n[0] += 1
                        ins.then_inc(dv, 1)
                        v.wait_ge(dv, n[0])

                    v.wait_ge(ld, 32)
                    v.wait_ge(pool, 2)
                    link(v.tensor_scalar(lasti[:, :], lasti[:, :], 7, None, ALU.arith_shift_right))
                    link(v.tensor_scalar(Lj[:, :], lasti[:, :], float(G - 1), None, ALU.min))
                    link(v.tensor_tensor(L[:, :], L[:, :], Lj[:, :], ALU.add))
                    for t in range(KT7):
                        link(v.tensor_scalar(Lj[:, :], L[:, :], kcol[:, t:t + 1], 0.0, ALU.is_lt, ALU.add,
                                             accum_out=ccol[:, t:t + 1]))
                    link(v.tensor_tensor(gcol[:, :], kcol[:, :], ccol[:, :], ALU.subtract))
                    link(v.tensor_scalar(gcol[:, :], gcol[:, :], float(G - 1), None, ALU.min))
                    v.tensor_copy(ccoli[:, :], ccol[:, :]).then_inc(rowc, 1)
                    v.wait_ge(gat, 16 * 3 * KT7)
                    v.tensor_copy(rf[:, 0, :, :], rs[:, :, :])
                    link(v.tensor_copy(rf[:, 1, :, :], rd[:, :, :]))
                    for t in range(KT7):
                        cols = slice(t * P, (t + 1) * P)
                        if t:
                            v.wait_ge(transposed, t)
                        v.tensor_copy(wide[:, 0, :], gcol[:, t:t + 1].broadcast_to([P, P]))
                        link(v.tensor_copy(wide[:, 1, :], ccol[:, t:t + 1].broadcast_to([P, P])))
                        v.sem_inc(rowc, 1)
                        v.wait_ge(transposed, t + 1)
                        bk = banks[0]
                        v.tensor_copy(srci[:, cols], bk[:, 0:P])
                        v.tensor_copy(cut[:, cols], bk[:, 2 * P:3 * P])
                        link(v.tensor_copy(dkey[:, cols], bk[:, P:2 * P]))
                        v.scalar_tensor_tensor(drel[:, cols], banks[1][:, 0:P], -float(P), dkey[:, cols], ALU.mult, ALU.add)
                        v.tensor_copy(gidx[0:1, cols], banks[1][0:1, 0:P])
                        link(v.tensor_copy(cidx[0:1, cols], banks[1][0:1, P:2 * P]))
                        v.sem_inc(evac, 1)
                    w = cut[:, :]
                    s = SCR[:, 0:KP]
                    q = SCR[:, KP:2 * KP]
                    link(v.tensor_scalar(s, w, 10.0, None, ALU.is_le))
                    link(v.scalar_tensor_tensor(q, w, 0.0, s, ALU.is_ge, ALU.mult))
                    link(v.tensor_scalar(w, w, 0.0, 10.0, ALU.max, ALU.min))
                    v.sem_inc(evac, 1)
                    v.wait_ge(sn, 1)
                    link(v.tensor_scalar(w, w, 0.5, 0.5, ALU.mult, ALU.add))
                    link(v.tensor_tensor(w, w, q, ALU.mult))

                @block.tensor
                def _(pe):
                    pe.wait_ge(pool, 2)
                    for t in range(KT7):
                        pe.wait_ge(rowc, t + 2)
                        if t:
                            pe.wait_ge(evac, t)
                        pe.transpose(banks[0][:, 0:P], rf[:, 0, t, :], ident[:, :])
                        pe.transpose(banks[0][:, P:2 * P], rf[:, 1, t, :], ident[:, :])
                        pe.transpose(banks[0][:, 2 * P:3 * P], re[:, t, :], ident[:, :])
                        pe.matmul(banks[1][:, 0:P], wide[:, 0, :], ident[:, :], start=True, stop=True)
                        pe.matmul(banks[1][:, P:2 * P], wide[:, 1, :], ident[:, :], start=True, stop=True).then_inc(transposed, 1)

                @block.scalar
                def _(ac):
                    ac.wait_ge(evac, KT7 + 1)
                    ac.activation(cut[:, :], cut[:, :], ACT.Sin, bias=half_pi[:, :], scale=-float(np.pi / 10)).then_inc(sn, 1)
        weights = {}

        def load_weights(names):
            with phase("ld") as (block, (ld,)):
                @block.sync
                def _(sp):
                    for n in names:
                        sp.dma_start(weights[n][:, :], a[n]).then_inc(ld, 16)
                    sp.wait_ge(ld, 16 * len(names))

        def steps(eng, count, body):
            body(0, True)
            with eng.Fori(1, count) as it:
                body(it, False)

        def pipeline(eng, count, body):
            body(0, True, 2)
            with eng.Fori(1, count - 2) as it:
                body(it, False, 2)
            body(count - 2, False, 1)
            body(count - 1, False, 0)

        def gather_units(po, table, gb, ic, indices_ready, used, depth):
            sems = gathered if depth == 2 else gathered4
            po.tensor_copy(ic[:, 0, :], srci[:, 0:4]).then_inc(indices_ready, 1)

            def body(it, first):
                for n in range(2 * Q):
                    u, q = it * (2 * Q) + n, n % Q
                    if not (first and n < depth):
                        used(it * 2 + n // Q, q)
                    po.tensor_copy(ic[:, (n + 1) % (2 * Q), :], srci[:, bass.ds(u * 4 + 4, 4)]).then_inc(indices_ready, 1)
                    po.wait_ge(indices_ready, u + 1)
                    po.nop(nofuse=True)
                    for j in range(4):
                        po.indirect_dma_start(out=gb[:, q % depth, j, :], out_offset=None, in_=table[:, :],
                                              in_offset=bass.IndirectOffsetOnAxis(ap=ic[:, n, j:j + 1], axis=0)
                                              ).then_inc(sems[4 * (q % depth) + j], 16)
            steps(po, STEPS // 2, body)

        Xg = X[:, :].rearrange("p (g f) -> p g f", f=D)
        SCRg = SCR[:, :].rearrange("p (g f) -> p g f", f=D)
        Zg = Z[:, :].rearrange("p (g f) -> p g f", f=D)
        stats = sb("stats", [P, 4, GB])
        rstd = stats[:, 3, :]

        def rsqrt_chain(link, v, y, var, t):
            link(v.tensor_tensor(t, y, y, ALU.mult))
            link(v.tensor_tensor(t, t, var, ALU.mult))
            link(v.tensor_scalar(t, t, -0.5, 1.5, ALU.mult, ALU.add))
            link(v.tensor_tensor(y, y, t, ALU.mult))

        def normalise(src, squares):
            with phase("cen sq lnexp dv") as (block, (cen, sq, lnexp, dv)):
                @block.vector
                def _(v):
                    n = [0]

                    def link(ins):
                        n[0] += 1
                        ins.then_inc(dv, 1)
                        v.wait_ge(dv, n[0])

                    mean, ssq, tmp, y = (stats[:, j, :] for j in range(4))
                    link(v.tensor_reduce(mean, src, AX.X, ALU.add))
                    link(v.tensor_scalar(mean, mean, 1.0 / D, None, ALU.mult))
                    v.tensor_tensor(SCRg, src, mean.unsqueeze(2).broadcast_to([P, GB, D]), ALU.subtract).then_inc(cen, 1)
                    v.wait_ge(sq, 1)
                    link(v.tensor_reduce(ssq, squares.rearrange("p (g f) -> p g f", f=D), AX.X, ALU.add))
                    v.tensor_scalar(ssq, ssq, 1.0 / D, EPS_LN, ALU.mult, ALU.add).then_inc(cen, 1)
                    v.wait_ge(lnexp, 2)
                    rsqrt_chain(link, v, y, ssq, tmp)
                    rsqrt_chain(link, v, y, ssq, tmp)

                @block.scalar
                def _(ac):
                    ac.preload_act_table_set("natural_log_exp_and_others")
                    ac.wait_ge(cen, 1)
                    ac.activation(squares, SCR[:, :], ACT.Square).then_inc(sq, 1)
                    ac.wait_ge(cen, 2)
                    ac.activation(stats[:, 2, :], stats[:, 1, :], ACT.Ln).then_inc(lnexp, 1)
                    ac.wait_ge(lnexp, 1)
                    ac.activation(stats[:, 3, :], stats[:, 2, :], ACT.Exp, scale=-0.5).then_inc(lnexp, 1)

        def relu_norm_block(v, g, out_tile):
            return v.tensor_scalar(out_tile, SCR[:, bass.ds(g * D, D)], 0.0, stats[:, 3, bass.ds(g, 1)], ALU.max, ALU.mult)

        ones3 = sb("ones3", [3, P], BF16)

        def split_row(row, parts3):
            n = row.shape[1]
            with scratch() as st:
                pt = st.enter_context(tile("pt", [1, 3, n], BF16))
                hi = st.enter_context(tile("hi", [1, n], F32))
                rest = st.enter_context(tile("rest", [1, n], F32))
                with phase("dv parts ld") as (block, (dv, parts, ld)):
                    @block.vector
                    def _(v):
                        m = [0]

                        def link(ins):
                            m[0] += 1
                            ins.then_inc(dv, 1)
                            v.wait_ge(dv, m[0])

                        link(v.tensor_copy(rest[:, :], row))
                        for k in range(3):
                            link(v.tensor_copy(pt[:, k, :], rest[:, :]))
                            link(v.tensor_copy(hi[:, :], pt[:, k, :]))
                            link(v.tensor_tensor(rest[:, :], rest[:, :], hi[:, :], ALU.subtract))
                        v.memset(ones3[:, :], 1.0)
                        v.sem_inc(parts, 1)

                    @block.sync
                    def _(sp):
                        sp.wait_ge(parts, 1)
                        for k in range(3):
                            sp.dma_start(parts3[k:k + 1, :], pt[:, k, :]).then_inc(ld, 16)
                        sp.wait_ge(ld, 48)

        def node_products(fill, W, bias, take, taker, store=None, store_cols=0):
            width = W.shape[1]
            with scratch() as st:
                hb = st.enter_context(tile("hb", [P, 2, P], F32))
                hT = st.enter_context(tile("hT", [P, 2, P], F32))
                ob = st.enter_context(tile("ob", [P, 2, max(store_cols, 1)], F32))
                with phase("filled transposed copied product taken stored0 stored1 self") as (
                        block, (filled, transposed, copied, product, taken, stored0, stored1, own)):
                    stored = (stored0, stored1)

                    def taking(eng, it, b, first):
                        u = it * 2 + b
                        eng.wait_ge(product, u + 1)
                        if store is not None and not first:
                            eng.wait_ge(stored[b], it * 16)
                        take(eng, u, banks[2 + b], ob[:, b, :]).then_inc(taken, 1)

                    @block.vector
                    def _(v):
                        def filling(u, b):
                            fill(v, u, hb[:, b, :]).then_inc(filled, 1)
                        filling(0, 0)
                        filling(1, 1)

                        def body(it, first, ahead):
                            for b in range(2):
                                if ahead > 0:
                                    v.wait_ge(transposed, it * 2 + b + 1)
                                    filling(it * 2 + b + 2, b)
                                if taker == "vector":
                                    taking(v, it, b, first)
                        pipeline(v, GB // 2, body)

                    @block.tensor
                    def _(pe):
                        def transpose(u, b):
                            pe.wait_ge(filled, u + 1)
                            pe.transpose(banks[b][:, 0:P], hb[:, b, :], ident[:, :]).then_inc(transposed, 1)
                        transpose(0, 0)

                        def body(it, first, ahead):
                            for b in range(2):
                                u = it * 2 + b
                                if b == 0 or ahead > 0:
                                    if not (first and b == 0):
                                        pe.wait_ge(copied, u)
                                    transpose(u + 1, 1 - b)
                                pe.wait_ge(copied, u + 1)
                                if not first:
                                    pe.wait_ge(taken, u - 1)
                                ps = banks[2 + b][:, 0:width]
                                if bias is not None:
                                    spread_row = ones3 if bias.shape[0] == 3 else ones[0:1, :]
                                    pe.matmul(ps, spread_row[:, :], bias[:, :], start=True, stop=False)
                                pe.matmul(ps, hT[:, b, :], W[:, :], start=bias is None, stop=True).then_inc(product, 1)
                        pipeline(pe, GB // 2, body)

                    @block.scalar
                    def _(ac):
                        def copying(u, b):
                            ac.wait_ge(transposed, u + 1)
                            ac.activation(hT[:, b, :], banks[b][:, 0:P], ACT.Copy).then_inc(copied, 1)
                        copying(0, 0)

                        def body(it, first, ahead):
                            for b in range(2):
                                u = it * 2 + b
                                if b == 0 or ahead > 0:
                                    if not (first and b == 0):
                                        ac.wait_ge(product, u)
                                    copying(u + 1, 1 - b)
                                if taker == "scalar":
                                    taking(ac, it, b, first)
                        pipeline(ac, GB // 2, body)

                    if store is not None:
                        @block.sync
                        def _(sp):
                            def body(it, first):
                                for b in range(2):
                                    sp.wait_ge(taken, it * 2 + b + 1)
                                    sp.dma_start(store[bass.ds((it * 2 + b) * P, P), :], ob[:, b, :]).then_inc(stored[b], 16)
                            steps(sp, GB // 2, body)
                            for b in range(2):
                                sp.wait_ge(stored[b], 16 * (GB // 2))

        w = scratch()
        tbw = lambda name, shape: w.enter_context(tile(f"w_{name}", shape, F32))
        for n, shape in (("lin1", [D, D]), ("w1", [NG, D]), ("b1", [D, 1]), ("w2", [D, D]), ("b2", [1, D]), ("b2w", [1, 512])):
            weights[n] = tbw(n, shape)
        b1m = tbw("b1m", [D, 1])
        load_weights(["lin1", "w1", "b1", "w2", "b2"])
        normalise(Xg, TAB[:, 0:GB * D])
        with phase("colsum") as (block, (colsum,)):
            @block.tensor
            def _(pe):
                pe.matmul(banks[0][0:1, 0:D], ones[:, 0:1], weights["w2"][:, :], start=True, stop=True).then_inc(colsum, 1)

            @block.vector
            def _(v):
                v.tensor_scalar(b1m[:, :], weights["b1"][:, :], -30.0, None, ALU.add)
                v.wait_ge(colsum, 1)
                for j in range(4):
                    v.scalar_tensor_tensor(weights["b2w"][:, j * D:(j + 1) * D], banks[0][0:1, 0:D], -LOG2, weights["b2"][:, :], ALU.mult, ALU.add)

        b2parts = w.enter_context(tile("b2parts", [3, 512], BF16))
        split_row(weights["b2w"][:, :], b2parts)
        node_products(lambda v, g, t: relu_norm_block(v, g, t), weights["lin1"], None,
                      lambda e, g, ps, t: e.activation(t, ps[:, 0:D], ACT.Copy), "scalar", T0, D)

        AGGT = AGG[:, 0:GB * P]
        with scratch() as st:
            tb = lambda name, shape, dt=F32: st.enter_context(tile(name, shape, dt))
            gb = tb("gb", [P, 2, 4, D])
            ab = tb("ab", [NG, U, P])
            ic = tb("ic", [P, 2 * Q, 4], I32)
            dc = tb("dc", [P, 2, U])
            xm = tb("xm", [P, 2, 512])
            rx = tb("rx", [P, 2, 512])
            ms = tb("ms", [P, 2, 4, D])
            oh = tb("oh", [P, 2, 4, P])
            with phase("at0 at1 at2 at3 at4 at5 at6 at7 indices_ready product1 clamped act_done softplus_ready product2 terms_ready summed columns_ready accumulated") as (block, S):
                got, att = gathered, S[0:8]
                indices_ready, product1, clamped, act_done, softplus_ready, product2, terms_ready, summed, columns_ready, accumulated = S[8:]

                @block.gpsimd
                def _(po):
                    gather_units(po, T0, gb, ic, indices_ready, lambda it, q: po.wait_ge(terms_ready, it * (4 * Q) + (4 * q - 4)), 2)

                @block.sync
                def _(sp):
                    regs = [sp.register(unique(f"chunk{j}")) for j in range(U)]
                    regs = [st.enter_context(r) for r in regs]

                    def body(it, first):
                        sp.load(regs, cidx[0:1, bass.ds(it * U, U)])
                        for j in range(U):
                            if not first and j % 4 == 0:
                                sp.wait_ge(product1, (it - 1) * 2 + j // 4 + 1)
                            c = sp.snap(regs[j], min_val=0, max_val=C)
                            sp.dma_start(ab[:, j, :], a["attrT"][:, bass.ds(c * P, P)]).then_inc(att[j], 16)
                    steps(sp, IT, body)

                @block.tensor
                def _(pe):
                    def filter1(it, h):
                        for j in range(4):
                            pe.wait_ge(att[4 * h + j], it * 16 + 16)
                        pe.matmul(banks[h][:, :], weights["w1"][:, :], ab[:, 4 * h:4 * h + 4, :].rearrange("p j e -> p (j e)"),
                                  start=True, stop=True).then_inc(product1, 1)

                    def filter2(it, h):
                        pe.wait_ge(softplus_ready, it * 2 + h + 1)
                        pe.matmul(banks[2 + h][:, 0:512], ones3[:, :], b2parts[:, :], start=True, stop=False)
                        for j in range(4):
                            last = pe.matmul(banks[2 + h][:, j * P:(j + 1) * P], rx[:, h, j * P:(j + 1) * P], weights["w2"][:, :],
                                             start=False, stop=(j == 3))
                        last.then_inc(product2, 1)

                    def body(it, first, ahead):
                        for h in range(2):
                            u = it * 2 + h
                            if h == 0 or ahead > 0:
                                filter2(it + h, 1 - h)
                            if ahead > h:
                                filter1(it + 1 + h, 1 - h)
                            for j in range(4):
                                if not first and j % 2 == 0:
                                    pe.wait_ge(accumulated, u * 4 + (2 * (j // 2) - 5))
                                pe.wait_ge(terms_ready, u * 4 + j + 1)
                                pe.matmul(banks[4 + 2 * h + j // 2][:, (j % 2) * P:(j % 2 + 1) * P], ms[:, h, j, :], oh[:, h, j, :],
                                          start=True, stop=True).then_inc(summed, 1)

                    filter1(0, 0)
                    filter1(0, 1)
                    filter2(0, 0)
                    filter1(1, 0)
                    pipeline(pe, IT, body)

                @block.scalar
                def _(ac):
                    def body(it, first):
                        for h in range(2):
                            hh = it * 2 + h
                            ac.wait_ge(clamped, hh + 1)
                            ac.activation(xm[:, h, :], xm[:, h, :], ACT.Exp).then_inc(act_done, 1)
                            if not first:
                                ac.wait_ge(product2, hh - 1)
                            ac.activation(rx[:, h, :], banks[h][:, 0:512], ACT.Relu, bias=b1m[:, :]).then_inc(act_done, 1)
                            ac.wait_ge(act_done, hh * 3 + 1)
                            ac.activation(xm[:, h, :], xm[:, h, :], ACT.Ln, bias=1.0).then_inc(act_done, 1)
                    steps(ac, IT, body)

                @block.vector
                def _(v):
                    regs = [st.enter_context(v.register(unique(f"blk{j}"))) for j in range(U)]
                    v.memset(AGGT, 0.0).then_inc(accumulated, 1)

                    def clamp(it, h):
                        v.wait_ge(product1, it * 2 + h + 1)
                        v.tensor_scalar(xm[:, h, :], banks[h][:, 0:512], weights["b1"][:, :], 30.0, ALU.add, ALU.min).then_inc(clamped, 1)

                    def softplus(it, h):
                        v.wait_ge(act_done, (it * 2 + h) * 3 + 3)
                        v.tensor_tensor(rx[:, h, :], rx[:, h, :], xm[:, h, :], ALU.add).then_inc(softplus_ready, 1)

                    def add_sum(u, h, j, block_reg):
                        g = v.snap(block_reg, min_val=0, max_val=G - 1)
                        if j % 2 == 0:
                            v.wait_ge(summed, u * 4 + (j + 2))
                        v.wait_ge(accumulated, u * 4 + (j + 1))
                        acc = AGG[:, bass.ds(g * P, P)]
                        v.tensor_tensor(acc, acc, banks[4 + 2 * h + j // 2][:, (j % 2) * P:(j % 2 + 1) * P], ALU.add).then_inc(accumulated, 1)

                    def body(it, first, ahead):
                        if not first:
                            v.wait_ge(terms_ready, it * U)
                        v.tensor_copy(dc[:, 0, :], drel[:, bass.ds(it * U, U)])
                        v.tensor_copy(dc[:, 1, :], cut[:, bass.ds(it * U, U)]).then_inc(columns_ready, 1)
                        for h in range(2):
                            u = it * 2 + h
                            adds = not (first and h == 0)
                            if ahead > 0:
                                clamp(it + 1, h)
                            if h == 0 or ahead > 0:
                                softplus(it + h, 1 - h)
                            if h == 0:
                                if first:
                                    v.load(regs[4:], gidx[0:1, 0:U - 4])
                                else:
                                    v.load(regs, gidx[0:1, bass.ds(it * U - 4, U)])
                                v.wait_ge(columns_ready, it + 1)
                            v.wait_ge(product2, u + 1)
                            for j in range(4):
                                v.wait_ge(got[4 * h + j], landed(it))
                                v.scalar_tensor_tensor(ms[:, h, j, :], banks[2 + h][:, j * P:(j + 1) * P], dc[:, 1, 4 * h + j:4 * h + j + 1],
                                                       gb[:, h, j, :], ALU.mult, ALU.mult)
                                v.tensor_scalar(oh[:, h, j, :], iota[:, :], dc[:, 0, 4 * h + j:4 * h + j + 1], None, ALU.is_equal).then_inc(terms_ready, 1)
                                if adds:
                                    add_sum(u - 1, 1 - h, j, regs[4 * h + j])
                    clamp(0, 0)
                    clamp(0, 1)
                    softplus(0, 0)
                    pipeline(v, IT, body)
                    v.load(regs[:4], gidx[0:1, IT * U - 4:IT * U])
                    for j in range(4):
                        add_sum(IT * 2 - 1, 1, j, regs[j])
        passes[0] += 1
        w.close()
        w = scratch()
        for n, shape in (("lin2", [D, D]), ("lin2b", [D, 1]), ("lin", [D, D]), ("linb", [1, D])):
            weights[n] = tbw(n, shape)
        lin2bm = tbw("lin2bm", [D, 1])
        load_weights(["lin2", "lin2b", "lin", "linb"])
        with phase("colsum") as (block, (colsum,)):
            @block.tensor
            def _(pe):
                pe.matmul(banks[0][0:1, 0:D], ones[:, 0:1], weights["lin"][:, :], start=True, stop=True).then_inc(colsum, 1)

            @block.vector
            def _(v):
                v.tensor_scalar(lin2bm[:, :], weights["lin2b"][:, :], -30.0, None, ALU.add)
                v.wait_ge(colsum, 1)
                v.scalar_tensor_tensor(weights["linb"][:, :], banks[0][0:1, 0:D], -LOG2, weights["linb"][:, :], ALU.mult, ALU.add)
        with scratch() as st:
            xm = st.enter_context(tile("xm", [P, 2, P], F32))
            rx = st.enter_context(tile("rx", [P, 2, P], F32))
            with phase("product1 clamped act_done softplus_ready product2 added") as (block, (product1, clamped, act_done, softplus_ready, product2, added)):
                @block.tensor
                def _(pe):
                    def body(it, first):
                        for b in range(2):
                            g = it * 2 + b
                            if not first:
                                pe.wait_ge(clamped, g - 1)
                                pe.wait_ge(act_done, (g - 2) * 3 + 3)
                            pe.matmul(banks[b][:, 0:P], weights["lin2"][:, :], AGG[:, bass.ds(g * P, P)], start=True, stop=True).then_inc(product1, 1)
                        for b in range(2):
                            g = it * 2 + b
                            pe.wait_ge(softplus_ready, g + 1)
                            if not first:
                                pe.wait_ge(added, g - 1)
                            pe.matmul(banks[2 + b][:, 0:D], ones[0:1, :], weights["linb"][0:1, :], start=True, stop=False)
                            pe.matmul(banks[2 + b][:, 0:D], rx[:, b, :], weights["lin"][:, :], start=False, stop=True).then_inc(product2, 1)
                    steps(pe, GB // 2, body)

                @block.scalar
                def _(ac):
                    def body(it, first):
                        for b in range(2):
                            g = it * 2 + b
                            ac.wait_ge(clamped, g + 1)
                            ac.activation(xm[:, b, :], xm[:, b, :], ACT.Exp).then_inc(act_done, 1)
                            if not first:
                                ac.wait_ge(product2, g - 1)
                            ac.activation(rx[:, b, :], banks[b][:, 0:P], ACT.Relu, bias=lin2bm[:, :]).then_inc(act_done, 1)
                            ac.wait_ge(act_done, g * 3 + 1)
                            ac.activation(xm[:, b, :], xm[:, b, :], ACT.Ln, bias=1.0).then_inc(act_done, 1)
                    steps(ac, GB // 2, body)

                @block.vector
                def _(v):
                    def body(it, first):
                        for b in range(2):
                            g = it * 2 + b
                            v.wait_ge(product1, g + 1)
                            if not first:
                                v.wait_ge(softplus_ready, g - 1)
                            v.tensor_scalar(xm[:, b, :], banks[b][:, 0:P], weights["lin2b"][:, :], 30.0, ALU.add, ALU.min).then_inc(clamped, 1)
                        for b in range(2):
                            g = it * 2 + b
                            v.wait_ge(act_done, g * 3 + 3)
                            v.tensor_tensor(rx[:, b, :], rx[:, b, :], xm[:, b, :], ALU.add).then_inc(softplus_ready, 1)
                        for b in range(2):
                            g = it * 2 + b
                            v.wait_ge(product2, g + 1)
                            xb = X[:, bass.ds(g * D, D)]
                            v.tensor_tensor(xb, xb, banks[2 + b][:, 0:D], ALU.add).then_inc(added, 1)
                    steps(v, GB // 2, body)
        w.close()
        normalise(Xg, TAB[:, 0:GB * D])

        w = scratch()
        for n, shape in (("wqvks", [D, 4 * D]), ("bqvks", [1, 4 * D])):
            weights[n] = tbw(n, shape)
        load_weights(["wqvks", "bqvks"])
        bparts = w.enter_context(tile("bparts", [3, 4 * D], BF16))
        split_row(weights["bqvks"][:, :], bparts)

        def take_qvks(e, g, ps, t):
            e.activation(TAB[:, bass.ds(g * MW, D)], ps[:, 2 * D:3 * D], ACT.Copy)
            e.activation(Z[:, bass.ds(g * D, D)], ps[:, 3 * D:4 * D], ACT.Copy)
            return e.activation(t, ps[:, 0:2 * D], ACT.Copy)

        node_products(relu_norm_block, weights["wqvks"], bparts, take_qvks, "scalar", QV, 2 * D)
        w.close()

        with scratch() as st:
            tb = lambda name, shape, dt=F32: st.enter_context(tile(name, shape, dt))
            gb = tb("gb", [P, Q, 4, 2 * D])
            ic = tb("ic", [P, 2 * Q, 4], I32)
            dc = tb("dc", [P, U])
            oh = tb("oh", [P, 2, 4, P])
            ot = tb("ot", [P, 2, 4, P])
            pr = tb("pr", [P, 2, 4, D])
            with phase("vs0 vs1 vs2 vs3 indices_ready onehots_ready transposed turned_ready k_ready products_ready own") as (block, S):
                got, vst = gathered4, S[0:4]
                indices_ready, onehots_ready, transposed, turned_ready, k_ready, products_ready, own = S[4:]

                @block.gpsimd
                def _(po):
                    def used(it, q):
                        po.wait_ge(products_ready, it * Q + (q - 3))
                        po.wait_ge(vst[q], it * 16)
                    gather_units(po, QV, gb, ic, indices_ready, used, Q)

                @block.sync
                def _(sp):
                    def body(it, first):
                        for q in range(Q):
                            for j in range(4):
                                sp.wait_ge(got[4 * q + j], landed4(it))
                            sp.dma_start(VE[bass.ds(it * (4 * Q) + 4 * q, 4), :, :].rearrange("k p f -> p k f"),
                                         gb[:, q, :, D:2 * D]).then_inc(vst[q], 16)
                    steps(sp, STEPS, body)
                    for q in range(Q):
                        sp.wait_ge(vst[q], 16 * STEPS)

                @block.vector
                def _(v):
                    def body(it, first):
                        for pair in range(2):
                            first = first and pair == 0
                            i = it * 2 + pair
                            if not first:
                                v.wait_ge(onehots_ready, i * 2)
                            v.tensor_copy(dc[:, :], drel[:, bass.ds(i * U, U)]).then_inc(own, 1)
                            v.wait_ge(own, i + 1)
                            for h in range(2):
                                if not first:
                                    v.wait_ge(transposed, i * 2 + h - 1)
                                for j in range(4):
                                    last = v.tensor_scalar(oh[:, h, j, :], iota[:, :], dc[:, 4 * h + j:4 * h + j + 1], None, ALU.is_equal)
                                last.then_inc(onehots_ready, 1)
                            for h in range(2):
                                q = 2 * pair + h
                                for j in range(4):
                                    v.wait_ge(got[4 * q + j], landed4(it))
                                v.wait_ge(k_ready, i * 2 + h + 1)
                                v.tensor_tensor(pr[:, h, :, :], gb[:, q, :, 0:D],
                                                banks[2 + h][:, :].rearrange("p (j f) -> p j f", j=4), ALU.mult).then_inc(products_ready, 1)
                                v.wait_ge(products_ready, i * 2 + h + 1)
                                v.tensor_reduce(A[:, :, bass.ds((i * 2 + h) * 4, 4)].rearrange("p h j -> p j h"),
                                                pr[:, h, :, :].rearrange("p j (h f) -> p j h f", h=H), AX.X, ALU.add)
                    steps(v, STEPS, body)

                @block.tensor
                def _(pe):
                    regs = [st.enter_context(pe.register(unique(f"pblk{j}"))) for j in range(U)]

                    def body(it, first):
                        pe.load(regs, gidx[0:1, bass.ds(it * U, U)])
                        for h in range(2):
                            hh = it * 2 + h
                            pe.wait_ge(onehots_ready, hh + 1)
                            if not first:
                                pe.wait_ge(turned_ready, hh - 1)
                            for j in range(4):
                                last = pe.transpose(banks[h][:, j * P:(j + 1) * P], oh[:, h, j, :], ident[:, :])
                            last.then_inc(transposed, 1)
                        for h in range(2):
                            hh = it * 2 + h
                            pe.wait_ge(turned_ready, hh + 1)
                            if not first:
                                pe.wait_ge(products_ready, hh - 1)
                            for j in range(4):
                                g = pe.snap(regs[4 * h + j], min_val=0, max_val=G - 1)
                                last = pe.matmul(banks[2 + h][:, j * D:(j + 1) * D], ot[:, h, j, :], TAB[:, bass.ds(g * MW, D)], start=True, stop=True)
                            last.then_inc(k_ready, 1)
                    steps(pe, IT, body)

                @block.scalar
                def _(ac):
                    def body(it, first):
                        for h in range(2):
                            hh = it * 2 + h
                            ac.wait_ge(transposed, hh + 1)
                            if not first:
                                ac.wait_ge(k_ready, hh - 1)
                            ac.activation(ot[:, h, :, :].rearrange("p j n -> p (j n)"), banks[h][:, :], ACT.Copy).then_inc(turned_ready, 1)
                    steps(ac, IT, body)

        passes4[0] += 1

        LL = K * P // 32
        KC, FW = AGG[:, 0:LL], AGG[:, LL:2 * LL]
        BW, SC = SCR[:, 0:LL], TAB[:, 0:LL]
        with scratch() as st:
            tb = lambda name, shape, dt=F32: st.enter_context(tile(name, shape, dt))
            stage = TAB[:, 0:5 * KP].rearrange("p (t j e) -> p t j e", t=KT7, j=5)
            keyi = SCR[:, 0:KP]
            val = SCR[:, KP:2 * KP]
            pad = tb("pad", [1, P])
            cols = tb("cols", [P, 2])
            rows = tb("rows", [1, 4, P])
            cin = tb("cin", [P, 1])
            with phase("dv ready transposed ev st") as (block, (dv, ready, transposed, ev, sto)):
                @block.vector
                def _(v):
                    n = [0]

                    def link(ins):
                        n[0] += 1
                        ins.then_inc(dv, 1)
                        v.wait_ge(dv, n[0])

                    v.memset(pad[:, :], -2.0)
                    link(v.tensor_scalar(val, drel[:, :], 0.0, None, ALU.is_ge))
                    link(v.scalar_tensor_tensor(val, drel[:, :], float(P - 1), val, ALU.is_le, ALU.mult))
                    link(v.scalar_tensor_tensor(keyi, dkey[:, :], 1.0, val, ALU.add, ALU.mult))
                    link(v.tensor_scalar(keyi, keyi, -1.0, None, ALU.add))
                    v.sem_inc(ready, 1)
                    for t in range(KT7):
                        v.wait_ge(transposed, t + 1)
                        v.tensor_copy(stage[:, t, 0:4, :], banks[2 * (t % 2)][:, :].rearrange("p (j e) -> p j e", j=4))
                        v.tensor_copy(stage[:, t, 4, :], banks[2 * (t % 2) + 1][:, 0:P]).then_inc(ev, 1)

                @block.tensor
                def _(pe):
                    pe.wait_ge(ready, 1)
                    for t in range(KT7):
                        if t >= 2:
                            pe.wait_ge(ev, t - 1)
                        for h in range(H):
                            pe.transpose(banks[2 * (t % 2)][:, h * P:(h + 1) * P], A[:, h, t * P:(t + 1) * P], ident[:, :])
                        pe.transpose(banks[2 * (t % 2) + 1][:, 0:P], keyi[:, t * P:(t + 1) * P], ident[:, :]).then_inc(transposed, 1)

                @block.sync
                def _(sp):
                    sp.wait_ge(ready, 1)
                    sp.dma_start(KEY[0:P].rearrange("(a n) -> a n", a=1), pad[:, :]).then_inc(sto, 16)
                    for t in range(KT7):
                        sp.wait_ge(ev, t + 1)
                        sp.dma_start(SEQ[:, t * P * P:(t + 1) * P * P].rearrange("h (k e) -> k h e", e=P), stage[:, t, 0:4, :]).then_inc(sto, 16)
                        sp.dma_start(KEY[P + t * P * P:P + (t + 1) * P * P].rearrange("(k e) -> k e", e=P), stage[:, t, 4, :]).then_inc(sto, 16)
                    sp.wait_ge(sto, 16 * (2 * KT7 + 1))

            with phase("ld dv pe back ex sto") as (block, (ld, dv, pes, back, exd, sto)):
                @block.sync
                def _(sp):
                    for h in range(H):
                        part = slice(32 * h, 32 * h + 32)
                        sp.dma_start(SC[part, :], SEQ[h, 0:K * P].rearrange("(l j) -> l j", j=LL)).then_inc(ld, 16)
                        for dst, off in ((KC, 0), (FW, -1), (BW, 1)):
                            sp.dma_start(dst[part, :], KEY[P + off:P + off + K * P].rearrange("(l j) -> l j", j=LL)).then_inc(ld, 16)
                    sp.wait_ge(exd, 1)
                    sp.dma_start(SEX.rearrange("h (l j) -> (h l) j", j=LL), KC).then_inc(sto, 16)
                    sp.wait_ge(sto, 16)

                @block.vector
                def _(v):
                    n = [0]

                    def link(ins):
                        n[0] += 1
                        ins.then_inc(dv, 1)
                        v.wait_ge(dv, n[0])

                    def carries(i, last, flags, back_to_front):
                        v.tensor_copy(cols[:, 0:1], last)
                        link(v.tensor_reduce(cols[:, 1:2], flags, AX.X, ALU.add))
                        v.sem_inc(back, 1)
                        v.wait_ge(pes, 2 * i + 1)
                        v.memset(rows[:, 3, :], -BIG)
                        link(v.tensor_copy(rows[:, 0:2, :], banks[0][0:1, 0:2 * P].rearrange("p (j n) -> p j n", j=2)))
                        if back_to_front:
                            link(v.tensor_tensor_scan(rows[:, 2, ::-1], rows[:, 1, ::-1], rows[:, 0, ::-1], -BIG, ALU.add, ALU.max))
                            link(v.tensor_copy(rows[:, 3, 0:P - 1], rows[:, 2, 1:P]))
                        else:
                            link(v.tensor_tensor_scan(rows[:, 2, :], rows[:, 1, :], rows[:, 0, :], -BIG, ALU.add, ALU.max))
                            link(v.tensor_copy(rows[:, 3, 1:P], rows[:, 2, 0:P - 1]))
                        v.sem_inc(back, 1)
                        v.wait_ge(pes, 2 * i + 2)
                        link(v.tensor_copy(cin[:, :], banks[1][:, 0:1]))

                    v.wait_ge(ld, 16 * 16)
                    link(v.tensor_tensor(FW, FW, KC, ALU.not_equal))
                    link(v.tensor_tensor(BW, BW, KC, ALU.not_equal))
                    link(v.tensor_scalar(FW, FW, -BIG, None, ALU.mult))
                    link(v.tensor_scalar(BW, BW, -BIG, None, ALU.mult))
                    link(v.tensor_tensor_scan(KC, FW, SC, -BIG, ALU.add, ALU.max))
                    carries(0, KC[:, LL - 1:LL], FW, False)
                    link(v.tensor_tensor_scan(KC, FW, SC, cin[:, :], ALU.add, ALU.max))
                    link(v.tensor_tensor_scan(FW[:, ::-1], BW[:, ::-1], KC[:, ::-1], -BIG, ALU.add, ALU.max))
                    carries(1, FW[:, 0:1], BW, True)
                    link(v.tensor_tensor_scan(FW[:, ::-1], BW[:, ::-1], KC[:, ::-1], cin[:, :], ALU.add, ALU.max))
                    link(v.tensor_tensor(SC, SC, FW, ALU.subtract))
                    v.sem_inc(back, 1)

                @block.tensor
                def _(pe):
                    for i in range(2):
                        pe.wait_ge(back, 2 * i + 1)
                        pe.matmul(banks[0][0:1, 0:P], cols[:, 0:1], ident[:, :], start=True, stop=True)
                        pe.matmul(banks[0][0:1, P:2 * P], cols[:, 1:2], ident[:, :], start=True, stop=True).then_inc(pes, 1)
                        pe.wait_ge(back, 2 * i + 2)
                        pe.matmul(banks[1][:, 0:1], rows[0:1, 3, :], ones[0:1, 0:1], start=True, stop=True).then_inc(pes, 1)

                @block.scalar
                def _(ac):
                    ac.wait_ge(back, 5)
                    ac.activation(KC, SC, ACT.Exp, scale=float(DH) ** -0.5).then_inc(exd, 1)

            xs = TAB[:, 0:4 * KP].rearrange("p (t h e) -> p t h e", t=KT7, h=H)
            with phase("ld transposed ev") as (block, (ld, transposed, ev)):
                tiles = [(t, min(P, K - t * P)) for t in range(KT7)]

                @block.sync
                def _(sp):
                    for t, m in tiles:
                        sp.dma_start(xs[0:m, t, :, :], SEX[:, t * P * P:(t * P + m) * P].rearrange("h (k e) -> k h e", e=P)).then_inc(ld, 16)

                @block.tensor
                def _(pe):
                    pe.wait_ge(ld, 16 * KT7)
                    for t, m in tiles:
                        if t >= 2:
                            pe.wait_ge(ev, t - 1)
                        for h in range(H):
                            last = pe.transpose(banks[t % 2][:, h * P:h * P + m], xs[0:m, t, h, :], ident[0:m, 0:m])
                        last.then_inc(transposed, 1)

                @block.vector
                def _(v):
                    for t, m in tiles:
                        v.wait_ge(transposed, t + 1)
                        v.tensor_copy(A[:, :, t * P:t * P + m],
                                      banks[t % 2][:, :].rearrange("p (h k) -> p h k", h=H)[:, :, 0:m]).then_inc(ev, 1)

        AGGg = AGG[:, :].rearrange("p (g f) -> p g f", f=136)

        def edge_sum(width, table):
            with scratch() as st:
                tb = lambda name, shape, dt=F32: st.enter_context(tile(name, shape, dt))
                gb = tb("gb", [P, 2, 4, width])
                ic = tb("ic", [P, 2 * Q, 4], I32)
                dc = tb("dc", [P, U])
                oh = tb("oh", [P, 2, 4, P])
                with phase("indices_ready onehots_ready summed own") as (block, (indices_ready, onehots_ready, summed, own)):
                    got = gathered

                    @block.gpsimd
                    def _(po):
                        gather_units(po, table, gb, ic, indices_ready, lambda it, q: po.wait_ge(summed, it * (4 * Q) + (4 * q - 4)), 2)

                    @block.vector
                    def _(v):
                        regs = [st.enter_context(v.register(unique(f"eblk{j}"))) for j in range(U)]
                        v.memset(AGG[:, :], 0.0).then_inc(own, 1)
                        per = U + 1

                        def body(it, first):
                            v.load(regs, gidx[0:1, bass.ds(it * U, U)])
                            v.wait_ge(own, it * per + 1)
                            v.tensor_copy(dc[:, :], drel[:, bass.ds(it * U, U)]).then_inc(own, 1)
                            v.wait_ge(own, it * per + 2)
                            for h in range(2):
                                hh = it * 2 + h
                                if not first:
                                    v.wait_ge(summed, (hh - 2) * 4 + 4)
                                for j in range(4):
                                    last = v.tensor_scalar(oh[:, h, j, :], iota[:, :], dc[:, 4 * h + j:4 * h + j + 1], None, ALU.is_equal)
                                last.then_inc(onehots_ready, 1)
                            for h in range(2):
                                for j in range(4):
                                    k = (it * 2 + h) * 4 + j
                                    g = v.snap(regs[4 * h + j], min_val=0, max_val=G - 1)
                                    v.wait_ge(summed, k + 1)
                                    if h or j:
                                        v.wait_ge(own, it * per + 2 + 4 * h + j)
                                    acc = AGG[:, bass.ds(g * 136, width)]
                                    v.tensor_tensor(acc, acc, banks[4 * h + j][:, 0:width], ALU.add).then_inc(own, 1)
                        steps(v, IT, body)

                    @block.tensor
                    def _(pe):
                        def body(it, first):
                            for h in range(2):
                                pe.wait_ge(onehots_ready, it * 2 + h + 1)
                                for j in range(4):
                                    k = (it * 2 + h) * 4 + j
                                    if not first:
                                        pe.wait_ge(own, (it - 1) * (U + 1) + 3 + 4 * h + j)
                                    pe.wait_ge(got[4 * h + j], landed(it))
                                    pe.matmul(banks[4 * h + j][:, 0:width], oh[:, h, j, :], gb[:, h, j, :], start=True, stop=True).then_inc(summed, 1)
                        steps(pe, IT, body)

            passes[0] += 1

        def attention_sum():
            W1 = D + H + 1
            with scratch() as st:
                tb = lambda name, shape, dt=F32: st.enter_context(tile(name, shape, dt))
                gb = tb("gb", [P, Q, 4, D])
                dc = tb("dc", [P, Q, 4])
                ms = tb("ms", [P, 2, 4, 136])
                oh = tb("oh", [P, Q, 4, P])
                with phase("ld0 ld1 ld2 ld3 columns_ready onehots_ready exps_ready terms_ready summed accumulated") as (block, S):
                    loaded = S[0:4]
                    columns_ready, onehots_ready, exps_ready, terms_ready, summed, accumulated = S[4:]

                    @block.sync
                    def _(sp):
                        def body(it, first):
                            for q in range(Q):
                                if not first:
                                    sp.wait_ge(terms_ready, it * (4 * Q) + (4 * q - 12))
                                sp.dma_start(gb[:, q, :, :], VE[bass.ds(it * (4 * Q) + 4 * q, 4), :, :].rearrange("k p f -> p k f")).then_inc(loaded[q], 16)
                        steps(sp, STEPS, body)

                    @block.gpsimd
                    def _(po):
                        def body(it, first):
                            for q in range(Q):
                                if not first:
                                    po.wait_ge(summed, it * (4 * Q) + (4 * q - 12))
                                po.tensor_copy(dc[:, q, :], drel[:, bass.ds(it * (4 * Q) + 4 * q, 4)]).then_inc(columns_ready, 1)
                                po.wait_ge(columns_ready, it * Q + (q + 1))
                                po.nop(nofuse=True)
                                for j in range(3):
                                    last = po.tensor_scalar(oh[:, q, j, :], iota[:, :], dc[:, q, j:j + 1], None, ALU.is_equal)
                                last.then_inc(onehots_ready, 1)
                        steps(po, STEPS, body)

                    @block.vector
                    def _(v):
                        regs = [st.enter_context(v.register(unique(f"ablk{j}"))) for j in range(4 * Q)]
                        v.memset(ms[:, :, :, W1 - 1:W1], 1.0)
                        v.memset(AGG[:, :], 0.0).then_inc(accumulated, 1)

                        def add_sum(u, h, j, block_reg):
                            g = v.snap(block_reg, min_val=0, max_val=G - 1)
                            if j % 2 == 0:
                                v.wait_ge(summed, u * 4 + (j + 2))
                            v.wait_ge(accumulated, u * 4 + (j + 1))
                            acc = AGG[:, bass.ds(g * 136, W1)]
                            v.tensor_tensor(acc, acc, banks[4 * h + j][:, 0:W1], ALU.add).then_inc(accumulated, 1)

                        def body(it, first):
                            for q in range(Q):
                                u = it * Q + q
                                h = q % 2
                                adds = not (first and q == 0)
                                if not (first and q < 2):
                                    v.wait_ge(summed, u * 4 - 4)
                                v.tensor_copy(ms[:, h, :, D:D + H], A[:, :, bass.ds(u * 4, 4)].rearrange("p h j -> p j h")).then_inc(exps_ready, 1)
                                v.wait_ge(columns_ready, u + 1)
                                v.tensor_scalar(oh[:, q, 3, :], iota[:, :], dc[:, q, 3:4], None, ALU.is_equal)
                                if q == 0:
                                    if first:
                                        v.load(regs[4:], gidx[0:1, 0:4 * Q - 4])
                                    else:
                                        v.load(regs, gidx[0:1, bass.ds(it * (4 * Q) - 4, 4 * Q)])
                                v.wait_ge(exps_ready, u + 1)
                                v.wait_ge(loaded[q], it * 16 + 16)
                                for j in range(4):
                                    v.tensor_tensor(ms[:, h, j, 0:D].rearrange("p (h f) -> p h f", h=H), gb[:, q, j, :].rearrange("p (h f) -> p h f", h=H),
                                                    ms[:, h, j, D:D + H].unsqueeze(2).broadcast_to([P, H, DH]), ALU.mult).then_inc(terms_ready, 1)
                                    if adds:
                                        add_sum(u - 1, 1 - h, j, regs[4 * q + j])
                        steps(v, STEPS, body)
                        v.load(regs[:4], gidx[0:1, K - 4:K])
                        for j in range(4):
                            add_sum(K // 4 - 1, 1, j, regs[j])

                    @block.tensor
                    def _(pe):
                        def body(it, first):
                            for q in range(Q):
                                u = it * Q + q
                                h = q % 2
                                pe.wait_ge(onehots_ready, u + 1)
                                for j in range(4):
                                    pe.wait_ge(terms_ready, u * 4 + (j + 1))
                                    if not (first and q < 2):
                                        pe.wait_ge(accumulated, u * 4 + (j - 6))
                                    pe.matmul(banks[4 * h + j][:, 0:W1], oh[:, q, j, :], ms[:, h, j, 0:W1], start=True, stop=True).then_inc(summed, 1)
                        steps(pe, STEPS, body)

        attention_sum()

        w = scratch()
        row = lambda n, width: tbw(n, [P, width])
        wgb, gab, beb, bgb, alb = row("wgb", 3 * D), row("gab", D), row("beb", D), row("bgb", 1), row("alb", 1)
        rden = tbw("rden", [P, GB, H])
        with phase("ld dv sg sgr sq lx") as (block, (ld, dv, sg, sgr, sq, lx)):
            @block.sync
            def _(sp):
                for dst, n in ((wgb, "wg"), (gab, "gamma"), (beb, "beta"), (bgb, "bg"), (alb, "alpha")):
                    sp.dma_start(dst[:, :], a[n].broadcast_to([P, dst.shape[1]])).then_inc(ld, 16)

            @block.vector
            def _(v):
                n = [0]

                def link(ins):
                    n[0] += 1
                    ins.then_inc(dv, 1)
                    v.wait_ge(dv, n[0])

                spread = lambda col: col.unsqueeze(2).broadcast_to([P, GB, D])
                along = lambda r: r.unsqueeze(1).broadcast_to([P, GB, D])
                agg = AGGg[:, :, 0:D]
                v.wait_ge(ld, 16 * 5)
                den = AGGg[:, :, D:D + H]
                v.tensor_copy(cnt[:, :], AGG[:, D + H::136])
                link(v.scalar_tensor_tensor(rden[:, :, :], den, 0.0, den, ALU.is_le, ALU.add))
                link(v.reciprocal(rden[:, :, :], rden[:, :, :]))
                for h in range(H):
                    link(v.tensor_tensor(agg[:, :, h * DH:(h + 1) * DH], agg[:, :, h * DH:(h + 1) * DH],
                                         rden[:, :, h:h + 1].broadcast_to([P, GB, DH]), ALU.mult))
                link(v.tensor_tensor(wgb[:, 0:D], wgb[:, 0:D], wgb[:, 2 * D:3 * D], ALU.add))
                link(v.tensor_tensor(wgb[:, D:2 * D], wgb[:, D:2 * D], wgb[:, 2 * D:3 * D], ALU.subtract))
                z0, z1, gate = (stats[:, j, :] for j in range(3))
                link(v.tensor_tensor(SCRg, Zg, along(wgb[:, 0:D]), ALU.mult))
                link(v.tensor_reduce(z0, SCRg, AX.X, ALU.add))
                link(v.tensor_tensor(SCRg, agg, along(wgb[:, D:2 * D]), ALU.mult))
                link(v.tensor_reduce(z1, SCRg, AX.X, ALU.add))
                link(v.scalar_tensor_tensor(z0, z0, bgb[:, 0:1], z1, ALU.add, ALU.add))
                link(v.tensor_scalar(z0, z0, -80.0, None, ALU.max))
                v.sem_inc(sg, 1)
                v.tensor_tensor(SCRg, Zg, agg, ALU.subtract)
                v.wait_ge(sgr, 1)
                link(v.tensor_scalar(gate, gate, 1.0, None, ALU.add))
                link(v.reciprocal(gate, gate))
                link(v.tensor_tensor(SCRg, SCRg, spread(gate), ALU.mult))
                link(v.tensor_tensor(SCRg, SCRg, agg, ALU.add))
                mean, ssq, tmp, y = (stats[:, j, :] for j in range(4))
                link(v.tensor_reduce(mean, SCRg, AX.X, ALU.add))
                link(v.tensor_scalar(mean, mean, 1.0 / D, None, ALU.mult))
                link(v.tensor_tensor(SCRg, SCRg, spread(mean), ALU.subtract))
                v.sem_inc(sg, 1)
                v.wait_ge(sq, 1)
                link(v.tensor_reduce(ssq, Zg, AX.X, ALU.add))
                link(v.tensor_scalar(ssq, ssq, 1.0 / D, EPS_LN, ALU.mult, ALU.add))
                v.sem_inc(sg, 1)
                v.wait_ge(lx, 2)
                rsqrt_chain(link, v, y, ssq, tmp)
                rsqrt_chain(link, v, y, ssq, tmp)
                link(v.tensor_tensor(SCRg, SCRg, spread(y), ALU.mult))
                link(v.tensor_tensor(SCRg, SCRg, along(gab[:, :]), ALU.mult))
                link(v.tensor_tensor(SCRg, SCRg, along(beb[:, :]), ALU.add))
                link(v.tensor_scalar(Z[:, :], SCR[:, :], 0.0, alb[:, 0:1], ALU.min, ALU.mult))
                link(v.scalar_tensor_tensor(SCR[:, :], SCR[:, :], 0.0, Z[:, :], ALU.max, ALU.add))
                link(v.tensor_tensor(X[:, :], X[:, :], SCR[:, :], ALU.add))

            @block.scalar
            def _(ac):
                ac.wait_ge(sg, 1)
                ac.activation(stats[:, 2, :], stats[:, 0, :], ACT.Exp, scale=-1.0).then_inc(sgr, 1)
                ac.wait_ge(sg, 2)
                ac.activation(Z[:, :], SCR[:, :], ACT.Square).then_inc(sq, 1)
                ac.wait_ge(sg, 3)
                ac.activation(stats[:, 2, :], stats[:, 1, :], ACT.Ln).then_inc(lx, 1)
                ac.wait_ge(lx, 1)
                ac.activation(stats[:, 3, :], stats[:, 2, :], ACT.Exp, scale=-0.5).then_inc(lx, 1)
        w.close()

        normalise(Xg, TAB[:, 0:GB * D])
        w = scratch()
        weights["wlr1"], weights["b21w"], weights["wlr2"], weights["b22"] = (
            tbw("wlr1", [D, D]), tbw("b21w", [1, D]), tbw("wlr2", [D, D]), tbw("b22", [1, D]))
        rdeg = tbw("rdeg", [P, GB])
        with phase("ld z") as (block, (ld, z)):
            @block.vector
            def _(v):
                v.memset(weights["b21w"][:, 0:64], 0.0).then_inc(z, 1)

            @block.sync
            def _(sp):
                sp.dma_start(weights["b21w"][:, 64:128], a["b21"]).then_inc(ld, 16)
                for n in ("wlr1", "wlr2", "b22"):
                    sp.dma_start(weights[n][:, :], a[n]).then_inc(ld, 16)
                sp.wait_ge(ld, 64)

        def take_yz(e, g, ps, t):
            e.activation(Z[:, bass.ds(g * D, 64)], ps[:, 64:128], ACT.Copy)
            return e.activation(t, ps[:, 0:64], ACT.Copy)

        node_products(relu_norm_block, weights["wlr1"], weights["b21w"], take_yz, "scalar", Y1, 64)
        edge_sum(64, Y1)
        with phase("dv r st") as (block, (dv, r, sto)):
            @block.vector
            def _(v):
                n = [0]

                def link(ins):
                    n[0] += 1
                    ins.then_inc(dv, 1)
                    v.wait_ge(dv, n[0])

                zz = Zg[:, :, 64:128]
                link(v.tensor_scalar(rdeg[:, :], cnt[:, :], 1.0, None, ALU.max))
                link(v.reciprocal(rdeg[:, :], rdeg[:, :]))
                link(v.tensor_tensor(zz, AGGg[:, :, 0:64], rdeg[:, :].unsqueeze(2).broadcast_to([P, GB, 64]), ALU.mult))
                link(v.tensor_tensor(zz, zz, Zg[:, :, 0:64], ALU.add))
                link(v.tensor_scalar(zz, zz, 0.0, None, ALU.max))
                v.sem_inc(r, 1)

            @block.sync
            def _(sp):
                sp.wait_ge(r, 1)
                sp.dma_start(H2.rearrange("(g p) f -> p g f", p=P), Zg[:, :, 64:128]).then_inc(sto, 16)
                sp.wait_ge(sto, 16)
        edge_sum(64, H2)
        with phase("dv") as (block, (dv,)):
            @block.vector
            def _(v):
                v.tensor_tensor(Zg[:, :, 0:64], AGGg[:, :, 0:64], rdeg[:, :].unsqueeze(2).broadcast_to([P, GB, 64]), ALU.mult)

        def add_x(e, g, ps, t):
            xb = X[:, bass.ds(g * D, D)]
            return e.tensor_tensor(xb, xb, ps[:, 0:D], ALU.add)

        node_products(lambda v, g, t: v.tensor_copy(t, Z[:, bass.ds(g * D, D)]), weights["wlr2"], weights["b22"], add_x, "vector")
        w.close()
        normalise(Xg, TAB[:, 0:GB * D])
        TABg = TAB[:, :].rearrange("p (g f) -> p g f", f=MW)
        with phase("dv h sq st") as (block, (dv, hr, sq, sto)):
            @block.vector
            def _(v):
                v.memset(TABg[:, :, D:MW], 0.0).then_inc(dv, 1)
                v.scalar_tensor_tensor(TABg[:, :, 0:D], SCRg, 0.0, rstd.unsqueeze(2).broadcast_to([P, GB, D]), ALU.max, ALU.mult).then_inc(hr, 1)
                v.wait_ge(sq, 1)
                v.wait_ge(dv, 1)
                v.tensor_reduce(TABg[:, :, D], SCRg, AX.X, ALU.add).then_inc(hr, 1)

            @block.scalar
            def _(ac):
                ac.wait_ge(hr, 1)
                ac.activation(SCRg, TABg[:, :, 0:D], ACT.Square).then_inc(sq, 1)

            @block.sync
            def _(sp):
                sp.wait_ge(hr, 2)
                sp.dma_start(H3.rearrange("(g p) f -> p g f", p=P), TABg).then_inc(sto, 16)
                sp.wait_ge(sto, 16)

        with scratch() as st:
            tb = lambda name, shape, dt=F32: st.enter_context(tile(name, shape, dt))
            gb = tb("gb", [P, Q, 4, MW])
            ic = tb("ic", [P, 2 * Q, 4], I32)
            dc = tb("dc", [P, Q, 4])
            oh = tb("oh", [P, 2, 4, P])
            ot = tb("ot", [P, 2, 4, P])
            junk = tb("junk", [P, 4, D])
            junk2 = tb("junk2", [P, 4, D])
            sc = tb("sc", [P, Q, 7, 4])
            tm = tb("tm", [P, 2, 4, D])
            mr = tb("mr", [P, Q, 4, MW])
            got = gathered4

            def units(unit):
                every = 10 * Q

                def run(it, q, lo, hi):
                    unit(it, q, lambda d: lo <= q + d < hi)

                def whole(eng):
                    for q in range(1, Q):
                        run(-1, q, Q, every)
                    for q in range(Q):
                        run(0, q, 0, every)
                    with eng.Fori(1, STEPS - 1) as it:
                        for q in range(Q):
                            run(it, q, -every, every)
                    for q in range(Q):
                        run(STEPS - 1, q, -every, Q)
                    for q in range(2):
                        run(STEPS, q, -every, 0)
                return whole

            with phase("ms0 ms1 ms2 ms3 indices_ready columns_ready onehots_ready transposed turned_ready hdst_ready factors_ready scaled_ready messages_ready norms_ready rows_ready own") as (block, S):
                mst = S[0:4]
                indices_ready, columns_ready, onehots_ready, transposed, turned_ready, hdst_ready, factors_ready, scaled_ready, messages_ready, norms_ready, rows_ready, own = S[4:]

                @block.gpsimd
                def _(po):
                    gather_units(po, H3, gb, ic, indices_ready, lambda it, q: po.wait_ge(messages_ready, it * (4 * Q) + (4 * q - 12)), Q)

                @block.vector
                def _(v):
                    LINKS = 7

                    def unit(it, q, ok):
                        u = it * Q + q
                        h = q % 2

                        def one_hot():
                            if ok(0):
                                v.wait_ge(transposed, u + 1)
                            v.wait_ge(columns_ready, u + 3)
                            for j in range(4):
                                last = v.tensor_scalar(oh[:, h, j, :], iota[:, :], dc[:, (q + 2) % Q, j:j + 1], None, ALU.is_equal)
                            last.then_inc(onehots_ready, 1)

                        def columns():
                            if ok(-1):
                                v.wait_ge(onehots_ready, u)
                            v.tensor_copy(dc[:, (q + 3) % Q, :], drel[:, bass.ds(u * 4 + 12, 4)]).then_inc(columns_ready, 1)

                        n = [0]

                        def link(ins):
                            n[0] += 1
                            ins.then_inc(own, 1)
                            return n[0]

                        def linked(m):
                            v.wait_ge(own, u * LINKS + m)

                        def message(j):
                            if ok(-1):
                                if j == 0:
                                    if ok(-1 - Q):
                                        v.wait_ge(mst[(q - 1) % Q], (it + (q - 1) // Q) * 16)
                                    v.wait_ge(own, u * LINKS)
                                v.wait_ge(scaled_ready, u * 4 + (j - 3))
                                v.scalar_tensor_tensor(mr[:, (q - 1) % Q, j, 0:D], gb[:, (q - 1) % Q, j, 0:D], sc[:, (q - 1) % Q, 4, j:j + 1],
                                                       tm[:, 1 - h, j, :], ALU.mult, ALU.subtract).then_inc(messages_ready, 1)

                        def norms():
                            if ok(-2):
                                v.wait_ge(norms_ready, u * 4 - 4)
                                y2 = sc[:, (q - 2) % Q, 6, :]
                                for k, f in enumerate((-0.5, 0.5, 1.0, -1.0)):
                                    last = v.tensor_scalar(mr[:, (q - 2) % Q, :, D + k], y2, f, None, ALU.mult)
                                last.then_inc(rows_ready, 1)

                        if ok(2):
                            one_hot()
                        if ok(3):
                            columns()
                        if not ok(0):
                            for j in range(4):
                                message(j)
                            norms()
                            return
                        sd, d2, p1, den, ca, cb = (sc[:, q, k, :] for k in range(6))
                        s2 = gb[:, q, :, D]
                        for j in range(4):
                            v.wait_ge(got[4 * q + j], landed4(it))
                            if j % 2 == 0:
                                v.wait_ge(hdst_ready, u * 2 + (j // 2 + 1))
                                v.tensor_copy(d2[:, j:j + 2], banks[2 + 2 * h + j // 2][:, 0:258].rearrange("p (j c) -> p j c", j=2)[:, :, D])
                            hd = banks[2 + 2 * h + j // 2][:, (j % 2) * 129:(j % 2) * 129 + D]
                            last = v.tensor_tensor_reduce(junk[:, j, :], gb[:, q, j, 0:D], hd, 1.0, 0.0, ALU.mult, ALU.add, sd[:, j:j + 1])
                        dots = link(last)
                        message(0)
                        linked(dots)
                        one = link(v.tensor_scalar(p1, sd, -2.0, 1.0, ALU.mult, ALU.add))
                        v.tensor_scalar(cb, s2, -1.0, 1.0, ALU.mult, ALU.add)
                        prod = link(v.tensor_tensor(den, s2, d2, ALU.mult))
                        message(1)
                        linked(prod)
                        v.tensor_tensor(ca, p1, d2, ALU.add)
                        ds_ = link(v.tensor_tensor(den, den, p1, ALU.add))
                        message(2)
                        linked(ds_)
                        mx = link(v.tensor_scalar(den, den, EPS_M, None, ALU.max))
                        message(3)
                        linked(mx)
                        rc = link(v.reciprocal(den, den))
                        norms()
                        linked(rc)
                        v.tensor_tensor(cb, cb, den, ALU.mult).then_inc(factors_ready, 1)
                        link(v.tensor_tensor(ca, ca, den, ALU.mult))
                        assert n[0] == LINKS
                    units(unit)(v)

                @block.tensor
                def _(pe):
                    regs = [st.enter_context(pe.register(unique(f"pblk{j}"))) for j in range(4)]

                    def unit(it, q, ok):
                        u = it * Q + q
                        h = q % 2
                        if ok(1):
                            pe.load(regs, gidx[0:1, bass.ds(u * 4 + 4, 4)])
                        if ok(2):
                            pe.wait_ge(onehots_ready, u + 3)
                            if ok(0):
                                pe.wait_ge(turned_ready, u + 1)
                            for j in range(4):
                                last = pe.transpose(banks[h][:, j * P:(j + 1) * P], oh[:, h, j, :], ident[:, :])
                            last.then_inc(transposed, 1)
                        if ok(1):
                            pe.wait_ge(turned_ready, u + 2)
                            if ok(-1):
                                pe.wait_ge(scaled_ready, u * 4)
                            for j in range(4):
                                g = pe.snap(regs[j], min_val=0, max_val=G - 1)
                                o = (j % 2) * 129
                                last = pe.matmul(banks[2 + 2 * (1 - h) + j // 2][:, o:o + 129], ot[:, 1 - h, j, :], TAB[:, bass.ds(g * MW, 129)],
                                                 start=True, stop=True)
                                if j % 2:
                                    last.then_inc(hdst_ready, 1)
                    units(unit)(pe)

                @block.scalar
                def _(ac):
                    def unit(it, q, ok):
                        u = it * Q + q
                        h = q % 2
                        if ok(2):
                            ac.wait_ge(transposed, u + 3)
                            if ok(0):
                                ac.wait_ge(hdst_ready, u * 2 + 2)
                            ac.activation(ot[:, h, :, :].rearrange("p j n -> p (j n)"), banks[h][:, :], ACT.Copy).then_inc(turned_ready, 1)
                        if ok(-1):
                            for j in range(4):
                                ac.wait_ge(messages_ready, u * 4 + (j - 3))
                                ac.activation(junk2[:, j, :], mr[:, (q - 1) % Q, j, 0:D], ACT.Square,
                                              accum_out=sc[:, (q - 1) % Q, 6, j:j + 1]).then_inc(norms_ready, 1)
                        if ok(0):
                            ac.wait_ge(factors_ready, u + 1)
                            for j in range(4):
                                hd = banks[2 + 2 * h + j // 2][:, (j % 2) * 129:(j % 2) * 129 + D]
                                ac.activation(tm[:, h, j, :], hd, ACT.Copy, scale=sc[:, q, 5, j:j + 1]).then_inc(scaled_ready, 1)
                    units(unit)(ac)

                @block.sync
                def _(sp):
                    rows = MSG.rearrange("(k p) c -> k p c", p=P)

                    def body(it, first):
                        for q in range(Q):
                            sp.wait_ge(rows_ready, it * Q + (q + 1))
                            sp.dma_start(rows[bass.ds(it * (4 * Q) + 4 * q, 4), :, :].rearrange("k p c -> p k c"), mr[:, q, :, :]).then_inc(mst[q], 16)
                    steps(sp, STEPS, body)
                    for q in range(Q):
                        sp.wait_ge(mst[q], 16 * STEPS)

        w = scratch()
        WR = 2
        wfirst, woff, weff = tbw("wfirst", [P, GB]), tbw("woff", [P, GB]), tbw("weff", [P, GB])
        tcount = tbw("tcount", [1, GB + 2])
        tcounti = w.enter_context(tile("tcounti", [1, GB + 2], I32))
        with scratch() as st:
            tb = lambda name, shape, dt=F32: st.enter_context(tile(name, shape, dt))
            before = tb("before", [P, P])
            gpos = tb("gpos", [P, GB])
            tot, pos, nw, fr = tb("tot", [P, GB]), tb("pos", [P, GB]), tb("nw", [P, GB]), tb("fr", [P, GB])
            ii = tb("ii", [P, GB], I32)
            mx = tb("mx", [GB, 1])
            with phase("pr pe1 dv nwr pe2 mxr pe3") as (block, (pr, pe1, dv, nwr, pe2, mxr, pe3)):
                @block.gpsimd
                def _(po):
                    po.memset(before[:, :], 1.0).then_inc(pr, 1)
                    po.iota(gpos[:, :], [[P, GB]], base=0, channel_multiplier=0, allow_small_or_imprecise_dtypes=True)
                    po.wait_ge(pr, 1)
                    po.affine_select(out=before[:, :], in_=before[:, :], compare_op=ALU.is_gt, fill=0.0, base=0,
                                     pattern=[[1, P]], channel_multiplier=-1).then_inc(pr, 1)

                @block.tensor
                def _(pe):
                    pe.wait_ge(pr, 2)
                    pe.matmul(banks[0][:, 0:GB], before[:, :], cnt[:, :], start=True, stop=True)
                    pe.matmul(banks[0][:, GB:2 * GB], ones[:, :], cnt[:, :], start=True, stop=True).then_inc(pe1, 1)
                    pe.wait_ge(nwr, 1)
                    pe.transpose(banks[1][0:GB, 0:P], nw[:, :], ident[:, :]).then_inc(pe2, 1)
                    pe.wait_ge(mxr, 1)
                    pe.matmul(banks[2][0:1, 0:GB], mx[:, :], ident[0:GB, 0:GB], start=True, stop=True).then_inc(pe3, 1)

                @block.vector
                def _(v):
                    n = [0]

                    def link(ins):
                        n[0] += 1
                        ins.then_inc(dv, 1)
                        v.wait_ge(dv, n[0])

                    v.wait_ge(pr, 2)
                    v.wait_ge(pe1, 1)
                    link(v.tensor_copy(tot[:, :], banks[0][:, GB:2 * GB]))
                    link(v.memset(fr[:, :], 0.0))
                    link(v.tensor_tensor_scan(nw[:, :], tot[:, :], fr[:, :], 0.0, ALU.add, ALU.add))
                    link(v.tensor_tensor(pos[:, :], nw[:, :], tot[:, :], ALU.subtract))
                    link(v.tensor_tensor(pos[:, :], pos[:, :], banks[0][:, 0:GB], ALU.add))
                    link(v.tensor_tensor(pos[:, :], pos[:, :], gpos[:, :], ALU.add))
                    link(v.tensor_copy(ii[:, :], pos[:, :]))
                    link(v.tensor_scalar(ii[:, :], ii[:, :], 1, None, ALU.arith_shift_right))
                    link(v.tensor_copy(wfirst[:, :], ii[:, :]))
                    link(v.scalar_tensor_tensor(woff[:, :], wfirst[:, :], -float(WR), pos[:, :], ALU.mult, ALU.add))
                    link(v.tensor_tensor(weff[:, :], woff[:, :], cnt[:, :], ALU.add))
                    link(v.tensor_scalar(nw[:, :], weff[:, :], float(2 * WR - 1), None, ALU.add))
                    link(v.tensor_copy(ii[:, :], nw[:, :]))
                    link(v.tensor_scalar(ii[:, :], ii[:, :], 2, None, ALU.arith_shift_right))
                    link(v.tensor_copy(nw[:, :], ii[:, :]))
                    link(v.scalar_tensor_tensor(nw[:, :], cnt[:, :], 0.0, nw[:, :], ALU.is_gt, ALU.mult))
                    v.sem_inc(nwr, 1)
                    v.wait_ge(pe2, 1)
                    link(v.tensor_reduce(mx[:, :], banks[1][0:GB, 0:P], AX.X, ALU.max))
                    v.sem_inc(mxr, 1)
                    v.wait_ge(pe3, 1)
                    link(v.tensor_scalar(tcount[:, 0:GB], banks[2][0:1, 0:GB], 1.0, None, ALU.max))
                    link(v.tensor_reduce(tcount[:, GB:GB + 1], tcount[:, 1:GB], AX.X, ALU.add))
                    link(v.tensor_tensor(tcount[:, GB + 1:GB + 2], tcount[:, 0:1], tcount[:, GB:GB + 1], ALU.subtract))
                    link(v.tensor_scalar(tcount[:, GB + 1:GB + 2], tcount[:, GB + 1:GB + 2], 1.0, None, ALU.max))
                    v.tensor_copy(tcounti[:, :], tcount[:, :])

        LAST = K * P // WR - 1
        MAXT = E // (2 * WR) + 2 * GB
        with scratch() as st:
            tb = lambda name, shape, dt=F32: st.enter_context(tile(name, shape, dt))
            S2 = tb("S2", [P, 2, MW])
            mw = tb("mw", [P, 2, 2, WR, MW])
            mk = tb("mk", [P, 2, 2, WR, MW])
            wrow = tb("wrow", [P, 2, 2 * WR])
            wlen = tb("wlen", [P, 2])
            widx = tb("widx", [P, 2])
            wi = tb("wi", [P, 2, 2], I32)
            m0 = tb("m0", [P, 2, 2 * WR])
            msk = tb("msk", [P, 2, 2 * WR])
            woff1 = tb("woff1", [P, 1])
            jrow = tb("jrow", [P, 2 * WR])
            jk = tb("jk", [P, 2, 130])
            wv = tb("wv", [P, 2, D])
            den, rdn, be = tb("den", [P, 2]), tb("rdn", [P, 2]), tb("be", [P, 2])
            wgat = [[st.enter_context(nc.semaphore(unique(f"wgat{b}{s}"))) for s in range(2)] for b in range(2)]
            windows = MSG.rearrange("(w r) c -> w (r c)", r=WR)

            def turns(eng, begin_block, turn):
                done = st.enter_context(eng.register(unique("done")))
                left = st.enter_context(eng.register(unique("left")))
                eng.reg_mov(done, 0)

                def one(g):
                    turn(g, eng.snap(done, min_val=0, max_val=MAXT))
                    eng.reg_add(done, done, 1)

                with eng.Fori(1, GB) as g:
                    begin_block(g, eng.snap(done, min_val=0, max_val=MAXT))
                    eng.load(left, tcounti[0:1, bass.ds(g, 1)])
                    with eng.Fori(0, eng.snap(left, min_val=1, max_val=MAXT)) as _:
                        one(g)
                eng.load(left, tcounti[0:1, GB + 1:GB + 2])
                with eng.Fori(0, eng.snap(left, min_val=1, max_val=MAXT)) as _:
                    one(GB - 1)
                return eng.snap(done, min_val=2, max_val=MAXT)

            OPS = 10
            DT = 2 * WR * OPS
            with phase("pool_done masks_ready masked begun own") as (block, (pool_done, masks_ready, masked, begun, own)):
                @block.gpsimd
                def _(po):
                    PT, PB, P0 = 7, 4, 4
                    po.sem_inc(masks_ready, 1)
                    po.iota(jrow[:, :], [[1, 2 * WR]], base=0, channel_multiplier=0, allow_small_or_imprecise_dtypes=True).then_inc(pool_done, 1)
                    po.wait_ge(pool_done, 1)
                    po.tensor_copy(widx[:, 0:1], wfirst[:, 0:1]).then_inc(pool_done, 1)
                    po.tensor_copy(wlen[:, 0:1], cnt[:, 0:1]).then_inc(pool_done, 1)
                    po.tensor_scalar(wrow[:, 0, :], jrow[:, :], woff[:, 0:1], None, ALU.subtract).then_inc(pool_done, 1)

                    def begin_block(g, t):
                        po.wait_ge(pool_done, t * PT + (g * PB + (P0 - PB)))
                        po.tensor_copy(widx[:, 1:2], wfirst[:, bass.ds(g, 1)]).then_inc(pool_done, 1)
                        po.tensor_copy(wlen[:, 1:2], cnt[:, bass.ds(g, 1)]).then_inc(pool_done, 1)
                        po.tensor_copy(woff1[:, :], woff[:, bass.ds(g, 1)]).then_inc(pool_done, 1)
                        po.wait_ge(pool_done, t * PT + (g * PB + (P0 - PB + 3)))
                        po.nop(nofuse=True)
                        po.tensor_scalar(wrow[:, 1, :], jrow[:, :], woff1[:, :], None, ALU.subtract).then_inc(pool_done, 1)

                    def turn(g, t):
                        n = [0]

                        def do(ins):
                            n[0] += 1
                            ins.then_inc(pool_done, 1)

                        def done():
                            po.wait_ge(pool_done, t * PT + (g * PB + (P0 + n[0])))
                            po.nop(nofuse=True)

                        def gather(b):
                            for s in range(2):
                                po.indirect_dma_start(out=mw[:, b, s, :, :].rearrange("p r c -> p (r c)"), out_offset=None, in_=windows[:, :],
                                                      in_offset=bass.IndirectOffsetOnAxis(ap=wi[:, b, s:s + 1], axis=0)).then_inc(wgat[b][s], 16)

                        done()
                        po.wait_ge(masked, t * 2 + 1)
                        po.nop(nofuse=True)
                        do(po.tensor_scalar(wi[:, 0, :], widx[:, :], float(LAST), None, ALU.min))
                        done()
                        gather(0)
                        po.wait_ge(masks_ready, t + 1)
                        po.wait_ge(masked, t * 2 + 2)
                        po.nop(nofuse=True)
                        do(po.tensor_tensor(m0[:, :, :], wlen[:, :].unsqueeze(2).broadcast_to([P, 2, 2 * WR]), wrow[:, :, :], ALU.subtract))
                        do(po.tensor_scalar(msk[:, :, :], wrow[:, :, :], 0.0, None, ALU.is_ge))
                        do(po.tensor_scalar(wi[:, 1, :], widx[:, :], 1.0, float(LAST), ALU.add, ALU.min))
                        done()
                        do(po.tensor_scalar(m0[:, :, :], m0[:, :, :], 0.0, None, ALU.is_gt))
                        do(po.tensor_scalar(widx[:, :], widx[:, :], 2.0, None, ALU.add))
                        do(po.tensor_scalar(wrow[:, :, :], wrow[:, :, :], 2.0 * WR, None, ALU.add))
                        done()
                        po.tensor_tensor(msk[:, :, :], msk[:, :, :], m0[:, :, :], ALU.mult).then_inc(masks_ready, 1)
                        assert n[0] == PT
                        gather(1)
                    turns(po, begin_block, turn)

                @block.scalar
                def _(ac):
                    ac.sem_inc(masked, 2)

                    def turn(g, t):
                        ac.wait_ge(masks_ready, t + 2)
                        for b in range(2):
                            ac.wait_ge(own, t * DT + (b + 1) * DT // 2)
                            for s in range(2):
                                ac.wait_ge(wgat[b][s], t * 16 + 16)
                                for r in range(WR):
                                    last = ac.activation(mk[:, b, s, r, :], mw[:, b, s, r, :], ACT.Copy, scale=msk[:, s, WR * b + r:WR * b + r + 1])
                            last.then_inc(masked, 1)
                    turns(ac, lambda g, t: None, turn)

                @block.vector
                def _(v):
                    v.sem_inc(own, DT)
                    v.memset(S2[:, :, 0:D], 0.0).then_inc(begun, 1)
                    v.memset(S2[:, :, D:D + 2], 1.0).then_inc(begun, 1)

                    def begin_block(g, t):
                        v.wait_ge(own, t * DT + DT)
                        v.wait_ge(begun, g * 3 - 1)
                        v.tensor_copy(AGG[:, bass.ds(g * 136 - 136, D)], S2[:, 1, 0:D]).then_inc(begun, 1)
                        v.wait_ge(begun, g * 3)
                        v.memset(S2[:, 1, 0:D], 0.0).then_inc(begun, 1)
                        v.memset(S2[:, 1, D:D + 2], 1.0).then_inc(begun, 1)

                    def turn(g, t):
                        n = [0]

                        def done(m):
                            v.wait_ge(own, t * DT + (DT + m))

                        def do(ins):
                            n[0] += 1
                            ins.then_inc(own, 1)
                            return n[0]

                        d_done = sum_done = 0
                        v.wait_ge(begun, g * 3 + 2)
                        for b in range(2):
                            v.wait_ge(masked, t * 2 + (b + 3))
                            for r in range(WR):
                                M = mk[:, b, :, r, :]
                                done(d_done)
                                do(v.tensor_tensor_reduce(jk[:, 0, :], S2[:, 0, 0:130], M[:, 0, 0:130], 2.0, 1.0, ALU.mult, ALU.add, den[:, 0:1]))
                                done(sum_done)
                                dots = do(v.tensor_tensor_reduce(jk[:, 1, :], S2[:, 1, 0:130], M[:, 1, 0:130], 2.0, 1.0, ALU.mult, ALU.add, den[:, 1:2]))
                                do(v.scalar_tensor_tensor(wv[:, 0, :], S2[:, 0, 0:D], M[:, 0, D + 2:D + 3], M[:, 0, 0:D], ALU.mult, ALU.add))
                                done(dots)
                                clipped = do(v.tensor_scalar(den[:, :], den[:, :], EPS_M, None, ALU.max))
                                do(v.scalar_tensor_tensor(wv[:, 1, :], S2[:, 1, 0:D], M[:, 1, D + 2:D + 3], M[:, 1, 0:D], ALU.mult, ALU.add))
                                done(clipped)
                                done(do(v.reciprocal(rdn[:, :], den[:, :])))
                                done(do(v.tensor_tensor(be[:, :], S2[:, :, D], rdn[:, :], ALU.mult)))
                                do(v.scalar_tensor_tensor(S2[:, 0, 0:D], wv[:, 0, :], be[:, 0:1], S2[:, 0, 0:D], ALU.mult, ALU.add))
                                d_done = do(v.scalar_tensor_tensor(S2[:, :, D], M[:, :, D + 3], 1.0, be[:, :], ALU.add, ALU.mult))
                                sum_done = do(v.scalar_tensor_tensor(S2[:, 1, 0:D], wv[:, 1, :], be[:, 1:2], S2[:, 1, 0:D], ALU.mult, ALU.add))
                        assert n[0] == DT
                    all_turns = turns(v, begin_block, turn)
                    v.wait_ge(own, all_turns * DT + DT)
                    v.tensor_copy(AGG[:, (GB - 1) * 136:(GB - 1) * 136 + D], S2[:, 1, 0:D])
                    v.tensor_copy(AGG[:, 0:D], S2[:, 0, 0:D])

        with scratch() as st:
            tb = lambda name, shape, dt=F32: st.enter_context(tile(name, shape, dt))
            small = tb("small", [P, 10, GB])
            with phase("dv go acd st") as (block, (dv, go, acd, sto)):
                n2, nn, nr, q0, q1, sc_, xy, q2, q3, f = (small[:, j, :] for j in range(10))
                sums = AGGg[:, :, 0:D]
                hs = TABg[:, :, 0:D]
                spread = lambda col: col.unsqueeze(2).broadcast_to([P, GB, D])

                @block.vector
                def _(v):
                    n = [0]

                    def link(ins):
                        n[0] += 1
                        ins.then_inc(dv, 1)
                        v.wait_ge(dv, n[0])

                    link(v.tensor_tensor(SCRg, sums, sums, ALU.mult))
                    link(v.tensor_reduce(n2, SCRg, AX.X, ALU.add))
                    link(v.tensor_scalar(q0, n2, 1e-30, None, ALU.max))
                    v.sem_inc(go, 1)
                    link(v.tensor_tensor(SCRg, sums, hs, ALU.mult))
                    link(v.tensor_reduce(xy, SCRg, AX.X, ALU.add))
                    link(v.tensor_scalar(sc_, cnt[:, :], 1.0, None, ALU.max))
                    link(v.reciprocal(sc_, sc_))
                    v.wait_ge(acd, 1)
                    link(v.reciprocal(nr, nn))
                    link(v.tensor_tensor(nr, nr, q0, ALU.mult))
                    link(v.tensor_tensor(nn, nn, nr, ALU.add))
                    link(v.tensor_scalar(nn, nn, 0.5, None, ALU.mult))
                    link(v.tensor_scalar(nr, nn, EPS_M, float(np.float32(1.0) - np.float32(EPS_M)), ALU.max, ALU.min))
                    link(v.tensor_scalar(q0, nr, -1.0, 1.0, ALU.mult, ALU.add))
                    link(v.reciprocal(q0, q0))
                    link(v.tensor_scalar(q1, nr, 1.0, None, ALU.add))
                    link(v.tensor_tensor(q0, q0, q1, ALU.mult))
                    v.sem_inc(go, 1)
                    link(v.tensor_tensor(q2, nr, nr, ALU.mult))
                    link(v.tensor_scalar(q3, q2, 1.0 / 9, 1.0 / 7, ALU.mult, ALU.add))
                    for c in (1.0 / 5, 1.0 / 3, 1.0):
                        link(v.tensor_tensor(q3, q3, q2, ALU.mult))
                        link(v.tensor_scalar(q3, q3, c, None, ALU.add))
                    link(v.tensor_tensor(q3, q3, nr, ALU.mult))
                    link(v.tensor_scalar(q2, nr, 0.15, None, ALU.is_lt))
                    v.wait_ge(acd, 2)
                    link(v.tensor_scalar(f, f, 0.5, None, ALU.mult))
                    link(v.tensor_tensor(q3, q3, f, ALU.subtract))
                    link(v.tensor_tensor(q3, q3, q2, ALU.mult))
                    link(v.tensor_tensor(f, f, q3, ALU.add))
                    link(v.tensor_tensor(f, f, sc_, ALU.mult))
                    v.sem_inc(go, 1)
                    v.wait_ge(acd, 3)
                    link(v.reciprocal(q0, nr))
                    link(v.tensor_tensor(f, f, q0, ALU.mult))
                    link(v.scalar_tensor_tensor(f, nn, EPS_M, f, ALU.is_gt, ALU.mult))
                    x2 = TABg[:, :, D]
                    link(v.tensor_tensor(xy, xy, f, ALU.mult))
                    link(v.tensor_tensor(n2, n2, f, ALU.mult))
                    link(v.tensor_tensor(n2, n2, f, ALU.mult))
                    link(v.tensor_scalar(q0, xy, 2.0, 1.0, ALU.mult, ALU.add))
                    link(v.tensor_tensor(q1, x2, n2, ALU.mult))
                    link(v.tensor_tensor(q1, q1, q0, ALU.add))
                    link(v.tensor_scalar(q1, q1, EPS_M, None, ALU.max))
                    link(v.reciprocal(q1, q1))
                    link(v.tensor_tensor(q0, q0, n2, ALU.add))
                    link(v.tensor_tensor(q0, q0, q1, ALU.mult))
                    link(v.tensor_scalar(q2, x2, -1.0, 1.0, ALU.mult, ALU.add))
                    link(v.tensor_tensor(q2, q2, f, ALU.mult))
                    link(v.tensor_tensor(q2, q2, q1, ALU.mult))
                    link(v.tensor_tensor(SCRg, hs, spread(q0), ALU.mult))
                    link(v.tensor_tensor(X[:, :], X[:, :], SCR[:, :], ALU.add))
                    link(v.tensor_tensor(SCRg, sums, spread(q2), ALU.mult))
                    link(v.tensor_tensor(X[:, :], X[:, :], SCR[:, :], ALU.add))
                    v.sem_inc(go, 1)

                @block.scalar
                def _(ac):
                    ac.wait_ge(go, 1)
                    ac.activation(nn, q0, ACT.Sqrt).then_inc(acd, 1)
                    ac.wait_ge(go, 2)
                    ac.activation(f, q0, ACT.Ln).then_inc(acd, 1)
                    ac.wait_ge(go, 3)
                    ac.activation(f, f, ACT.Tanh).then_inc(acd, 1)

                @block.sync
                def _(sp):
                    sp.wait_ge(go, 4)
                    sp.dma_start(out.rearrange("(g p) f -> p g f", p=P), Xg).then_inc(sto, 16)
                    sp.wait_ge(sto, 16)
        w.close()


def layout(inputs):
    i = {k: np.asarray(v) for k, v in inputs.items()}
    pad = (C + 1) * P - E
    one = lambda n: np.ascontiguousarray(i[n].reshape(1, -1))
    col = lambda n: np.ascontiguousarray(i[n].reshape(-1, 1))
    dst2d = np.concatenate([i["dst"], np.full(pad, FARAWAY, np.int32)]).reshape(C + 1, P)
    return {
        "x": np.concatenate([i["x"], np.zeros((NP - N, D), np.float32)]),
        "src2d": np.concatenate([i["src"], np.zeros(pad, np.int32)]).reshape(C + 1, P),
        "dst2d": dst2d,
        "dst_last": np.ascontiguousarray(dst2d[:C, P - 1]),
        "ew2d": np.concatenate([i["edge_weight"], np.zeros(pad, np.float32)]).reshape(C + 1, P),
        "attrT": np.ascontiguousarray(np.concatenate([i["edge_attr_50"], np.zeros((pad, NG), np.float32)]).T),
        "w1": i["L0_gnn_mlp_w1"], "b1": col("L0_gnn_mlp_b1"), "w2": i["L0_gnn_mlp_w2"], "b2": one("L0_gnn_mlp_b2"),
        "lin1": i["L0_gnn_lin1_w"], "lin2": i["L0_gnn_lin2_w"], "lin2b": col("L0_gnn_lin2_b"),
        "lin": i["L0_gnn_lin_w"], "linb": one("L0_gnn_lin_b"),
        "wqvks": np.concatenate([i["L1_gnn_Wq"], i["L1_gnn_Wv"], i["L1_gnn_Wk"], i["L1_gnn_Ws"]], 1),
        "bqvks": np.concatenate([i["L1_gnn_bq"], i["L1_gnn_bv"], i["L1_gnn_bk"], i["L1_gnn_bs"]]).reshape(1, -1),
        "wg": i["L1_gnn_Wg"].reshape(1, 3 * D), "bg": i["L1_gnn_bg"].reshape(1, 1),
        "gamma": one("L1_gnn_gamma"), "beta": one("L1_gnn_beta"), "alpha": i["L1_gnn_alpha"].reshape(1, 1),
        "wlr1": np.concatenate([i["L2_gnn_W_l1"].T, i["L2_gnn_W_r1"].T], 1),
        "b21": one("L2_gnn_b1"),
        "wlr2": np.concatenate([i["L2_gnn_W_l2"].T, i["L2_gnn_W_r2"].T], 0),
        "b22": one("L2_gnn_b2"),
    }


def kernel(**inputs):
    import concourse.bacc as _bacc
    from concourse.bass_utils import run_bass_kernel_spmd as _run

    nc = _bacc.Bacc("TRN2", target_bir_lowering=False, num_devices=1)
    arrays = {f"in_{k}": np.ascontiguousarray(v) for k, v in layout(inputs).items()}
    aps = {n[3:]: nc.dram_tensor(n, v.shape, mybir.dt.from_np(v.dtype), kind="ExternalInput").ap() for n, v in arrays.items()}
    out = nc.dram_tensor("out", (NP, D), F32, kind="ExternalOutput").ap()
    build(nc, aps, out)
    r = _run(nc, [arrays], core_ids=[0])
    return r.results[0]["out"][:N]
```
